# Optimizing a Trainium2 kernel written in Bass

```python
import numpy as np
import jax
import jax.numpy as jnp

def _softmax(x, axis=-1):
    return jax.nn.softmax(x, axis=axis)

def _gelu(x):
    return jax.nn.gelu(x, approximate=True)

def _silu(x):
    return jax.nn.silu(x)

def _sigmoid(x):
    return jax.nn.sigmoid(x)

def _layernorm(x, axis=-1, eps=1e-05):
    m = jnp.mean(x, axis=axis, keepdims=True)
    v = jnp.var(x, axis=axis, keepdims=True)
    return (x - m) / jnp.sqrt(v + eps)

def _scatter_add(tgt, idx, src, axis=0):
    return tgt.at[idx].add(src)

def _segment_sum(src, seg, n):
    return jax.ops.segment_sum(src, seg, n)
kernel_name = 'mk_gnn_preln_d4_gnn_r64_73181d'

def setup_inputs(seed: int=0):
    np.random.seed(seed)
    _w = jnp.asarray

    def _rec_inputs():
        import jax
        import jax.numpy as jnp
        _gk = jax.random.key(seed)
        x = -0.000202 + 1 * jax.random.normal(jax.random.fold_in(_gk, 1), (50000, 128), jnp.float32)
        src = jax.random.randint(jax.random.fold_in(_gk, 2), (12500,), 0, 50000, jnp.int32)
        dst = jax.random.randint(jax.random.fold_in(_gk, 3), (12500,), 0, 50000, jnp.int32)
        _o = jnp.argsort(dst, stable=True)
        src = src[_o]
        dst = dst[_o]
        edge_attr_32 = 0.000196303 + 1.00016 * jax.random.normal(jax.random.fold_in(_gk, 12), (12500, 32), jnp.float32)
        edge_weight = jax.random.uniform(jax.random.fold_in(_gk, 14), (12500,), jnp.float32, 0.0, 1)
        return (x, src, dst, edge_attr_32, edge_weight)
    x, src, dst, edge_attr_32, edge_weight = _rec_inputs()

    def _L0_gnn_setup():
        import jax, jax.numpy as jnp
        import numpy as np
        N = 50000
        E = 12500
        H, C = (2, 64)
        IN_DIM = 128
        EDGE_DIM = 32
        NEG_SLOPE = 0.2

        def gatv2_layer(x, src, dst, edge_attr, Wl, Wr, We, att, b):
            xl = (x @ Wl).reshape(-1, H, C)
            xr = (x @ Wr).reshape(-1, H, C)
            ea = (edge_attr @ We).reshape(-1, H, C)
            xj = xl[src]
            e = jax.nn.leaky_relu(xj + xr[dst] + ea, NEG_SLOPE)
            logits = jnp.einsum('ehc,hc->eh', e, att)
            m = jax.ops.segment_max(logits, dst, num_segments=N)
            m = jnp.where(jnp.isfinite(m), m, 0.0)
            ex = jnp.exp(logits - m[dst])
            denom = jax.ops.segment_sum(ex, dst, num_segments=N)
            alpha = ex / (denom[dst] + 1e-16)
            out = jax.ops.segment_sum(alpha[:, :, None] * xj, dst, num_segments=N)
            return out.reshape(-1, H * C) + b
        key = jax.random.key(seed)
        ks = jax.random.split(key, 20)
        s = 0.05
        inp = {'x': jax.random.normal(ks[0], (N, IN_DIM), jnp.float32), 'edge_index': jax.random.randint(ks[1], (2, E), 0, N, jnp.int64), 'edge_attr': jax.random.normal(ks[2], (E, EDGE_DIM), jnp.float32)}
        k = 3
        for l in range(3):
            inp[f'Wl{l}'] = jax.random.normal(ks[k], (IN_DIM, H * C), jnp.float32) * s
            k += 1
            inp[f'Wr{l}'] = jax.random.normal(ks[k], (IN_DIM, H * C), jnp.float32) * s
            k += 1
            inp[f'We{l}'] = jax.random.normal(ks[k], (EDGE_DIM, H * C), jnp.float32) * s
            k += 1
            inp[f'att{l}'] = jax.random.normal(ks[k], (H, C), jnp.float32) * s
            k += 1
            inp[f'b{l}'] = jnp.zeros((H * C,), jnp.float32)
        return inp
    _L0_gnn_all = _L0_gnn_setup()
    _L0_gnn_in = {k: v for k, v in _L0_gnn_all.items() if k in ('Wl0', 'Wr0', 'We0', 'att0', 'b0', 'Wl1', 'Wr1', 'We1', 'att1', 'b1', 'Wl2', 'Wr2', 'We2', 'att2', 'b2')}
    del _L0_gnn_all

    def _L1_gnn_setup():
        import jax, jax.numpy as jnp
        import numpy as np
        NUM_NODES = 50000
        NUM_EDGES = 12500
        IN_DIM = 128
        OUT_DIM = 128
        key = jax.random.key(seed)
        k1, k2, k3 = jax.random.split(key, 3)
        x = jax.random.normal(k1, (NUM_NODES, IN_DIM), dtype=jnp.float32)
        edge_index = jax.random.randint(k2, (2, NUM_EDGES), 0, NUM_NODES, dtype=jnp.int64)
        limit = float(np.sqrt(6.0 / (IN_DIM + OUT_DIM)))
        weight = jax.random.uniform(k3, (IN_DIM, OUT_DIM), minval=-limit, maxval=limit, dtype=jnp.float32)
        bias = jnp.zeros((OUT_DIM,), dtype=jnp.float32)
        return {'x': x, 'edge_index': edge_index, 'weight': weight, 'bias': bias}
    _L1_gnn_all = _L1_gnn_setup()
    _L1_gnn_in = {k: v for k, v in _L1_gnn_all.items() if k in ('weight', 'bias')}
    del _L1_gnn_all

    def _L2_gnn_setup():
        import jax, jax.numpy as jnp
        import numpy as np
        NUM_LAYERS = 3

        def _spmm(edge_row, edge_col, edge_val, emb, num_nodes):
            msgs = edge_val[:, None] * emb[edge_col]
            return jax.ops.segment_sum(msgs, edge_row, num_segments=num_nodes)
        key = jax.random.key(seed)
        k1, k2, k3, k4 = jax.random.split(key, 4)
        N, D, E = (100000, 128, 50000)
        x = jax.random.normal(k1, (N, D), dtype=jnp.float32)
        edge_row = jax.random.randint(k2, (E,), 0, N, dtype=jnp.int64 if jax.config.jax_enable_x64 else jnp.int32)
        edge_col = jax.random.randint(k3, (E,), 0, N, dtype=jnp.int64 if jax.config.jax_enable_x64 else jnp.int32)
        edge_val = jax.random.uniform(k4, (E,), dtype=jnp.float32)
        return {'x': x, 'edge_row': edge_row, 'edge_col': edge_col, 'edge_val': edge_val}
    _L2_gnn_all = _L2_gnn_setup()
    _L2_gnn_in = {k: v for k, v in _L2_gnn_all.items() if k in ()}
    del _L2_gnn_all

    def _L3_gnn_setup():
        import jax, jax.numpy as jnp
        import numpy as np
        N_NODES = 50000
        key = jax.random.key(seed)
        ks = jax.random.split(key, 4)
        x = jax.random.normal(ks[0], (N_NODES, 128), dtype=jnp.float32)
        edge_index = jax.random.randint(ks[1], (2, 12500), 0, N_NODES, dtype=jnp.int64)
        W = jax.random.normal(ks[2], (8, 128, 128), dtype=jnp.float32) * (1.0 / np.sqrt(128))
        b = jnp.zeros((8, 128), dtype=jnp.float32)
        W_dict = jax.random.normal(ks[3], (128, 8), dtype=jnp.float32) * (1.0 / np.sqrt(128))
        b_dict = jnp.zeros((8,), dtype=jnp.float32)
        return {'x': x, 'edge_index': edge_index, 'W': W, 'b': b, 'W_dict': W_dict, 'b_dict': b_dict}
    _L3_gnn_all = _L3_gnn_setup()
    _L3_gnn_in = {k: v for k, v in _L3_gnn_all.items() if k in ('W', 'b', 'W_dict', 'b_dict')}
    del _L3_gnn_all
    return {'x': x, 'src': src, 'dst': dst, 'edge_attr_32': edge_attr_32, 'edge_weight': edge_weight, 'L0_gnn_Wl0': _L0_gnn_in['Wl0'], 'L0_gnn_Wr0': _L0_gnn_in['Wr0'], 'L0_gnn_We0': _L0_gnn_in['We0'], 'L0_gnn_att0': _L0_gnn_in['att0'], 'L0_gnn_b0': _L0_gnn_in['b0'], 'L0_gnn_Wl1': _L0_gnn_in['Wl1'], 'L0_gnn_Wr1': _L0_gnn_in['Wr1'], 'L0_gnn_We1': _L0_gnn_in['We1'], 'L0_gnn_att1': _L0_gnn_in['att1'], 'L0_gnn_b1': _L0_gnn_in['b1'], 'L0_gnn_Wl2': _L0_gnn_in['Wl2'], 'L0_gnn_Wr2': _L0_gnn_in['Wr2'], 'L0_gnn_We2': _L0_gnn_in['We2'], 'L0_gnn_att2': _L0_gnn_in['att2'], 'L0_gnn_b2': _L0_gnn_in['b2'], 'L1_gnn_weight': _L1_gnn_in['weight'], 'L1_gnn_bias': _L1_gnn_in['bias'], 'L3_gnn_W': _L3_gnn_in['W'], 'L3_gnn_b': _L3_gnn_in['b'], 'L3_gnn_W_dict': _L3_gnn_in['W_dict'], 'L3_gnn_b_dict': _L3_gnn_in['b_dict']}

def reference(x, src, dst, edge_attr_32, edge_weight, L0_gnn_Wl0, L0_gnn_Wr0, L0_gnn_We0, L0_gnn_att0, L0_gnn_b0, L0_gnn_Wl1, L0_gnn_Wr1, L0_gnn_We1, L0_gnn_att1, L0_gnn_b1, L0_gnn_Wl2, L0_gnn_Wr2, L0_gnn_We2, L0_gnn_att2, L0_gnn_b2, L1_gnn_weight, L1_gnn_bias, L3_gnn_W, L3_gnn_b, L3_gnn_W_dict, L3_gnn_b_dict):
    import jax
    import jax.numpy as jnp

    def _L0_gnn_ref(x, edge_index, edge_attr, Wl0, Wr0, We0, att0, b0, Wl1, Wr1, We1, att1, b1, Wl2, Wr2, We2, att2, b2):
        import jax, jax.numpy as jnp
        import numpy as np
        N = 50000
        E = 12500
        H, C = (2, 64)
        IN_DIM = 128
        EDGE_DIM = 32
        NEG_SLOPE = 0.2

        def gatv2_layer(x, src, dst, edge_attr, Wl, Wr, We, att, b):
            xl = (x @ Wl).reshape(-1, H, C)
            xr = (x @ Wr).reshape(-1, H, C)
            ea = (edge_attr @ We).reshape(-1, H, C)
            xj = xl[src]
            e = jax.nn.leaky_relu(xj + xr[dst] + ea, NEG_SLOPE)
            logits = jnp.einsum('ehc,hc->eh', e, att)
            m = jax.ops.segment_max(logits, dst, num_segments=N)
            m = jnp.where(jnp.isfinite(m), m, 0.0)
            ex = jnp.exp(logits - m[dst])
            denom = jax.ops.segment_sum(ex, dst, num_segments=N)
            alpha = ex / (denom[dst] + 1e-16)
            out = jax.ops.segment_sum(alpha[:, :, None] * xj, dst, num_segments=N)
            return out.reshape(-1, H * C) + b
        src, dst = (edge_index[0], edge_index[1])
        h = gatv2_layer(x, src, dst, edge_attr, Wl0, Wr0, We0, att0, b0)
        h = jax.nn.relu(h)
        h = gatv2_layer(h, src, dst, edge_attr, Wl1, Wr1, We1, att1, b1)
        h = jax.nn.relu(h)
        h = gatv2_layer(h, src, dst, edge_attr, Wl2, Wr2, We2, att2, b2)
        return h

    def _L1_gnn_ref(x, edge_index, weight, bias):
        import jax, jax.numpy as jnp
        import numpy as np
        NUM_NODES = 50000
        NUM_EDGES = 12500
        IN_DIM = 128
        OUT_DIM = 128
        num_nodes = x.shape[0]
        self_loops = jnp.broadcast_to(jnp.arange(num_nodes, dtype=edge_index.dtype)[None, :], (2, num_nodes))
        ei = jnp.concatenate([edge_index, self_loops], axis=1)
        row, col = (ei[0], ei[1])
        transformed = x @ weight
        deg = jax.ops.segment_sum(jnp.ones_like(row, dtype=x.dtype), row, num_segments=num_nodes)
        deg_inv_sqrt = jnp.where(deg > 0, deg ** (-0.5), 0.0)
        norm = deg_inv_sqrt[row] * deg_inv_sqrt[col]
        messages = norm[:, None] * transformed[row]
        out = jax.ops.segment_sum(messages, col, num_segments=num_nodes)
        return out + bias

    def _L2_gnn_ref(x, edge_row, edge_col, edge_val):
        import jax, jax.numpy as jnp
        import numpy as np
        NUM_LAYERS = 3

        def _spmm(edge_row, edge_col, edge_val, emb, num_nodes):
            msgs = edge_val[:, None] * emb[edge_col]
            return jax.ops.segment_sum(msgs, edge_row, num_segments=num_nodes)
        N = x.shape[0]
        emb = x
        acc = x
        for _ in range(NUM_LAYERS):
            emb = _spmm(edge_row, edge_col, edge_val, emb, N)
            acc = acc + emb
        return acc / jnp.float32(NUM_LAYERS + 1)

    def _L3_gnn_ref(x, edge_index, W, b, W_dict, b_dict):
        import jax, jax.numpy as jnp
        import numpy as np
        N_NODES = 50000
        N = x.shape[0]
        K = W.shape[0]
        num_atoms = W_dict.shape[1]
        loop = jnp.arange(N, dtype=edge_index.dtype)
        src = jnp.concatenate([edge_index[0], loop])
        dst = jnp.concatenate([edge_index[1], loop])
        deg = jax.ops.segment_sum(jnp.ones_like(dst, dtype=x.dtype), dst, num_segments=N)
        dis = jnp.where(deg > 0, jax.lax.rsqrt(jnp.maximum(deg, 1.0)), 0.0)
        norm = (dis[src] * dis[dst])[:, None]
        coeff = jax.nn.softmax(x @ W_dict + b_dict, axis=-1)
        total = jnp.zeros((N, W.shape[2]), dtype=x.dtype)
        for k in range(K):
            h = x @ W[k]
            agg = jax.ops.segment_sum(h[src] * norm, dst, num_segments=N) + b[k]
            feat = jax.nn.relu(agg)
            total = total + feat * coeff[:, k % num_atoms, None]
        return total
    edge_index = jnp.stack([src, dst])
    h = jnp.maximum(_layernorm(x, axis=-1), 0.0)
    x = x + _L0_gnn_ref(h, edge_index, edge_attr_32, L0_gnn_Wl0, L0_gnn_Wr0, L0_gnn_We0, L0_gnn_att0, L0_gnn_b0, L0_gnn_Wl1, L0_gnn_Wr1, L0_gnn_We1, L0_gnn_att1, L0_gnn_b1, L0_gnn_Wl2, L0_gnn_Wr2, L0_gnn_We2, L0_gnn_att2, L0_gnn_b2)
    h = jnp.maximum(_layernorm(x, axis=-1), 0.0)
    x = x + _L1_gnn_ref(h, edge_index, L1_gnn_weight, L1_gnn_bias)
    h = jnp.maximum(_layernorm(x, axis=-1), 0.0)
    x = x + _L2_gnn_ref(h, src, dst, edge_weight)
    h = jnp.maximum(_layernorm(x, axis=-1), 0.0)
    x = x + _L3_gnn_ref(h, edge_index, L3_gnn_W, L3_gnn_b, L3_gnn_W_dict, L3_gnn_b_dict)
    return x

_drawn_inputs = setup_inputs


def setup_inputs(seed=0):
    import zlib

    import numpy as np

    out = dict(_drawn_inputs(seed))
    spreads = {'L0_gnn_b0': (0.0, 0.8),
     'L0_gnn_b1': (0.0, 0.468),
     'L0_gnn_b2': (0.0, 0.1),
     'L1_gnn_bias': (0.0, 0.1),
     'L3_gnn_b': (0.0, 0.418),
     'L3_gnn_b_dict': (0.0, 0.506)}
    factors = {'edge_attr_32': 8.0,
     'edge_weight': 2.73,
     'L0_gnn_Wl0': 8.0,
     'L0_gnn_Wr0': 8.0,
     'L0_gnn_We0': 8.0,
     'L0_gnn_att0': 8.0,
     'L0_gnn_Wl1': 8.0,
     'L0_gnn_Wr1': 8.0,
     'L0_gnn_We1': 8.0,
     'L0_gnn_att1': 8.0,
     'L0_gnn_Wl2': 3.041,
     'L0_gnn_Wr2': 8.0,
     'L0_gnn_We2': 8.0,
     'L0_gnn_att2': 8.0}
    for name, (base, spread) in spreads.items():
        noise = np.random.default_rng([zlib.crc32(name.encode()), seed]).standard_normal(out[name].shape)
        drawn = base * np.exp(spread * noise) if base else spread * noise
        out[name] = jnp.asarray(drawn.astype(out[name].dtype))
    for name, factor in factors.items():
        out[name] = (out[name] * factor).astype(out[name].dtype)
    return out
```

```python
import concourse.bass as bass
from concourse import mybir
from contextlib import ExitStack, contextmanager

F32, I32, BF16 = mybir.dt.float32, mybir.dt.int32, mybir.dt.bfloat16
ALU, ACT = mybir.AluOpType, mybir.ActivationFunctionType
D = 128
P = 125
T = 4
CH = P * T
SLOTS = 5
REC = 48
LO = 512
BIG = 1e30
FAR = 1 << 20
EPS = 1e-5
GT = 5
DSLOTS = 3
ROW = 2 * D + 8
HEADS = 8
R_RHO, R_SIGS, R_SIGD, R_SIDX, R_DIDX = 0, 1, 2, 3, 4
R_CMSG, R_SELFS, R_SELFD, R_CMSG3, R_SELF3, R_NSTART, R_NLAST = 5, 6, 7, 8, 9, 10, 11
R_SRC, R_DST = 12, 13
R_EA = 16
J_LINK, J_POSD, J_W, J_NSTART = 0, 1, 2, 3


class Box:
    pass


@contextmanager
def phase(nc, at, names, slots=(), each=SLOTS):
    one = {name: nc.alloc_semaphore(f"{at}_{name}") for name in ("s_held", *names)}
    many = {name: [nc.alloc_semaphore(f"{at}_{name}{u}") for u in range(each)] for name in slots}
    every = [*one.values(), *(h for hs in many.values() for h in hs)]
    s = type("Semaphores", (), {**one, **many, "by_name": one})()
    with ExitStack() as bufs:
        s.sb = lambda name, shape, dt=F32: bufs.enter_context(nc.sbuf_tensor(f"{at}_{name}", shape, dt))
        s.ps = lambda name, shape, dt=F32: bufs.enter_context(nc.psum_tensor(f"{at}_ps_{name}", shape, dt))
        with nc.Block() as block:
            yield block, s
    nc.clear_and_free_semaphores(every)
    nc.all_engine_barrier()


def hold(eng, s):
    eng.sem_inc(s.s_held, 1)


def peeled(eng, n):
    if n > 0:
        yield 0
    if n > 1:
        with eng.Fori(1, n) as i:
            yield i


def rows_of(dram, start, n=CH):
    return dram[bass.ds(start, n), :].rearrange("(t p) d -> p t d", p=P)


def constants(nc, K, a):
    with phase(nc, "const", ["s_load", "s_set", "s_sel", "s_dma2", "s_z"]) as (block, s):
        att_c = s.sb("att_c", [D, 3, 1])
        bsrc = s.sb("bsrc", [1, 4, D])
        zero = s.sb("zero", [1, D])
        iota_i = s.sb("iota_i", [D, LO], I32)
        part_i = s.sb("part_i", [D, 1], I32)
        b3 = s.sb("b3", [1, HEADS * D])
        b3p = [s.sb(f"b3p{n}", [1, HEADS * D], BF16) for n in range(3)]
        NLOADS = 3 * 5 + 10

        @block.sync
        def _(sp):
            for l in range(3):
                sp.dma_start(K.wl[:, l, :], a[f"L0_gnn_Wl{l}"][:, :]).then_inc(s.s_load, 16)
                sp.dma_start(K.wr[:, l, :], a[f"L0_gnn_Wr{l}"][:, :]).then_inc(s.s_load, 16)
                sp.dma_start(K.we[:, l, :], a[f"L0_gnn_We{l}"][:, :]).then_inc(s.s_load, 16)
                sp.dma_start(att_c[:, l, :], a[f"L0_gnn_att{l}"].rearrange("h (c o) -> (h c) o", o=1)).then_inc(s.s_load, 16)
                sp.dma_start(K.bcol[:, l:l + 1], a[f"L0_gnn_b{l}"].rearrange("(p o) -> p o", o=1)).then_inc(s.s_load, 16)
            for l in range(3):
                sp.dma_start(bsrc[:, l, :], a[f"L0_gnn_b{l}"].rearrange("(o d) -> o d", o=1)).then_inc(s.s_load, 16)
            sp.dma_start(K.w1[:], a["L1_gnn_weight"][:, :]).then_inc(s.s_load, 16)
            sp.dma_start(K.w3[:], a["L3_gnn_W"].rearrange("k i o -> i k o")).then_inc(s.s_load, 16)
            sp.dma_start(K.wd[:], a["L3_gnn_W_dict"][:, :]).then_inc(s.s_load, 16)
            sp.dma_start(K.b2row[:], a["L0_gnn_b2"].rearrange("(o d) -> o d", o=1).to_broadcast((D, D))).then_inc(s.s_load, 16)
            sp.dma_start(K.b1row[:], a["L1_gnn_bias"].rearrange("(o d) -> o d", o=1).to_broadcast((D, D))).then_inc(s.s_load, 16)
            sp.dma_start(K.bdrow[:], a["L3_gnn_b_dict"].rearrange("(o d) -> o d", o=1).to_broadcast((D, HEADS))).then_inc(s.s_load, 16)
            sp.dma_start(b3[:], a["L3_gnn_b"].rearrange("(o k) d -> o (k d)", o=1)).then_inc(s.s_load, 16)
            sp.wait_ge(s.s_z, 2)
            for l in range(3):
                sp.dma_start(K.tab[l][K.E:K.E + 1, :], bsrc[:, l, :]).then_inc(s.s_dma2, 16)
            for t in (K.tabu, *K.tabe, K.taba):
                sp.dma_start(t[K.E:K.E + 1, :], zero[:]).then_inc(s.s_dma2, 16)
            for n in range(3):
                sp.dma_start(K.b3s[n:n + 1, :, :].rearrange("p k d -> p (k d)"), b3p[n][:]).then_inc(s.s_dma2, 16)
            sp.wait_ge(s.s_dma2, 16 * (6 + 2 + len(K.tabe)))

        @block.gpsimd
        def _(g):
            nc.gpsimd.memset(K.ident[:], 0.0)
            nc.gpsimd.memset(K.before[:], 1.0)
            nc.gpsimd.memset(K.carry[:], 1.0)
            nc.gpsimd.memset(K.onesb[:], 1.0)
            nc.gpsimd.iota(iota_i[:], pattern=[[1, LO]], base=0, channel_multiplier=0)
            nc.gpsimd.iota(part_i[:], pattern=[[0, 1]], base=0, channel_multiplier=1)
            g.drain()
            nc.gpsimd.affine_select(out=K.ident[:], in_=K.ident[:], compare_op=ALU.not_equal, fill=1.0,
                                    base=0, pattern=[[-1, D]], channel_multiplier=1)
            nc.gpsimd.affine_select(out=K.before[:], in_=K.before[:], compare_op=ALU.is_gt, fill=0.0,
                                    base=0, pattern=[[-1, D]], channel_multiplier=1)
            nc.gpsimd.affine_select(out=K.carry[:], in_=K.carry[:], compare_op=ALU.is_gt, fill=0.0,
                                    base=0, pattern=[[1, D]], channel_multiplier=-1)
            nc.gpsimd.drain().then_inc(s.s_set, 1)

        @block.vector
        def _(v):
            nc.vector.memset(K.block2[:], 0.0)
            v.drain()
            nc.vector.memset(K.block2[0:64, 0:64], 1.0)
            nc.vector.memset(K.block2[64:128, 64:128], 1.0)
            v.wait_ge(s.s_set, 1)
            nc.vector.tensor_copy(K.identb[:], K.ident[:])
            nc.vector.tensor_copy(K.iota[:], iota_i[:])
            nc.vector.tensor_copy(K.part[:], part_i[:])
            nc.vector.memset(zero[:], 0.0).then_inc(s.s_z, 1)
            v.drain()
            v.wait_ge(s.s_load, 16 * NLOADS)
            for l in range(3):
                nc.vector.tensor_scalar(K.att[:, l, :], K.block2[:], att_c[:, l, :], None, ALU.mult)
            for l in range(2):
                nc.vector.tensor_scalar(bsrc[:, l, :], bsrc[:, l, :], 0.0, None, ALU.max)
            for n in range(3):
                nc.vector.tensor_copy(b3p[n][:], b3[:])
                v.drain()
                if n < 2:
                    nc.vector.tensor_tensor(b3[:], b3[:], b3p[n][:], ALU.subtract)
                    v.drain()
            nc.vector.drain().then_inc(s.s_z, 1)


def ranks(nc, K, a):
    KEYS = ("src", "dst")
    with phase(nc, "rank", ["s_rows", "s_keyb", "s_cast", "s_tp", "s_cols", "s_zero"]
               + [f"{n}_{k}" for n in ("oh", "copied", "looked", "counted", "dotted") for k in KEYS]
               ) as (block, s):
        keyb = {k: s.sb(f"keyb_{k}", [D, K.E], I32) for k in KEYS}
        raw = s.sb("raw", [K.NT, 2, P], I32)
        rowf = s.sb("rowf", [K.NT, 3, P])
        coli = s.sb("coli", [P, K.NT], I32)
        keyi = s.sb("keyi", [P, K.NT], I32)
        colp = {k: s.sb(f"colp_{k}", [P, K.NT]) for k in KEYS}
        colc = {k: s.sb(f"colc_{k}", [P, K.NT]) for k in KEYS}
        pbi = s.sb("pbi", [K.NP, P], I32)
        ohp = {(k, b): s.sb(f"ohp_{k}{b}", [P, K.NP], BF16) for k in KEYS for b in (0, 1)}
        ohc = {(k, b): s.sb(f"ohc_{k}{b}", [P, LO], BF16) for k in KEYS for b in (0, 1)}
        ohpt = {(k, b): s.sb(f"ohpt_{k}{b}", [K.NP, P]) for k in KEYS for b in (0, 1)}
        zb = s.sb("zb", [P, LO], BF16)
        junk = s.sb("junk", [P, LO])
        o0, o1 = s.sb("o0", [P, 1]), s.sb("o1", [P, 1])
        count = {k: s.ps(f"count_{k}", [K.NP, LO]) for k in KEYS}
        look = {(k, b): s.ps(f"look_{k}{b}", [P, LO]) for k in KEYS for b in (0, 1)}
        pt = s.ps("pt", [P, 3, K.NT])

        @block.sync
        def _(sp):
            tiles = lambda x: x.rearrange("(t p) -> t p", p=P)
            sp.dma_start(raw[:, 0, :], tiles(a["src"])).then_inc(s.s_rows, 16)
            sp.dma_start(raw[:, 1, :], tiles(a["dst"])).then_inc(s.s_rows, 16)
            sp.dma_start(rowf[:, 2, :], tiles(a["edge_weight"])).then_inc(s.s_rows, 16)
            for k in KEYS:
                sp.dma_start(keyb[k][:], a[k].rearrange("(o e) -> o e", o=1).to_broadcast((D, K.E))).then_inc(s.s_keyb, 16)

        @block.tensor
        def _(pe):
            pe.wait_ge(s.s_cast, 1)
            for n in range(3):
                last = nc.tensor.transpose(pt[:, n, :], rowf[:, n, :], K.ident[0:K.NT, 0:K.NT])
            last.then_inc(s.s_tp, 1)
            pe.wait_ge(s.s_zero, 1)
            for k in KEYS:
                nc.tensor.matmul(count[k][:], zb[:, 0:K.NP], zb[:], start=True, stop=True).then_inc(s.by_name[f"counted_{k}"], 1)
            for c in peeled(pe, K.NCH):
                for t in range(T):
                    n = c * T + t
                    for k in KEYS:
                        pe.wait_ge(s.by_name[f"oh_{k}"], n + 1)
                        pe.wait_ge(s.by_name[f"copied_{k}"], n + 1)
                        pe.wait_ge(s.by_name[f"dotted_{k}"], c * T + max(t - 1, 0))
                        nc.tensor.matmul(look[k, t % 2][:], ohpt[k, t % 2][:], K.cnt[k][:], start=True,
                                         stop=True).then_inc(s.by_name[f"looked_{k}"], 1)
                        nc.tensor.matmul(count[k][:], ohp[k, t % 2][:], ohc[k, t % 2][:], start=False, stop=True,
                                         skip_group_check=True).then_inc(s.by_name[f"counted_{k}"], 1)

        @block.scalar
        def _(act):
            for c in peeled(act, K.NCH):
                for t in range(T):
                    n = c * T + t
                    for k in KEYS:
                        act.wait_ge(s.by_name[f"counted_{k}"], n + 1)
                        act.wait_ge(s.by_name[f"looked_{k}"], n)
                        nc.scalar.copy(K.cnt[k][:], count[k][:]).then_inc(s.by_name[f"copied_{k}"], 1)
            for k in KEYS:
                act.wait_ge(s.by_name[f"counted_{k}"], K.NT + 1)
                act.wait_ge(s.by_name[f"looked_{k}"], K.NT)
                nc.scalar.copy(K.cnt[k][:], count[k][:])

        @block.vector
        def _(v):
            nc.vector.memset(zb[:], 0.0).then_inc(s.s_zero, 1)
            v.wait_ge(s.s_rows, 48)
            nc.vector.tensor_copy(rowf[:, 0:2, :], raw[:]).then_inc(s.s_cast, 1)
            v.wait_ge(s.s_tp, 1)
            for n, k in enumerate(KEYS):
                nc.vector.tensor_copy(K.col[k][:], pt[:, n, :])
                nc.vector.tensor_copy(keyi[:], pt[:, n, :])
                v.drain()
                nc.vector.tensor_scalar(coli[:], keyi[:], 9, None, ALU.arith_shift_right)
                v.drain()
                nc.vector.tensor_copy(colp[k][:], coli[:])
                v.drain()
                nc.vector.tensor_scalar(coli[:], keyi[:], LO - 1, None, ALU.bitwise_and)
                v.drain()
                nc.vector.tensor_copy(colc[k][:], coli[:])
                v.drain()
            nc.vector.tensor_copy(K.wcol[:], pt[:, 2, :])
            v.drain()
            v.wait_ge(s.s_keyb, 32)

            def onehots(c, t, k):
                n, b = c * T + t, t % 2
                nc.vector.tensor_scalar(pbi[:], keyb[k][0:K.NP, bass.ds(n * P, P)], 9, None, ALU.arith_shift_right)
                v.drain()
                v.wait_ge(s.by_name[f"counted_{k}"], c * T + max(t, 1))
                nc.vector.tensor_scalar(ohpt[k, b][:], pbi[:], K.part[0:K.NP, :], None, ALU.is_equal)
                nc.vector.tensor_scalar(ohp[k, b][:], K.iota[0:P, 0:K.NP], colp[k][:, bass.ds(n, 1)], None, ALU.is_equal)
                nc.vector.tensor_scalar(ohc[k, b][:], K.iota[0:P, :], colc[k][:, bass.ds(n, 1)], None, ALU.is_equal)
                nc.vector.drain().then_inc(s.by_name[f"oh_{k}"], 1)

            def dot(c, t, k):
                n, b = c * T + t, t % 2
                nc.vector.scalar_tensor_tensor(out=junk[:, 0:P], in0=keyb[k][0:P, bass.ds(n * P, P)],
                                               scalar=K.col[k][:, bass.ds(n, 1)], in1=K.before[0:P, 0:P],
                                               op0=ALU.is_equal, op1=ALU.mult, accum_out=o0[:])
                v.drain()
                v.wait_ge(s.by_name[f"looked_{k}"], n + 1)
                nc.vector.scalar_tensor_tensor(out=junk[:], in0=look[k, b][:], scalar=1.0, in1=ohc[k, b][:],
                                               op0=ALU.mult, op1=ALU.mult, accum_out=o1[:])
                v.drain()
                nc.vector.tensor_tensor(K.occ[k][:, bass.ds(n, 1)], o0[:], o1[:], ALU.add)
                nc.vector.drain().then_inc(s.by_name[f"dotted_{k}"], 1)

            for c in peeled(v, K.NCH):
                for k in KEYS:
                    onehots(c, 0, k)
                for t in range(1, T):
                    for k in KEYS:
                        onehots(c, t, k)
                    for k in KEYS:
                        dot(c, t - 1, k)
                for k in KEYS:
                    dot(c, T - 1, k)


def node_table(nc, K):
    with phase(nc, "table", ["s_tot", "s_carry", "s_tab", "s_out"]) as (block, s):
        info = s.sb("info", [K.NP, LO, 4])
        scan = s.sb("scan", [K.NP, 2, LO])
        pc = s.ps("pc", [K.NP, 2])

        @block.vector
        def _(v):
            for n, k in enumerate(("src", "dst")):
                nc.vector.tensor_copy(info[:, :, n], K.cnt[k][:])
                nc.vector.tensor_tensor_scan(scan[:, n, :], K.cnt[k][:], K.cnt[k][:], 0.0, ALU.add, ALU.bypass)
            nc.vector.drain().then_inc(s.s_tot, 1)
            v.wait_ge(s.s_carry, 1)
            for n in range(2):
                nc.vector.tensor_scalar(info[:, :, 2 + n], scan[:, n, :], pc[:, n:n + 1], None, ALU.add)
            nc.vector.drain().then_inc(s.s_tab, 1)

        @block.tensor
        def _(pe):
            pe.wait_ge(s.s_tot, 1)
            for n in range(2):
                last = nc.tensor.matmul(pc[:, n:n + 1], K.carry[0:K.NP, 0:K.NP], scan[:, n, LO - 1:LO], start=True, stop=True)
            last.then_inc(s.s_carry, 1)

        @block.sync
        def _(sp):
            sp.wait_ge(s.s_tab, 1)
            hold(sp, s)
            sp.dma_start(K.info.rearrange("(p c) w -> p c w", c=LO), info[:]).then_inc(s.s_out, 16)
            sp.wait_ge(s.s_out, 16)


def records(nc, K, a):
    with phase(nc, "rec", ["s_idx", "s_arg", "s_root"], ["ea", "info", "made", "used", "sent"]) as (block, s):
        idx = [s.sb(f"idx{u}", [P, 2, T], I32) for u in range(SLOTS)]
        inf = [s.sb(f"inf{u}", [P, 2, T, 4]) for u in range(SLOTS)]
        rec = [s.sb(f"rec{u}", [P, T, REC]) for u in range(SLOTS)]
        recj = [s.sb(f"recj{u}", [P, T, 4]) for u in range(SLOTS)]
        pos = [s.sb(f"pos{u}", [P, 2, T], I32) for u in range(SLOTS)]
        arg = s.sb("arg", [P, 4, T])
        root = s.sb("root", [P, 4, T])
        inv = s.sb("inv", [P, 4, T])
        x = [s.sb(f"x{n}", [P, T]) for n in range(4)]

        @block.sync
        def _(sp):
            for i in peeled(sp, K.NI):
                for u in range(SLOTS):
                    sp.wait_ge(s.sent[u], i * (16 * 2 * T))
                    hold(sp, s)
                    sp.dma_start(rec[u][:, :, R_EA:R_EA + 32],
                                 rows_of(a["edge_attr_32"], i * (SLOTS * CH) + u * CH)).then_inc(s.ea[u], 16)

        @block.gpsimd
        def _(g):
            g.wait_ge(s.s_idx, 1)

            def gather(i, u):
                for n in range(2):
                    for t in range(T):
                        nc.gpsimd.indirect_dma_start(inf[u][:, n, t, :], None, K.info[:, :],
                                                     bass.IndirectOffsetOnAxis(ap=idx[u][:, n, t:t + 1], axis=0)
                                                     ).then_inc(s.info[u], 16)

            def scatter(i, u):
                g.wait_ge(s.made[u], i + 1)
                hold(g, s)
                for t in range(T):
                    nc.gpsimd.indirect_dma_start(K.recd[:, :], bass.IndirectOffsetOnAxis(ap=pos[u][:, 0, t:t + 1], axis=0),
                                                 rec[u][:, t, :], None).then_inc(s.sent[u], 16)
                    nc.gpsimd.indirect_dma_start(K.recj[:, :], bass.IndirectOffsetOnAxis(ap=pos[u][:, 1, t:t + 1], axis=0),
                                                 recj[u][:, t, :], None).then_inc(s.sent[u], 16)

            for i in peeled(g, K.NI):
                for u in range(SLOTS):
                    g.wait_ge(s.s_idx, i * SLOTS + u + 1)
                    hold(g, s)
                    gather(i, u)
                    if u:
                        scatter(i, u - 1)
                scatter(i, SLOTS - 1)
            for u in range(SLOTS):
                g.wait_ge(s.sent[u], K.NI * 16 * 2 * T)

        @block.scalar
        def _(act):
            for i in peeled(act, K.NI):
                for u in range(SLOTS):
                    act.wait_ge(s.s_arg, i * SLOTS + u + 1)
                    nc.scalar.activation(root[:], arg[:], ACT.Sqrt).then_inc(s.s_root, 1)

        @block.vector
        def _(v):
            for i in peeled(v, K.NI):
                for u in range(SLOTS):
                    v.wait_ge(s.info[u], i * (16 * 2 * T))
                    v.wait_ge(s.sent[u], i * (16 * 2 * T))
                    for n, k in enumerate(("src", "dst")):
                        nc.vector.tensor_copy(idx[u][:, n, :], K.col[k][:, bass.ds(i * (SLOTS * T) + u * T, T)])
                    nc.vector.drain().then_inc(s.s_idx, 1)
                for u in range(SLOTS):
                    v.wait_ge(s.info[u], (i + 1) * (16 * 2 * T))
                    v.wait_ge(s.ea[u], (i + 1) * 16)
                    tile = lambda b: b[:, bass.ds(i * (SLOTS * T) + u * T, T)]
                    f = inf[u]
                    outs, ins, ejs, eds = (f[:, 0, :, w] for w in range(4))
                    outd, ind, ejd, edd = (f[:, 1, :, w] for w in range(4))
                    ri = rec[u][:].bitcast(I32)
                    rf = rec[u]
                    ji = recj[u][:].bitcast(I32)
                    TS, TT, STT = nc.vector.tensor_scalar, nc.vector.tensor_tensor, nc.vector.scalar_tensor_tensor
                    occs, occd = tile(K.occ["src"]), tile(K.occ["dst"])
                    TS(arg[:, 0, :], outs, 1.0, None, ALU.add)
                    TS(arg[:, 1, :], outd, 1.0, None, ALU.add)
                    TS(arg[:, 2, :], ins, 1.0, None, ALU.add)
                    TS(arg[:, 3, :], ind, 1.0, None, ALU.add)
                    nc.vector.drain().then_inc(s.s_arg, 1)
                    TS(x[0][:], ins, 1.0, None, ALU.min)
                    TS(x[1][:], outd, 1.0, None, ALU.min)
                    TS(x[2][:], eds, -(K.E + 1.0), None, ALU.add)
                    TS(x[3][:], ejd, -(K.E + 1.0), None, ALU.add)
                    v.drain()
                    TT(x[2][:], x[2][:], x[0][:], ALU.mult)
                    TT(x[3][:], x[3][:], x[1][:], ALU.mult)
                    v.drain()
                    TS(ri[:, :, R_RHO], x[2][:], float(K.E), None, ALU.add)
                    TS(ri[:, :, R_SIGD], x[3][:], float(K.E), None, ALU.add)
                    TS(ji[:, :, J_LINK], x[3][:], float(K.E), None, ALU.add)
                    TS(ri[:, :, R_SIGS], ejs, -1.0, None, ALU.add)
                    nc.vector.tensor_copy(ri[:, :, R_SRC], tile(K.col["src"]))
                    nc.vector.tensor_copy(ri[:, :, R_DST], tile(K.col["dst"]))
                    v.drain()
                    TT(x[1][:], edd, ind, ALU.subtract)
                    TT(x[3][:], ejs, outs, ALU.subtract)
                    v.drain()
                    TT(x[1][:], x[1][:], occd, ALU.add)
                    TT(x[3][:], x[3][:], occs, ALU.add)
                    v.drain()
                    nc.vector.tensor_copy(pos[u][:, 0, :], x[1][:])
                    nc.vector.tensor_copy(pos[u][:, 1, :], x[3][:])
                    nc.vector.tensor_copy(ji[:, :, J_POSD], x[1][:])
                    nc.vector.tensor_copy(recj[u][:, :, J_W], tile(K.wcol))
                    TS(recj[u][:, :, J_NSTART], occs, 1.0, None, ALU.min)
                    TS(rf[:, :, R_NSTART], occd, 1.0, None, ALU.min)
                    v.drain()
                    TT(x[1][:], ind, occd, ALU.subtract)
                    TT(x[2][:], outs, occs, ALU.subtract)
                    v.drain()
                    TS(x[1][:], x[1][:], -1.0, 1.0, ALU.add, ALU.min)
                    TS(x[2][:], x[2][:], -1.0, 1.0, ALU.add, ALU.min)
                    v.drain()
                    nc.vector.tensor_copy(rf[:, :, R_NLAST], x[1][:])
                    TT(x[2][:], x[2][:], x[0][:], ALU.max)
                    v.drain()
                    STT(ri[:, :, R_SIDX], x[2][:], float(FAR), tile(K.col["src"]), ALU.mult, ALU.add)
                    STT(ri[:, :, R_DIDX], x[1][:], float(FAR), tile(K.col["dst"]), ALU.mult, ALU.add)
                    v.wait_ge(s.s_root, i * SLOTS + u + 1)
                    nc.vector.reciprocal(inv[:], root[:])
                    v.drain()
                    TT(rf[:, :, R_CMSG], inv[:, 0, :], inv[:, 1, :], ALU.mult)
                    TT(rf[:, :, R_SELFS], inv[:, 0, :], inv[:, 0, :], ALU.mult)
                    TT(rf[:, :, R_SELFD], inv[:, 1, :], inv[:, 1, :], ALU.mult)
                    TT(rf[:, :, R_CMSG3], inv[:, 2, :], inv[:, 3, :], ALU.mult)
                    TT(rf[:, :, R_SELF3], inv[:, 3, :], inv[:, 3, :], ALU.mult)
                    nc.vector.memset(rf[:, :, R_DST + 1:R_EA], 0.0)
                    nc.vector.drain().then_inc(s.made[u], 1)


def rounds(eng, K, first, body):
    first()
    for i in peeled(eng, K.NI - 1):
        for u in range(SLOTS):
            body(i, u, (i, u + 1) if u < SLOTS - 1 else (i + 1, 0))
    i = K.NI - 1
    for u in range(SLOTS):
        body(i, u, (i, u + 1) if u < SLOTS - 1 else None)


def ahead(eng, K, body):
    for i in peeled(eng, K.NI):
        for u in range(SLOTS):
            body(i, u)


def again(i):
    return not (isinstance(i, int) and i == 0)


def cnt(i, u):
    return i * SLOTS + u


def span(i, u):
    return bass.ds(i * (SLOTS * CH) + u * CH, CH)


def flags(nc, K, at, table, words, outs, width):
    with phase(nc, at, ["s_diag", "s_ps", "s_cp"], ["rec"]) as (block, s):
        rec = [s.sb(f"rec{u}", [P, T, width]) for u in range(SLOTS)]
        diag = s.sb("diag", [P, len(words), T, P], BF16)
        ps = [s.ps(f"ps{n}", [D, CH]) for n in range(len(words))]

        @block.sync
        def _(sp):
            for i in peeled(sp, K.NI):
                for u in range(SLOTS):
                    sp.wait_ge(s.s_diag, i * SLOTS)
                    hold(sp, s)
                    sp.dma_start(rec[u][:], rows_of(table, i * (SLOTS * CH) + u * CH)).then_inc(s.rec[u], 16)

        @block.vector
        def _(v):
            for i in peeled(v, K.NI):
                for u in range(SLOTS):
                    v.wait_ge(s.rec[u], (i + 1) * 16)
                    v.wait_ge(s.s_ps, cnt(i, u))
                    for n, w in enumerate(words):
                        nc.vector.tensor_tensor(diag[:, n], K.identb[0:P, 0:P].unsqueeze(1).to_broadcast((P, T, P)),
                                                rec[u][:, :, w:w + 1].to_broadcast((P, T, P)), ALU.mult)
                    nc.vector.drain().then_inc(s.s_diag, 1)

        @block.tensor
        def _(pe):
            for i in peeled(pe, K.NI):
                for u in range(SLOTS):
                    pe.wait_ge(s.s_diag, cnt(i, u) + 1)
                    pe.wait_ge(s.s_cp, cnt(i, u))
                    for n in range(len(words)):
                        last = nc.tensor.matmul(ps[n][:], K.onesb[0:P, :], diag[:, n].rearrange("p t e -> p (t e)"),
                                                start=True, stop=True)
                    last.then_inc(s.s_ps, 1)

        @block.scalar
        def _(act):
            for i in peeled(act, K.NI):
                for u in range(SLOTS):
                    act.wait_ge(s.s_ps, cnt(i, u) + 1)
                    hold(act, s)
                    for n in range(len(words)):
                        last = nc.scalar.copy(outs[n][:, span(i, u)], ps[n][:])
                    nc.scalar.drain().then_inc(s.s_cp, 1)


def spread_back(nc, K, at, x):
    with phase(nc, at, []) as (block, s):
        @block.vector
        def _(v):
            E = K.E
            nc.vector.scalar_tensor_tensor(out=x[:], in0=K.nlast[:], scalar=-1.0, in1=x[:], op0=ALU.add, op1=ALU.mult)
            v.drain()
            nc.vector.tensor_tensor_scan(x[:, E - 1::-1], K.nlast[:, E - 1::-1], x[:, E - 1::-1], 0.0,
                                         ALU.mult, ALU.subtract)


def ln_stats(nc, v, L, x, n):
    for t in range(n):
        nc.vector.bn_stats(L.st[0:x.shape[0], t, :], x[:, t, :])
    v.drain()
    for t in range(n):
        nc.vector.bn_aggr(L.mv[0:x.shape[0], t, :], L.st[0:x.shape[0], t, :])
    v.drain()
    nc.vector.tensor_scalar(L.var[0:x.shape[0], 0:n], L.mv[0:x.shape[0], 0:n, 1], EPS, None, ALU.add)


def ln_scale(nc, v, L, n, np_=P):
    nc.vector.reciprocal(L.rstd[0:np_, 0:n], L.sd[0:np_, 0:n])
    v.drain()
    nc.vector.scalar_tensor_tensor(out=L.shift[0:np_, 0:n], in0=L.mv[0:np_, 0:n, 0], scalar=-1.0,
                                   in1=L.rstd[0:np_, 0:n], op0=ALU.mult, op1=ALU.mult)


def ln_bufs(s, n, name="ln", np_=P):
    L = Box()
    L.st = s.sb(name + "st", [np_, n, 6])
    L.mv = s.sb(name + "mv", [np_, n, 2])
    L.var, L.sd = s.sb(name + "var", [np_, n]), s.sb(name + "sd", [np_, n])
    L.rstd, L.shift = s.sb(name + "rstd", [np_, n]), s.sb(name + "shift", [np_, n])
    return L


def gat(nc, K, a, l):
    names = ["s_var", "s_sd", "s_sc", "s_ln", "s_xp", "s_in", "s_e", "s_er", "s_el", "s_l", "s_xj", "s_arg",
             "s_pj", "s_ex", "s_o", "s_h", "s_tr", "s_row", "s_st"]
    first_layer = l == 0
    NG = 2 if first_layer else 1
    with phase(nc, f"gat{l}", names, ["rec", "gat", "keep"]) as (block, s):
        rec = [s.sb(f"rec{u}", [P, T, REC]) for u in range(SLOTS)]
        g = [s.sb(f"g{u}", [P, NG * T, D]) for u in range(SLOTS)]
        if first_layer:
            L = ln_bufs(s, 2 * T)
            h = s.sb("h", [P, 2 * T, D])
            hdt = s.sb("hdt", [D, T, P])
        hst = s.sb("hst", [D, T, P])
        eat = s.sb("eat", [32, T, P])
        er, el = s.sb("er", [D, CH]), s.sb("el", [D, CH])
        m = s.sb("m", [D, CH + 1])
        low = s.sb("low", [D, CH])
        ta, tp = s.sb("ta", [D, CH]), s.sb("tp", [D, CH])
        xa, xp = s.sb("xa", [D, CH]), s.sb("xp", [D, CH])
        den, num = s.sb("den", [D, CH + 1]), s.sb("num", [D, CH + 1])
        wx = s.sb("wx", [D, CH])
        o = s.sb("o", [D, CH])
        ht = s.sb("ht", [D, T, P])
        orow = s.sb("orow", [P, T, D])
        ps_s = s.ps("s", [D, T, P])
        ps_d = s.ps("d", [D, T, P]) if first_layer else None
        ps_ea = s.ps("ea", [32, T, P])
        ps_xj, ps_e, ps_l = s.ps("xj", [D, CH]), s.ps("e", [D, CH]), s.ps("l", [D, CH])
        ps_o = s.ps("o", [P, T, D])
        flat = lambda b: b[:].rearrange("p t e -> p (t e)")

        @block.sync
        def _(sp):
            def load(i, u):
                sp.dma_start(rec[u][:], rows_of(K.recd, i * (SLOTS * CH) + u * CH)).then_inc(s.rec[u], 16)

            for u in range(SLOTS):
                load(0, u)

            def body(i, u, nxt):
                c = cnt(i, u)
                sp.wait_ge(s.s_row, c + 1)
                hold(sp, s)
                sp.dma_start(rows_of(K.tab[l], i * (SLOTS * CH) + u * CH), orow[:]).then_inc(s.s_st, 16)
                if first_layer:
                    sp.wait_ge(s.gat[u], (i + 1) * (16 * NG * T))
                    hold(sp, s)
                    sp.dma_start(rows_of(K.xs, i * (SLOTS * CH) + u * CH), g[u][:, 0:T, :]).then_inc(s.keep[u], 16)
                    sp.dma_start(rows_of(K.xd, i * (SLOTS * CH) + u * CH), g[u][:, T:2 * T, :]).then_inc(s.keep[u], 16)
                if not (isinstance(i, int) and i == K.NI - 1):
                    sp.wait_ge(s.gat[u], (i + 1) * (16 * NG * T))
                    hold(sp, s)
                    load(i + 1, u)

            rounds(sp, K, lambda: None, body)
            sp.wait_ge(s.s_st, 16 * K.NCH)
            if first_layer:
                for u in range(SLOTS):
                    sp.wait_ge(s.keep[u], 32 * K.NI)

        @block.gpsimd
        def _(gp):
            src = K.x if first_layer else K.tab[l - 1]
            words = (R_SRC, R_DST) if first_layer else (R_RHO,)

            def gathers(i, u):
                gp.wait_ge(s.rec[u], (i + 1) * 16)
                if again(i):
                    gp.wait_ge(s.s_xp, cnt(i - 1, u) + 1)
                    if first_layer:
                        gp.wait_ge(s.s_ln, cnt(i - 1, u) + 1)
                        gp.wait_ge(s.keep[u], i * 32)
                hold(gp, s)
                for n, w in enumerate(words):
                    for t in range(T):
                        nc.gpsimd.indirect_dma_start(
                            g[u][:, n * T + t, :], None, src[:, :],
                            bass.IndirectOffsetOnAxis(ap=rec[u][:].bitcast(I32)[:, t, w:w + 1], axis=0)
                        ).then_inc(s.gat[u], 16)

            ahead(gp, K, gathers)

        @block.tensor
        def _(pe):
            def front(i, u):
                c = cnt(i, u)
                rows = h if first_layer else g[u]
                if first_layer:
                    pe.wait_ge(s.s_ln, c + 1)
                else:
                    pe.wait_ge(s.gat[u], (i + 1) * (16 * NG * T))
                pe.wait_ge(s.rec[u], (i + 1) * 16)
                pe.wait_ge(s.s_in, c)
                for t in range(T):
                    nc.tensor.transpose(ps_s[:, t, :], rows[:, t, :], K.ident[0:P, 0:P])
                    if first_layer:
                        nc.tensor.transpose(ps_d[:, t, :], rows[:, T + t, :], K.ident[0:P, 0:P])
                    last = nc.tensor.transpose(ps_ea[:, t, :], rec[u][:, t, R_EA:R_EA + 32], K.ident[0:P, 0:P])
                last.then_inc(s.s_xp, 1)
                pe.wait_ge(s.s_in, c + 1)
                pe.wait_ge(s.s_el, c)
                nc.tensor.matmul(ps_e[:], K.wl[:, l, :], flat(hst), start=True, stop=False)
                hd = flat(hdt) if first_layer else K.hd[:, span(i, u)]
                nc.tensor.matmul(ps_e[:], K.wr[:, l, :], hd, start=False, stop=False)
                nc.tensor.matmul(ps_e[:], K.we[:, l, :], flat(eat), start=False, stop=True).then_inc(s.s_e, 1)

            def body(i, u, nxt):
                c = cnt(i, u)
                pe.wait_ge(s.s_el, c + 1)
                pe.wait_ge(s.s_arg, c)
                nc.tensor.matmul(ps_l[:], K.att[:, l, :], el[:], start=True, stop=True).then_inc(s.s_l, 1)
                pe.wait_ge(s.s_pj, c)
                nc.tensor.matmul(ps_xj[:], K.wl[:, l, :], flat(hst), start=True, stop=True).then_inc(s.s_xj, 1)
                if nxt:
                    front(*nxt)
                pe.wait_ge(s.s_h, c + 1)
                pe.wait_ge(s.s_row, c)
                for t in range(T):
                    last = nc.tensor.transpose(ps_o[:, t, :], ht[:, t, :], K.ident[:])
                last.then_inc(s.s_tr, 1)

            rounds(pe, K, lambda: front(0, 0), body)

        @block.scalar
        def _(act):
            def normed(i, u):
                c = cnt(i, u)
                act.wait_ge(s.s_var, c + 1)
                nc.scalar.activation(L.sd[:], L.var[:], ACT.Sqrt).then_inc(s.s_sd, 1)
                act.wait_ge(s.s_sc, c + 1)
                act.wait_ge(s.s_xp, c)
                for t in range(2 * T):
                    nc.scalar.activation(h[:, t, :], g[u][:, t, :], ACT.Relu, bias=L.shift[:, t:t + 1],
                                         scale=L.rstd[:, t:t + 1])
                nc.scalar.drain().then_inc(s.s_ln, 1)

            def front(i, u):
                c = cnt(i, u)
                if first_layer:
                    normed(i, u)
                act.wait_ge(s.s_xp, c + 1)
                act.wait_ge(s.s_e, c)
                act.wait_ge(s.s_xj, c)
                nc.scalar.copy(hst[:], ps_s[:])
                if first_layer:
                    nc.scalar.copy(hdt[:], ps_d[:])
                nc.scalar.copy(eat[:], ps_ea[:])
                nc.scalar.drain().then_inc(s.s_in, 1)
                act.wait_ge(s.s_e, c + 1)
                act.wait_ge(s.s_el, c)
                nc.scalar.activation(er[:], ps_e[:], ACT.Relu, scale=0.8).then_inc(s.s_er, 1)

            def body(i, u, nxt):
                c = cnt(i, u)
                act.wait_ge(s.s_arg, c + 1)
                nc.scalar.activation(xa[:], ta[:], ACT.Exp)
                nc.scalar.activation(xp[:], tp[:], ACT.Exp)
                nc.scalar.drain().then_inc(s.s_ex, 1)
                if nxt:
                    front(*nxt)
                act.wait_ge(s.s_o, c + 1)
                act.wait_ge(s.s_tr, c)
                fn = ACT.Relu if l < 2 else ACT.Identity
                nc.scalar.activation(flat(ht), o[:], fn, bias=K.bcol[:, l:l + 1])
                nc.scalar.activation(K.hd[:, span(i, u)], o[:], fn, bias=K.bcol[:, l:l + 1])
                nc.scalar.drain().then_inc(s.s_h, 1)
                act.wait_ge(s.s_tr, c + 1)
                act.wait_ge(s.s_st, c * 16)
                nc.scalar.copy(orow[:], ps_o[:]).then_inc(s.s_row, 1)

            rounds(act, K, lambda: front(0, 0), body)

        @block.vector
        def _(v):
            def normed(i, u):
                c = cnt(i, u)
                v.wait_ge(s.gat[u], (i + 1) * (16 * NG * T))
                v.wait_ge(s.s_ln, c)
                ln_stats(nc, v, L, g[u], 2 * T)
                nc.vector.drain().then_inc(s.s_var, 1)
                v.wait_ge(s.s_sd, c + 1)
                ln_scale(nc, v, L, 2 * T)
                nc.vector.drain().then_inc(s.s_sc, 1)

            def leaky(i, u):
                c = cnt(i, u)
                v.wait_ge(s.s_er, c + 1)
                v.wait_ge(s.s_l, c)
                nc.vector.scalar_tensor_tensor(out=el[:], in0=ps_e[:], scalar=0.2, in1=er[:], op0=ALU.mult,
                                               op1=ALU.add).then_inc(s.s_el, 1)

            def first():
                for b in (m, den, num):
                    nc.vector.memset(b[:, CH:CH + 1], 0.0)
                v.drain()
                if first_layer:
                    normed(0, 0)
                leaky(0, 0)

            def body(i, u, nxt):
                c = cnt(i, u)
                ns = K.nstart[:, span(i, u)]
                v.drain()
                for b in (m, den, num):
                    nc.vector.tensor_copy(b[:, 0:1], b[:, CH:CH + 1])
                nc.vector.tensor_scalar(low[:], ns, 2 * BIG, -BIG, ALU.mult, ALU.add)
                v.drain()
                v.wait_ge(s.s_l, c + 1)
                nc.vector.tensor_tensor_scan(m[:, 1:CH + 1], low[:], ps_l[:], m[:, 0:1], ALU.min, ALU.max)
                v.drain()
                v.wait_ge(s.s_ex, c)
                nc.vector.tensor_tensor(ta[:], m[:, 0:CH], m[:, 1:CH + 1], ALU.subtract)
                nc.vector.tensor_tensor(tp[:], ps_l[:], m[:, 1:CH + 1], ALU.subtract)
                v.drain()
                nc.vector.scalar_tensor_tensor(out=ta[:], in0=ta[:], scalar=0.0, in1=ns, op0=ALU.min, op1=ALU.mult)
                nc.vector.drain().then_inc(s.s_arg, 1)
                if nxt and first_layer:
                    normed(*nxt)
                v.wait_ge(s.s_ex, c + 1)
                v.wait_ge(s.s_xj, c + 1)
                nc.vector.tensor_tensor(xa[:], xa[:], ns, ALU.mult)
                nc.vector.tensor_tensor(wx[:], xp[:], ps_xj[:], ALU.mult)
                nc.vector.drain().then_inc(s.s_pj, 1)
                nc.vector.tensor_tensor_scan(den[:, 1:CH + 1], xa[:], xp[:], den[:, 0:1], ALU.mult, ALU.add)
                nc.vector.tensor_tensor_scan(num[:, 1:CH + 1], xa[:], wx[:], num[:, 0:1], ALU.mult, ALU.add)
                if nxt:
                    leaky(*nxt)
                v.drain()
                nc.vector.tensor_scalar(low[:], den[:, 1:CH + 1], 1e-16, None, ALU.add)
                v.drain()
                nc.vector.reciprocal(low[:], low[:])
                v.drain()
                v.wait_ge(s.s_h, c)
                nc.vector.tensor_tensor(o[:], num[:, 1:CH + 1], low[:], ALU.mult).then_inc(s.s_o, 1)

            rounds(v, K, first, body)


def gcn_messages(nc, K):
    names = ["s_hc", "s_dt", "s_x1", "s_sd", "s_sc", "s_h", "s_tm", "s_sum", "s_tr", "s_row",
             "s_st", "s_sv"]
    with phase(nc, "msg", names, ["rec", "ld", "gat", "stx"]) as (block, s):
        rec = [s.sb(f"rec{u}", [P, T, REC]) for u in range(SLOTS)]
        g = [s.sb(f"g{u}", [P, T, D]) for u in range(SLOTS)]
        x = [s.sb(f"x{u}", [P, 2 * T, D]) for u in range(SLOTS)]
        L = ln_bufs(s, 2 * T)
        sc, sh = s.sb("sc", [P, 3 * T]), s.sb("sh", [P, 3 * T])
        hc = s.sb("hc", [D, T, P])
        h = s.sb("h", [P, 3 * T, D])
        us = s.sb("us", [D, CH + 1])
        urow = s.sb("urow", [P, T, D])
        ps_d, ps_m, ps_u = s.ps("d", [P, T, D]), s.ps("m", [D, T, P]), s.ps("u", [P, T, D])

        @block.sync
        def _(sp):
            def loads(i, u):
                at = i * (SLOTS * CH) + u * CH
                if again(i):
                    prev = cnt(i - 1, u) + 1
                    sp.wait_ge(s.s_sc, prev)
                    hold(sp, s)
                    sp.wait_ge(s.s_h, prev)
                    hold(sp, s)
                    sp.wait_ge(s.stx[u], 32 * i)
                    hold(sp, s)
                    sp.wait_ge(s.gat[u], i * (16 * T))
                    hold(sp, s)
                sp.dma_start(rec[u][:], rows_of(K.recd, at)).then_inc(s.rec[u], 16)
                sp.dma_start(x[u][:, 0:T, :], rows_of(K.xs, at)).then_inc(s.ld[u], 16)
                sp.dma_start(x[u][:, T:2 * T, :], rows_of(K.xd, at)).then_inc(s.ld[u], 16)

            ahead(sp, K, loads)

        @block.gpsimd
        def _(gp):
            def gathers(i, u):
                gp.wait_ge(s.rec[u], (i + 1) * 16)
                if again(i):
                    gp.wait_ge(s.s_x1, cnt(i - 1, u) + 1)
                hold(gp, s)
                for t in range(T):
                    nc.gpsimd.indirect_dma_start(
                        g[u][:, t, :], None, K.tab[2][:, :],
                        bass.IndirectOffsetOnAxis(ap=rec[u][:].bitcast(I32)[:, t, R_RHO:R_RHO + 1], axis=0)
                    ).then_inc(s.gat[u], 16)

            ahead(gp, K, gathers)

        @block.tensor
        def _(pe):
            for i in peeled(pe, K.NI):
                for u in range(SLOTS):
                    c = cnt(i, u)
                    pe.wait_ge(s.s_hc, c + 1)
                    pe.wait_ge(s.s_x1, c)
                    for t in range(T):
                        last = nc.tensor.transpose(ps_d[:, t, :], hc[:, t, :], K.ident[:])
                    last.then_inc(s.s_dt, 1)
                    pe.wait_ge(s.s_h, c + 1)
                    pe.wait_ge(s.s_sum, c)
                    for t in range(T):
                        last = nc.tensor.transpose(ps_m[:, t, :], h[:, t, :], K.ident[0:P, 0:P])
                    last.then_inc(s.s_tm, 1)
                    pe.wait_ge(s.s_sum, c + 1)
                    pe.wait_ge(s.s_row, c)
                    for t in range(T):
                        last = nc.tensor.transpose(ps_u[:, t, :], us[:, 1 + t * P:1 + (t + 1) * P], K.ident[:])
                    last.then_inc(s.s_tr, 1)

        @block.scalar
        def _(act):
            for i in peeled(act, K.NI):
                for u in range(SLOTS):
                    c, at = cnt(i, u), i * (SLOTS * CH) + u * CH
                    act.wait_ge(s.s_dt, c)
                    hold(act, s)
                    nc.scalar.copy(hc[:].rearrange("p t e -> p (t e)"), K.hd[:, span(i, u)]).then_inc(s.s_hc, 1)
                    act.wait_ge(s.s_x1, c + 1)
                    act.dma_start(rows_of(K.xs, at), x[u][:, 0:T, :]).then_inc(s.stx[u], 16)
                    act.dma_start(rows_of(K.xd, at), x[u][:, T:2 * T, :]).then_inc(s.stx[u], 16)
                    nc.scalar.activation(L.sd[:], L.var[:], ACT.Sqrt).then_inc(s.s_sd, 1)
                    act.wait_ge(s.s_sc, c + 1)
                    act.wait_ge(s.s_tm, c)
                    act.wait_ge(s.s_sv, 32 * c)
                    for n in range(3):
                        for t in range(T):
                            nc.scalar.activation(h[:, n * T + t, :], x[u][:, (0, 0, T)[n] + t, :], ACT.Relu,
                                                 bias=sh[:, n * T + t:n * T + t + 1],
                                                 scale=sc[:, n * T + t:n * T + t + 1])
                    nc.scalar.drain().then_inc(s.s_h, 1)
                    act.wait_ge(s.s_h, c + 1)
                    act.dma_start(rows_of(K.vs, at), h[:, T:2 * T, :]).then_inc(s.s_sv, 16)
                    act.dma_start(rows_of(K.vd, at), h[:, 2 * T:3 * T, :]).then_inc(s.s_sv, 16)
                    act.wait_ge(s.s_tr, c + 1)
                    hold(act, s)
                    nc.scalar.copy(K.u[:, span(i, u)], us[:, 1:CH + 1])
                    act.wait_ge(s.s_st, 16 * c)
                    nc.scalar.copy(urow[:], ps_u[:])
                    nc.scalar.drain().then_inc(s.s_row, 1)
                    act.wait_ge(s.s_row, c + 1)
                    act.dma_start(rows_of(K.tabu, at), urow[:]).then_inc(s.s_st, 16)
            act.wait_ge(s.s_st, 16 * K.NCH)
            act.wait_ge(s.s_sv, 32 * K.NCH)
            for u in range(SLOTS):
                act.wait_ge(s.stx[u], 32 * K.NI)

        @block.vector
        def _(v):
            nc.vector.memset(us[:, CH:CH + 1], 0.0)
            v.drain()
            for i in peeled(v, K.NI):
                for u in range(SLOTS):
                    c = cnt(i, u)
                    v.wait_ge(s.gat[u], (i + 1) * (16 * T))
                    v.wait_ge(s.ld[u], (i + 1) * 32)
                    v.wait_ge(s.rec[u], (i + 1) * 16)
                    nc.vector.tensor_tensor(x[u][:, 0:T, :], x[u][:, 0:T, :], g[u][:], ALU.add)
                    v.wait_ge(s.s_dt, c + 1)
                    nc.vector.tensor_tensor(x[u][:, T:2 * T, :], x[u][:, T:2 * T, :], ps_d[:], ALU.add)
                    v.drain()
                    v.wait_ge(s.s_h, c)
                    ln_stats(nc, v, L, x[u], 2 * T)
                    nc.vector.drain().then_inc(s.s_x1, 1)
                    v.wait_ge(s.s_sd, c + 1)
                    ln_scale(nc, v, L, 2 * T)
                    v.drain()
                    for n, (w, t0) in enumerate(((R_CMSG, 0), (R_SELFS, 0), (R_SELFD, T))):
                        nc.vector.tensor_tensor(sc[:, n * T:(n + 1) * T], L.rstd[:, t0:t0 + T], rec[u][:, :, w], ALU.mult)
                        nc.vector.tensor_tensor(sh[:, n * T:(n + 1) * T], L.shift[:, t0:t0 + T], rec[u][:, :, w], ALU.mult)
                    nc.vector.drain().then_inc(s.s_sc, 1)
                    v.wait_ge(s.s_tr, c)
                    v.wait_ge(s.s_row, c)
                    nc.vector.tensor_copy(us[:, 0:1], us[:, CH:CH + 1])
                    v.drain()
                    v.wait_ge(s.s_tm, c + 1)
                    nc.vector.tensor_tensor_scan(us[:, 1:CH + 1], K.nstart[:, span(i, u)],
                                                 ps_m[:].rearrange("p t e -> p (t e)"), us[:, 0:1],
                                                 ALU.mult, ALU.add).then_inc(s.s_sum, 1)


def gcn_update(nc, K):
    names = ["s_y", "s_xp", "s_ys", "s_yt", "s_mm", "s_x2", "s_sd", "s_sc", "s_h", "s_sth"]
    with phase(nc, "upd", names, ["rec", "ld", "gat", "stx"]) as (block, s):
        rec = [s.sb(f"rec{u}", [P, T, REC]) for u in range(SLOTS)]
        g = [s.sb(f"g{u}", [P, T, D]) for u in range(SLOTS)]
        x = [s.sb(f"x{u}", [P, 2 * T, D]) for u in range(SLOTS)]
        vv = [s.sb(f"vv{u}", [P, 2 * T, D]) for u in range(SLOTS)]
        L = ln_bufs(s, T)
        yst, ydt = s.sb("yst", [D, T, P]), s.sb("ydt", [D, T, P])
        h = s.sb("h", [P, T, D])
        ps_s, ps_d = s.ps("s", [D, T, P]), s.ps("d", [D, T, P])
        ps_y = s.ps("y", [P, 2 * T, D])

        @block.sync
        def _(sp):
            def loads(i, u):
                at = i * (SLOTS * CH) + u * CH
                if again(i):
                    prev = cnt(i - 1, u) + 1
                    sp.wait_ge(s.s_h, prev)
                    hold(sp, s)
                    sp.wait_ge(s.s_xp, prev)
                    hold(sp, s)
                    sp.wait_ge(s.stx[u], 32 * i)
                    hold(sp, s)
                sp.dma_start(rec[u][:], rows_of(K.recd, at)).then_inc(s.rec[u], 16)
                sp.dma_start(x[u][:, 0:T, :], rows_of(K.xs, at)).then_inc(s.ld[u], 16)
                sp.dma_start(x[u][:, T:2 * T, :], rows_of(K.xd, at)).then_inc(s.ld[u], 16)
                sp.dma_start(vv[u][:, 0:T, :], rows_of(K.vs, at)).then_inc(s.ld[u], 16)
                sp.dma_start(vv[u][:, T:2 * T, :], rows_of(K.vd, at)).then_inc(s.ld[u], 16)

            ahead(sp, K, loads)

        @block.gpsimd
        def _(gp):
            def gathers(i, u):
                gp.wait_ge(s.rec[u], (i + 1) * 16)
                if again(i):
                    gp.wait_ge(s.s_y, cnt(i - 1, u) + 1)
                hold(gp, s)
                for t in range(T):
                    nc.gpsimd.indirect_dma_start(
                        g[u][:, t, :], None, K.tabu[:, :],
                        bass.IndirectOffsetOnAxis(ap=rec[u][:].bitcast(I32)[:, t, R_RHO:R_RHO + 1], axis=0)
                    ).then_inc(s.gat[u], 16)

            ahead(gp, K, gathers)

        @block.tensor
        def _(pe):
            for i in peeled(pe, K.NI):
                for u in range(SLOTS):
                    c = cnt(i, u)
                    pe.wait_ge(s.s_y, c + 1)
                    pe.wait_ge(s.s_yt, c)
                    for t in range(T):
                        nc.tensor.transpose(ps_s[:, t, :], vv[u][:, t, :], K.ident[0:P, 0:P])
                        last = nc.tensor.transpose(ps_d[:, t, :], vv[u][:, T + t, :], K.ident[0:P, 0:P])
                    last.then_inc(s.s_xp, 1)
                    pe.wait_ge(s.s_ys, c + 1)
                    pe.wait_ge(s.s_yt, c + 1)
                    pe.wait_ge(s.s_x2, c)
                    for t in range(T):
                        nc.tensor.matmul(ps_y[:, t, :], yst[:, t, :], K.w1[:], start=True, stop=True)
                        last = nc.tensor.matmul(ps_y[:, T + t, :], ydt[:, t, :], K.w1[:], start=True, stop=True)
                    last.then_inc(s.s_mm, 1)

        @block.scalar
        def _(act):
            for i in peeled(act, K.NI):
                for u in range(SLOTS):
                    c, at = cnt(i, u), i * (SLOTS * CH) + u * CH
                    act.wait_ge(s.s_xp, c + 1)
                    act.wait_ge(s.s_mm, c)
                    nc.scalar.copy(yst[:], ps_s[:]).then_inc(s.s_ys, 1)
                    act.wait_ge(s.s_x2, c + 1)
                    act.dma_start(rows_of(K.xs, at), x[u][:, 0:T, :]).then_inc(s.stx[u], 16)
                    act.dma_start(rows_of(K.xd, at), x[u][:, T:2 * T, :]).then_inc(s.stx[u], 16)
                    nc.scalar.activation(L.sd[:], L.var[:], ACT.Sqrt).then_inc(s.s_sd, 1)
                    act.wait_ge(s.s_sc, c + 1)
                    act.wait_ge(s.s_sth, 16 * c)
                    for t in range(T):
                        nc.scalar.activation(h[:, t, :], x[u][:, T + t, :], ACT.Relu, bias=L.shift[:, t:t + 1],
                                             scale=L.rstd[:, t:t + 1])
                    nc.scalar.drain().then_inc(s.s_h, 1)
                    act.wait_ge(s.s_h, c + 1)
                    act.dma_start(rows_of(K.h2, at), h[:]).then_inc(s.s_sth, 16)
            act.wait_ge(s.s_sth, 16 * K.NCH)
            for u in range(SLOTS):
                act.wait_ge(s.stx[u], 32 * K.NI)

        @block.vector
        def _(v):
            for i in peeled(v, K.NI):
                for u in range(SLOTS):
                    c = cnt(i, u)
                    v.wait_ge(s.gat[u], (i + 1) * (16 * T))
                    v.wait_ge(s.ld[u], (i + 1) * 64)
                    nc.vector.tensor_tensor(vv[u][:, 0:T, :], vv[u][:, 0:T, :], g[u][:], ALU.add)
                    bias = K.b1row[0:P, :].unsqueeze(1).to_broadcast((P, 2 * T, D))
                    nc.vector.tensor_tensor(x[u][:], x[u][:], bias, ALU.add)
                    nc.vector.drain().then_inc(s.s_y, 1)
                    v.wait_ge(s.s_xp, c + 1)
                    v.wait_ge(s.s_mm, c)
                    nc.vector.tensor_tensor(ydt[:].rearrange("p t e -> p (t e)"), ps_d[:].rearrange("p t e -> p (t e)"),
                                            K.u[:, span(i, u)], ALU.add)
                    v.wait_ge(s.s_ys, c + 1)
                    hold(v, s)
                    nc.vector.drain().then_inc(s.s_yt, 1)
                    v.wait_ge(s.s_mm, c + 1)
                    nc.vector.tensor_tensor(x[u][:], x[u][:], ps_y[:], ALU.add)
                    v.drain()
                    v.wait_ge(s.s_h, c)
                    ln_stats(nc, v, L, x[u][:, T:2 * T, :], T)
                    nc.vector.drain().then_inc(s.s_x2, 1)
                    v.wait_ge(s.s_sd, c + 1)
                    ln_scale(nc, v, L, T)
                    nc.vector.drain().then_inc(s.s_sc, 1)


def hop(nc, K, n):
    source = K.h2 if n == 0 else K.tabe[n - 1]
    word = J_POSD if n == 0 else J_LINK
    out = K.tabe[n] if n < 2 else K.taba
    names = ["s_m", "s_tm", "s_sum", "s_tr", "s_row", "s_st"]
    with phase(nc, f"hop{n}", names, ["rec", "gat"]) as (block, s):
        rec = [s.sb(f"rec{u}", [P, T, 4]) for u in range(SLOTS)]
        g = [s.sb(f"g{u}", [P, T, D]) for u in range(SLOTS)]
        m = s.sb("m", [P, T, D])
        es = s.sb("es", [D, CH + 1])
        ac = s.sb("ac", [D, CH])
        orow = s.sb("orow", [P, T, D])
        ps_m, ps_o = s.ps("m", [D, T, P]), s.ps("o", [P, T, D])

        @block.sync
        def _(sp):
            def loads(i, u):
                if again(i):
                    sp.wait_ge(s.s_m, cnt(i - 1, u) + 1)
                    hold(sp, s)
                sp.dma_start(rec[u][:], rows_of(K.recj, i * (SLOTS * CH) + u * CH)).then_inc(s.rec[u], 16)

            ahead(sp, K, loads)

        @block.gpsimd
        def _(gp):
            def gathers(i, u):
                gp.wait_ge(s.rec[u], (i + 1) * 16)
                hold(gp, s)
                for t in range(T):
                    nc.gpsimd.indirect_dma_start(
                        g[u][:, t, :], None, source[:, :],
                        bass.IndirectOffsetOnAxis(ap=rec[u][:].bitcast(I32)[:, t, word:word + 1], axis=0)
                    ).then_inc(s.gat[u], 16)

            ahead(gp, K, gathers)

        @block.scalar
        def _(act):
            for i in peeled(act, K.NI):
                for u in range(SLOTS):
                    c = cnt(i, u)
                    act.wait_ge(s.s_tr, c + 1)
                    act.wait_ge(s.s_st, 16 * c)
                    nc.scalar.copy(orow[:], ps_o[:]).then_inc(s.s_row, 1)
                    act.wait_ge(s.s_row, c + 1)
                    act.dma_start(rows_of(out, i * (SLOTS * CH) + u * CH), orow[:]).then_inc(s.s_st, 16)
            act.wait_ge(s.s_st, 16 * K.NCH)

        @block.tensor
        def _(pe):
            for i in peeled(pe, K.NI):
                for u in range(SLOTS):
                    c = cnt(i, u)
                    pe.wait_ge(s.s_m, c + 1)
                    for t in range(T):
                        last = nc.tensor.transpose(ps_m[:, t, :], m[:, t, :], K.ident[0:P, 0:P])
                    last.then_inc(s.s_tm, 1)
                    pe.wait_ge(s.s_sum, c + 1)
                    pe.wait_ge(s.s_row, c)
                    cols = es[:, 1:CH + 1] if n < 2 else ac[:]
                    for t in range(T):
                        last = nc.tensor.transpose(ps_o[:, t, :], cols[:, t * P:(t + 1) * P], K.ident[:])
                    last.then_inc(s.s_tr, 1)

        @block.vector
        def _(v):
            nc.vector.memset(es[:, CH:CH + 1], 0.0)
            v.drain()
            for i in peeled(v, K.NI):
                for u in range(SLOTS):
                    c = cnt(i, u)
                    v.wait_ge(s.gat[u], (i + 1) * (16 * T))
                    v.wait_ge(s.rec[u], (i + 1) * 16)
                    v.wait_ge(s.s_tm, c)
                    nc.vector.tensor_tensor(m[:], g[u][:], rec[u][:, :, J_W:J_W + 1].to_broadcast((P, T, D)), ALU.mult)
                    nc.vector.drain().then_inc(s.s_m, 1)
                    v.wait_ge(s.s_tr, c)
                    nc.vector.tensor_copy(es[:, 0:1], es[:, CH:CH + 1])
                    v.drain()
                    v.wait_ge(s.s_tm, c + 1)
                    nc.vector.tensor_tensor_scan(es[:, 1:CH + 1], K.nstart[:, span(i, u)],
                                                 ps_m[:].rearrange("p t e -> p (t e)"), es[:, 0:1], ALU.mult, ALU.add)
                    v.drain()
                    if n == 0:
                        nc.vector.tensor_copy(K.u[:, span(i, u)], es[:, 1:CH + 1])
                    elif n == 1:
                        nc.vector.tensor_tensor(K.u[:, span(i, u)], K.u[:, span(i, u)], es[:, 1:CH + 1], ALU.add)
                    else:
                        nc.vector.tensor_tensor(ac[:], K.u[:, span(i, u)], es[:, 1:CH + 1], ALU.add)
                    nc.vector.drain().then_inc(s.s_sum, 1)


def gate_messages(nc, K):
    names = ["s_var", "s_sd", "s_sc", "s_h2", "s_h3", "s_msg", "s_tm", "s_th", "s_ht", "s_lg", "s_sum", "s_ms", "s_tr",
             "s_made", "s_x3"]
    with phase(nc, "gate", names, ["rec", "ld", "gat", "sent"]) as (block, s):
        rec = [s.sb(f"rec{u}", [P, T, REC]) for u in range(SLOTS)]
        g = [s.sb(f"g{u}", [P, 2 * T, D]) for u in range(SLOTS)]
        x = [s.sb(f"x{u}", [P, 2 * T, D]) for u in range(SLOTS)]
        row = [s.sb(f"row{u}", [P, 2 * T, ROW]) for u in range(SLOTS)]
        L = ln_bufs(s, 2 * T)
        h = s.sb("h", [P, 2 * T, D])
        msg = s.sb("msg", [P, T, D])
        ht = s.sb("ht", [D, 2 * T, D])
        ms = s.sb("ms", [D, CH + 1])
        ps_m, ps_u = s.ps("m", [D, T, P]), s.ps("u", [P, T, D])
        ps_h = s.ps("h", [D, 2 * T, D])
        ps_g = s.ps("g", [P, 2 * T, HEADS])

        @block.sync
        def _(sp):
            def loads(i, u):
                at = i * (SLOTS * CH) + u * CH
                if again(i):
                    sp.wait_ge(s.sent[u], i * (16 * 2 * T))
                    hold(sp, s)
                sp.dma_start(rec[u][:], rows_of(K.recd, at)).then_inc(s.rec[u], 16)
                sp.dma_start(x[u][:, 0:T, :], rows_of(K.xs, at)).then_inc(s.ld[u], 16)
                sp.dma_start(x[u][:, T:2 * T, :], rows_of(K.xd, at)).then_inc(s.ld[u], 16)

            ahead(sp, K, loads)

        @block.gpsimd
        def _(gp):
            def gathers(i, u):
                gp.wait_ge(s.rec[u], (i + 1) * 16)
                hold(gp, s)
                for n, w in enumerate((R_SIGS, R_SIGD)):
                    for t in range(T):
                        nc.gpsimd.indirect_dma_start(
                            g[u][:, n * T + t, :], None, K.taba[:, :],
                            bass.IndirectOffsetOnAxis(ap=rec[u][:].bitcast(I32)[:, t, w:w + 1], axis=0)
                        ).then_inc(s.gat[u], 16)

            def scatters(i, u):
                gp.wait_ge(s.s_made, cnt(i, u) + 1)
                hold(gp, s)
                for n, w in enumerate((R_SIDX, R_DIDX)):
                    for t in range(T):
                        nc.gpsimd.indirect_dma_start(
                            K.rows[:, :],
                            bass.IndirectOffsetOnAxis(ap=rec[u][:].bitcast(I32)[:, t, w:w + 1], axis=0),
                            row[u][:, n * T + t, :], None, bounds_check=K.N - 1, oob_is_err=False
                        ).then_inc(s.sent[u], 16)

            def body(i, u, nxt):
                if nxt:
                    gathers(*nxt)
                scatters(i, u)

            rounds(gp, K, lambda: gathers(0, 0), body)
            for u in range(SLOTS):
                gp.wait_ge(s.sent[u], K.NI * (16 * 2 * T))

        @block.tensor
        def _(pe):
            for i in peeled(pe, K.NI):
                for u in range(SLOTS):
                    c = cnt(i, u)
                    pe.wait_ge(s.s_h3, c + 1)
                    pe.wait_ge(s.s_msg, c + 1)
                    pe.wait_ge(s.s_sum, c)
                    for t in range(T):
                        last = nc.tensor.transpose(ps_m[:, t, :], msg[:, t, :], K.ident[0:P, 0:P])
                    last.then_inc(s.s_tm, 1)
                    pe.wait_ge(s.s_ht, c)
                    for t in range(2 * T):
                        last = nc.tensor.transpose(ps_h[:, t, 0:P], h[:, t, :], K.ident[0:P, 0:P])
                    last.then_inc(s.s_th, 1)
                    pe.wait_ge(s.s_ht, c + 1)
                    pe.wait_ge(s.s_made, c)
                    for t in range(2 * T):
                        last = nc.tensor.matmul(ps_g[:, t, :], ht[:, t, 0:P], K.wd[:], start=True, stop=True)
                    last.then_inc(s.s_lg, 1)
                    pe.wait_ge(s.s_sum, c + 1)
                    for t in range(T):
                        last = nc.tensor.transpose(ps_u[:, t, :], ms[:, 1 + t * P:1 + (t + 1) * P], K.ident[:])
                    last.then_inc(s.s_tr, 1)

        @block.scalar
        def _(act):
            for i in peeled(act, K.NI):
                for u in range(SLOTS):
                    c = cnt(i, u)
                    for half in (0, 1):
                        act.wait_ge(s.s_var, 2 * c + half + 1)
                        nc.scalar.activation(L.sd[:], L.var[:], ACT.Sqrt).then_inc(s.s_sd, 1)
                        act.wait_ge(s.s_sc, 2 * c + half + 1)
                        if half == 0:
                            act.wait_ge(s.s_th, c)
                            act.wait_ge(s.s_made, c)
                        src = x[u] if half == 0 else row[u]
                        for t in range(2 * T):
                            nc.scalar.activation(h[:, t, :], src[:, t, 0:D], ACT.Relu, bias=L.shift[:, t:t + 1],
                                                 scale=L.rstd[:, t:t + 1])
                        nc.scalar.drain().then_inc((s.s_h2, s.s_h3)[half], 1)
                    act.wait_ge(s.s_th, c + 1)
                    act.wait_ge(s.s_lg, c)
                    nc.scalar.copy(ht[:, :, 0:P], ps_h[:, :, 0:P]).then_inc(s.s_ht, 1)

        @block.vector
        def _(v):
            nc.vector.memset(ms[:, CH:CH + 1], 0.0)
            v.drain()
            for i in peeled(v, K.NI):
                for u in range(SLOTS):
                    c = cnt(i, u)
                    v.wait_ge(s.ld[u], (i + 1) * 32)
                    v.wait_ge(s.s_h3, c)
                    ln_stats(nc, v, L, x[u], 2 * T)
                    nc.vector.drain().then_inc(s.s_var, 1)
                    v.wait_ge(s.s_sd, 2 * c + 1)
                    ln_scale(nc, v, L, 2 * T)
                    nc.vector.drain().then_inc(s.s_sc, 1)
                    v.wait_ge(s.s_h2, c + 1)
                    v.wait_ge(s.gat[u], (i + 1) * (16 * 2 * T))
                    nc.vector.tensor_tensor(g[u][:], g[u][:], h[:], ALU.add)
                    v.drain()
                    nc.vector.scalar_tensor_tensor(out=row[u][:, :, 0:D], in0=g[u][:], scalar=0.25, in1=x[u][:],
                                                   op0=ALU.mult, op1=ALU.add)
                    v.drain()
                    ln_stats(nc, v, L, row[u][:, :, 0:D], 2 * T)
                    nc.vector.drain().then_inc(s.s_var, 1)
                    v.wait_ge(s.s_sd, 2 * c + 2)
                    ln_scale(nc, v, L, 2 * T)
                    nc.vector.drain().then_inc(s.s_sc, 1)
                    v.wait_ge(s.rec[u], (i + 1) * 16)
                    v.wait_ge(s.s_h3, c + 1)
                    nc.vector.tensor_tensor(msg[:], h[:, 0:T, :], rec[u][:, :, R_CMSG3:R_CMSG3 + 1].to_broadcast((P, T, D)),
                                            ALU.mult)
                    nc.vector.drain().then_inc(s.s_msg, 1)
                    nc.vector.tensor_copy(row[u][:, 0:T, D:2 * D], h[:, 0:T, :])
                    nc.vector.tensor_tensor(row[u][:, T:2 * T, D:2 * D], h[:, T:2 * T, :],
                                            rec[u][:, :, R_SELF3:R_SELF3 + 1].to_broadcast((P, T, D)), ALU.mult)
                    v.wait_ge(s.s_tr, c)
                    nc.vector.tensor_copy(ms[:, 0:1], ms[:, CH:CH + 1])
                    v.drain()
                    v.wait_ge(s.s_tm, c + 1)
                    nc.vector.tensor_tensor_scan(ms[:, 1:CH + 1], K.nstart[:, span(i, u)],
                                                 ps_m[:].rearrange("p t e -> p (t e)"), ms[:, 0:1],
                                                 ALU.mult, ALU.add).then_inc(s.s_sum, 1)
                    v.wait_ge(s.s_lg, c + 1)
                    nc.vector.tensor_tensor(row[u][:, :, 2 * D:ROW], ps_g[:],
                                            K.bdrow[0:P, :].unsqueeze(1).to_broadcast((P, 2 * T, HEADS)), ALU.add)
                    v.wait_ge(s.s_tr, c + 1)
                    nc.vector.tensor_tensor(row[u][:, T:2 * T, D:2 * D], row[u][:, T:2 * T, D:2 * D], ps_u[:], ALU.add)
                    nc.vector.drain().then_inc(s.s_made, 1)


def groups(eng, K, body):
    for i in peeled(eng, K.NGI):
        for u in range(DSLOTS):
            body(i, u, D, i * (DSLOTS * GT * D) + u * (GT * D))
    if K.REM:
        body(K.NGI, 0, K.REM, K.NGI * DSLOTS * GT * D)


def dense_first(nc, K):
    names = ["s_x1", "s_var", "s_sd", "s_sc", "s_h", "s_tp", "s_ct", "s_mm"]
    n3 = lambda i, u, j: (i * DSLOTS + u) * 3 + j
    with phase(nc, "first", names, ["ld", "st"], DSLOTS) as (block, s):
        ld, st = s.ld, s.st
        x = [s.sb(f"x{u}", [D, GT, D]) for u in range(DSLOTS)]
        row = [s.sb(f"row{u}", [D, GT, ROW]) for u in range(DSLOTS)]
        h = s.sb("h", [D, GT, D])
        ht = s.sb("ht", [D, GT, D])
        L = ln_bufs(s, GT, np_=D)
        ps_t, ps_y = s.ps("t", [D, 8, D]), s.ps("y", [D, 8, D])
        ps_g = s.ps("g", [D, GT, HEADS])

        @block.sync
        def _(sp):
            def body(i, u, q, at):
                sp.wait_ge(st[u], i * 16)
                hold(sp, s)
                sp.dma_start(x[u][0:q], K.x[bass.ds(at, q * GT), :].rearrange("(p t) d -> p t d", t=GT)).then_inc(ld[u], 16)

            groups(sp, K, body)

        @block.vector
        def _(v):
            def norm(k, src, q):
                v.wait_ge(s.s_h, k)
                ln_stats(nc, v, L, src, GT)
                nc.vector.drain().then_inc(s.s_var, 1)
                v.wait_ge(s.s_sd, k + 1)
                ln_scale(nc, v, L, GT, q)
                nc.vector.drain().then_inc(s.s_sc, 1)

            def body(i, u, q, at):
                c = i * DSLOTS + u
                wide = lambda b: b[0:q, :].unsqueeze(1).to_broadcast((q, GT, D))
                v.wait_ge(ld[u], (i + 1) * 16)
                v.wait_ge(st[u], i * 16)
                nc.vector.tensor_tensor(x[u][0:q], x[u][0:q], wide(K.b2row), ALU.add)
                v.drain()
                norm(n3(i, u, 0), x[u][0:q], q)
                v.wait_ge(s.s_h, n3(i, u, 1))
                nc.vector.tensor_tensor(x[u][0:q], x[u][0:q], wide(K.b1row), ALU.add)
                v.drain()
                v.wait_ge(s.s_mm, 2 * c + 1)
                nc.vector.tensor_tensor(x[u][0:q], x[u][0:q], ps_y[0:q, 0:GT, :], ALU.add)
                v.drain()
                norm(n3(i, u, 1), x[u][0:q], q)
                v.wait_ge(s.s_h, n3(i, u, 2))
                nc.vector.scalar_tensor_tensor(out=row[u][0:q, :, 0:D], in0=h[0:q], scalar=0.25, in1=x[u][0:q],
                                               op0=ALU.mult, op1=ALU.add)
                v.drain()
                norm(n3(i, u, 2), row[u][0:q, :, 0:D], q)
                v.wait_ge(s.s_h, n3(i, u, 3))
                nc.vector.tensor_copy(row[u][0:q, :, D:2 * D], h[0:q])
                v.wait_ge(s.s_mm, 2 * c + 2)
                nc.vector.tensor_tensor(row[u][0:q, :, 2 * D:ROW], ps_g[0:q],
                                        K.bdrow[0:q, :].unsqueeze(1).to_broadcast((q, GT, HEADS)), ALU.add)
                nc.vector.drain().then_inc(s.s_x1, 1)

            groups(v, K, body)

        @block.scalar
        def _(act):
            def body(i, u, q, at):
                c = i * DSLOTS + u
                for j in range(3):
                    k = n3(i, u, j)
                    act.wait_ge(s.s_var, k + 1)
                    nc.scalar.activation(L.sd[0:q], L.var[0:q], ACT.Sqrt).then_inc(s.s_sd, 1)
                    act.wait_ge(s.s_sc, k + 1)
                    if j == 1:
                        act.wait_ge(s.s_tp, 2 * c + 1)
                    if j == 0:
                        act.wait_ge(s.s_tp, 2 * c)
                        act.wait_ge(s.s_x1, c)
                    src = x[u] if j < 2 else row[u]
                    for t in range(GT):
                        nc.scalar.activation(h[0:q, t, :], src[0:q, t, 0:D], ACT.Relu, bias=L.shift[0:q, t:t + 1],
                                             scale=L.rstd[0:q, t:t + 1])
                    nc.scalar.drain().then_inc(s.s_h, 1)
                    if j != 1:
                        k = 2 * c + (j == 2)
                        act.wait_ge(s.s_tp, k + 1)
                        act.wait_ge(s.s_mm, k)
                        nc.scalar.copy(ht[:, :, 0:q], ps_t[:, 0:GT, 0:q]).then_inc(s.s_ct, 1)
                act.wait_ge(s.s_x1, c + 1)
                act.dma_start(K.rows[bass.ds(at, q * GT), :].rearrange("(p t) d -> p t d", t=GT), row[u][0:q]).then_inc(st[u], 16)

            groups(act, K, body)
            for u in range(DSLOTS):
                act.wait_ge(st[u], 16 * (K.NGI + (1 if K.REM and u == 0 else 0)))

        @block.tensor
        def _(pe):
            def body(i, u, q, at):
                c = i * DSLOTS + u
                for j in range(2):
                    pe.wait_ge(s.s_h, n3(i, u, 1 + 2 * j))
                    pe.wait_ge(s.s_ct, 2 * c + j)
                    for t in range(GT):
                        last = nc.tensor.transpose(ps_t[:, t, 0:q], h[0:q, t, :], K.ident[0:q, 0:q])
                    last.then_inc(s.s_tp, 1)
                    pe.wait_ge(s.s_ct, 2 * c + j + 1)
                    pe.wait_ge(s.s_x1, c)
                    for t in range(GT):
                        out, w = ((ps_y[0:q, t, :], K.w1[:]), (ps_g[0:q, t, :], K.wd[:]))[j]
                        last = nc.tensor.matmul(out, ht[:, t, 0:q], w, start=True, stop=True)
                    last.then_inc(s.s_mm, 1)

            groups(pe, K, body)


def dense_last(nc, K):
    ZB = DSLOTS
    names = ["s_tp", "s_ct", "s_mx", "s_exp", "s_dn", "s_init"]
    with phase(nc, "last", names, ["ld", "st", "comb", "zdone", "zread"], DSLOTS) as (block, s):
        ld, st, comb, zdone, zread = s.ld, s.st, s.comb, s.zdone, s.zread
        row = [s.sb(f"row{u}", [D, GT, ROW]) for u in range(DSLOTS)]
        at_ = [s.sb(f"at{u}", [D, GT, D]) for u in range(DSLOTS)]
        z = [s.sb(f"z{u}", [D, GT, HEADS, D]) for u in range(DSLOTS)]
        gate = s.sb("gate", [D, GT, HEADS])
        sm, rs = s.sb("sm", [D, GT]), s.sb("rs", [D, GT])
        ps_t = s.ps("t", [D, 8, D])
        ps_z = [s.ps(f"z{n}", [D, HEADS, D]) for n in range(ZB)]

        @block.sync
        def _(sp):
            def body(i, u, q, at):
                sp.wait_ge(st[u], i * 16)
                hold(sp, s)
                sp.dma_start(row[u][0:q], K.rows[bass.ds(at, q * GT), :].rearrange("(p t) d -> p t d", t=GT)).then_inc(ld[u], 16)

            groups(sp, K, body)

        @block.gpsimd
        def _(g):
            def body(i, u, q, at):
                g.wait_ge(comb[u], i + 1)
                g.dma_start(K.out[bass.ds(at, q * GT), :].rearrange("(p t) d -> p t d", t=GT), row[u][0:q, :, 0:D]).then_inc(st[u], 16)

            groups(g, K, body)
            for u in range(DSLOTS):
                g.wait_ge(st[u], 16 * (K.NGI + (1 if K.REM and u == 0 else 0)))

        @block.tensor
        def _(pe):
            def body(i, u, q, at):
                c = i * DSLOTS + u
                pe.wait_ge(ld[u], (i + 1) * 16)
                pe.wait_ge(s.s_ct, c)
                for t in range(GT):
                    last = nc.tensor.transpose(ps_t[:, t, 0:q], row[u][0:q, t, D:2 * D], K.ident[0:q, 0:q])
                last.then_inc(s.s_tp, 1)
                pe.wait_ge(s.s_ct, c + 1)
                for t in range(GT):
                    j = u * GT + t
                    pe.wait_ge(zread[j % ZB], i * (DSLOTS * GT // ZB) + j // ZB)
                    for half in (0, 1):
                        hs = slice(half * 4, half * 4 + 4)
                        nc.tensor.matmul(ps_z[j % ZB][0:q, hs, :], at_[u][:, t, 0:q], K.w3[:, hs, :], start=True, stop=False)
                        last = nc.tensor.matmul(ps_z[j % ZB][0:q, hs, :], K.onesb[0:3, 0:q], K.b3s[:, hs, :],
                                                start=False, stop=True)
                    last.then_inc(zdone[j % ZB], 1)

            groups(pe, K, body)

        @block.scalar
        def _(act):
            def body(i, u, q, at):
                c = i * DSLOTS + u
                act.wait_ge(s.s_tp, c + 1)
                act.wait_ge(comb[u], i)
                nc.scalar.copy(at_[u][:, :, 0:q], ps_t[:, 0:GT, 0:q]).then_inc(s.s_ct, 1)
                act.wait_ge(s.s_mx, c + 1)
                nc.scalar.activation(gate[0:q], gate[0:q], ACT.Exp).then_inc(s.s_exp, 1)
                for t in range(GT):
                    j = u * GT + t
                    act.wait_ge(zdone[j % ZB], i * (DSLOTS * GT // ZB) + j // ZB + 1)
                    nc.scalar.activation(z[u][0:q, t], ps_z[j % ZB][0:q], ACT.Relu).then_inc(zread[j % ZB], 1)

            groups(act, K, body)

        @block.vector
        def _(v):
            def body(i, u, q, at):
                c = i * DSLOTS + u
                per = DSLOTS * GT // ZB
                lg = row[u][0:q, :, 2 * D:ROW]
                v.wait_ge(ld[u], (i + 1) * 16)
                nc.vector.tensor_reduce(out=sm[0:q], in_=lg, axis=mybir.AxisListType.X, op=ALU.max)
                v.drain()
                nc.vector.tensor_tensor(gate[0:q], lg, sm[0:q].unsqueeze(2).to_broadcast((q, GT, HEADS)), ALU.subtract)
                nc.vector.drain().then_inc(s.s_mx, 1)
                v.wait_ge(s.s_exp, c + 1)
                nc.vector.tensor_reduce(out=sm[0:q], in_=gate[0:q], axis=mybir.AxisListType.X, op=ALU.add)
                v.drain()
                nc.vector.reciprocal(rs[0:q], sm[0:q])
                v.drain()
                nc.vector.tensor_tensor(gate[0:q], gate[0:q], rs[0:q].unsqueeze(2).to_broadcast((q, GT, HEADS)), ALU.mult)
                v.drain()
                for t in range(GT):
                    j = u * GT + t
                    v.wait_ge(zread[j % ZB], i * per + j // ZB + 1)
                for k in range(HEADS):
                    for t in range(GT):
                        nc.vector.scalar_tensor_tensor(out=row[u][0:q, t, 0:D], in0=z[u][0:q, t, k, :],
                                                       scalar=gate[0:q, t, k:k + 1], in1=row[u][0:q, t, 0:D],
                                                       op0=ALU.mult, op1=ALU.add)
                    v.drain()
                nc.vector.drain().then_inc(comb[u], 1)

            groups(v, K, body)


def build(nc, a, out):
    K = Box()
    K.N, K.E = a["x"].shape[0], a["src"].shape[0]
    K.NT, K.NCH = K.E // P, K.E // CH
    K.NI = K.NCH // SLOTS
    assert K.E == K.NI * SLOTS * CH and K.NT <= D
    K.NP = -(-K.N // LO)
    K.NGI, rest = divmod(K.N, DSLOTS * GT * D)
    K.REM = rest // GT
    assert rest == K.REM * GT and K.REM <= D
    K.x, K.out = a["x"], out
    dram = lambda name, shape: nc.dram_tensor(name, shape, F32, kind="Internal").ap()
    K.info = dram("node_info", (K.NP * LO, 4))
    K.recd, K.recj = dram("records_d", (K.E, REC)), dram("records_j", (K.E, 4))
    K.tab = [dram(f"gat_out{l}", (K.E + 1, D)) for l in range(3)]
    K.tabu, K.taba = dram("gcn_sum", (K.E + 1, D)), dram("hops_sum", (K.E + 1, D))
    K.tabe = [dram(f"hop{n}", (K.E + 1, D)) for n in range(2)]
    K.xs, K.xd, K.vs, K.vd, K.h2 = (dram(n, (K.E, D)) for n in ("x_src", "x_dst", "self_src", "self_dst", "h2_dst"))
    K.rows = dram("node_rows", (K.N, ROW))
    with ExitStack() as ctx:
        sb = lambda c, n, shape, dt=F32: c.enter_context(nc.sbuf_tensor("k_" + n, shape, dt))
        K.wl, K.wr, K.we = sb(ctx, "wl", [D, 3, D]), sb(ctx, "wr", [D, 3, D]), sb(ctx, "we", [32, 3, D])
        K.att, K.bcol = sb(ctx, "att", [D, 3, D]), sb(ctx, "bcol", [D, 3])
        K.w1, K.w3, K.wd = sb(ctx, "w1", [D, D]), sb(ctx, "w3", [D, HEADS, D]), sb(ctx, "wd", [D, HEADS])
        K.b1row, K.b2row, K.bdrow = sb(ctx, "b1row", [D, D]), sb(ctx, "b2row", [D, D]), sb(ctx, "bdrow", [D, HEADS])
        K.b3s = sb(ctx, "b3s", [3, HEADS, D], BF16)
        K.ident, K.identb = sb(ctx, "ident", [D, D]), sb(ctx, "identb", [D, D], BF16)
        K.onesb = sb(ctx, "onesb", [D, D], BF16)
        with ExitStack() as c1:
            K.before, K.carry, K.block2 = sb(c1, "before", [D, D]), sb(c1, "carry", [D, D]), sb(c1, "block2", [D, D])
            K.iota, K.part = sb(c1, "iota", [D, LO]), sb(c1, "part", [D, 1])
            K.cnt = {k: sb(c1, f"cnt_{k}", [K.NP, LO]) for k in ("src", "dst")}
            K.col = {k: sb(c1, f"col_{k}", [P, K.NT]) for k in ("src", "dst")}
            K.occ = {k: sb(c1, f"occ_{k}", [P, K.NT]) for k in ("src", "dst")}
            K.wcol = sb(c1, "wcol", [P, K.NT])
            constants(nc, K, a)
            dense_first(nc, K)
            ranks(nc, K, a)
            node_table(nc, K)
            records(nc, K, a)
        with ExitStack() as c2:
            K.nstart = sb(c2, "nstart", [D, K.E], BF16)
            K.nlast = sb(c2, "nlast", [D, K.E], BF16)
            K.hd = K.u = sb(c2, "hd", [D, K.E])
            flags(nc, K, "flags_d", K.recd, (R_NSTART, R_NLAST), (K.nstart, K.nlast), REC)
            for l in range(3):
                gat(nc, K, a, l)
                spread_back(nc, K, f"spread{l}", K.hd)
            gcn_messages(nc, K)
            spread_back(nc, K, "spread_u", K.u)
            gcn_update(nc, K)
            flags(nc, K, "flags_j", K.recj, (J_NSTART,), (K.nstart,), 4)
            for n in range(3):
                hop(nc, K, n)
        with ExitStack() as c2:
            K.nstart = sb(c2, "nstart2", [D, K.E], BF16)
            flags(nc, K, "flags_3", K.recd, (R_NSTART,), (K.nstart,), REC)
            gate_messages(nc, K)
        dense_last(nc, K)


_INS = ["x", "src", "dst", "edge_attr_32", "edge_weight"] + [
    f"L0_gnn_{w}{l}" for l in range(3) for w in ("Wl", "Wr", "We", "att", "b")] + [
    "L1_gnn_weight", "L1_gnn_bias", "L3_gnn_W", "L3_gnn_b", "L3_gnn_W_dict", "L3_gnn_b_dict"]


def kernel(**inputs):
    import numpy as _np
    import concourse.bacc as _bacc
    from concourse.bass_utils import run_bass_kernel_spmd as _run

    nc = _bacc.Bacc("TRN2", target_bir_lowering=False, num_devices=1)
    arrays, args = {}, {}
    for name in _INS:
        v = _np.ascontiguousarray(inputs[name])
        arrays[f"in_{name}"] = v
        args[name] = nc.dram_tensor(f"in_{name}", v.shape, mybir.dt.from_np(v.dtype), kind="ExternalInput").ap()
    shape = inputs["x"].shape
    out = nc.dram_tensor("out", shape, F32, kind="ExternalOutput").ap()
    build(nc, args, out)
    return _run(nc, [arrays], core_ids=[0]).results[0]["out"]
```

```python
import concourse.bass as bass
from concourse import mybir
from contextlib import ExitStack, contextmanager

F32, I32, BF16 = mybir.dt.float32, mybir.dt.int32, mybir.dt.bfloat16
ALU, ACT = mybir.AluOpType, mybir.ActivationFunctionType
D = 128
P = 125
T = 4
CH = P * T
SLOTS = 5
REC = 48
LO = 512
BIG = 1e30
FAR = 1 << 20
EPS = 1e-5
GT = 5
DSLOTS = 3
ROW = 2 * D + 8
HEADS = 8
R_RHO, R_SIGS, R_SIGD, R_SIDX, R_DIDX = 0, 1, 2, 3, 4
R_CMSG, R_SELFS, R_SELFD, R_CMSG3, R_SELF3, R_NSTART, R_NLAST = 5, 6, 7, 8, 9, 10, 11
R_SRC, R_DST = 12, 13
R_EA = 16
J_LINK, J_POSD, J_W, J_NSTART = 0, 1, 2, 3


class Box:
    pass


@contextmanager
def phase(nc, at, names, slots=(), each=SLOTS):
    one = {name: nc.alloc_semaphore(f"{at}_{name}") for name in ("s_held", *names)}
    many = {name: [nc.alloc_semaphore(f"{at}_{name}{u}") for u in range(each)] for name in slots}
    every = [*one.values(), *(h for hs in many.values() for h in hs)]
    s = type("Semaphores", (), {**one, **many, "by_name": one})()
    with ExitStack() as bufs:
        s.sb = lambda name, shape, dt=F32: bufs.enter_context(nc.sbuf_tensor(f"{at}_{name}", shape, dt))
        s.ps = lambda name, shape, dt=F32: bufs.enter_context(nc.psum_tensor(f"{at}_ps_{name}", shape, dt))
        with nc.Block() as block:
            yield block, s
    nc.clear_and_free_semaphores(every)
    nc.all_engine_barrier()


def hold(eng, s):
    eng.sem_inc(s.s_held, 1)


def peeled(eng, n):
    if n > 0:
        yield 0
    if n > 1:
        with eng.Fori(1, n) as i:
            yield i


def rows_of(dram, start, n=CH):
    return dram[bass.ds(start, n), :].rearrange("(t p) d -> p t d", p=P)


def constants(nc, K, a):
    with phase(nc, "const", ["s_load", "s_set", "s_sel", "s_dma2", "s_z"]) as (block, s):
        att_c = s.sb("att_c", [D, 3, 1])
        bsrc = s.sb("bsrc", [1, 4, D])
        zero = s.sb("zero", [1, D])
        iota_i = s.sb("iota_i", [D, LO], I32)
        part_i = s.sb("part_i", [D, 1], I32)
        b3 = s.sb("b3", [1, HEADS * D])
        b3p = [s.sb(f"b3p{n}", [1, HEADS * D], BF16) for n in range(3)]
        NLOADS = 3 * 5 + 10

        @block.sync
        def _(sp):
            for l in range(3):
                sp.dma_start(K.wl[:, l, :], a[f"L0_gnn_Wl{l}"][:, :]).then_inc(s.s_load, 16)
                sp.dma_start(K.wr[:, l, :], a[f"L0_gnn_Wr{l}"][:, :]).then_inc(s.s_load, 16)
                sp.dma_start(K.we[:, l, :], a[f"L0_gnn_We{l}"][:, :]).then_inc(s.s_load, 16)
                sp.dma_start(att_c[:, l, :], a[f"L0_gnn_att{l}"].rearrange("h (c o) -> (h c) o", o=1)).then_inc(s.s_load, 16)
                sp.dma_start(K.bcol[:, l:l + 1], a[f"L0_gnn_b{l}"].rearrange("(p o) -> p o", o=1)).then_inc(s.s_load, 16)
            for l in range(3):
                sp.dma_start(bsrc[:, l, :], a[f"L0_gnn_b{l}"].rearrange("(o d) -> o d", o=1)).then_inc(s.s_load, 16)
            sp.dma_start(K.w1[:], a["L1_gnn_weight"][:, :]).then_inc(s.s_load, 16)
            sp.dma_start(K.w3[:], a["L3_gnn_W"].rearrange("k i o -> i k o")).then_inc(s.s_load, 16)
            sp.dma_start(K.wd[:], a["L3_gnn_W_dict"][:, :]).then_inc(s.s_load, 16)
            sp.dma_start(K.b2row[:], a["L0_gnn_b2"].rearrange("(o d) -> o d", o=1).to_broadcast((D, D))).then_inc(s.s_load, 16)
            sp.dma_start(K.b1row[:], a["L1_gnn_bias"].rearrange("(o d) -> o d", o=1).to_broadcast((D, D))).then_inc(s.s_load, 16)
            sp.dma_start(K.bdrow[:], a["L3_gnn_b_dict"].rearrange("(o d) -> o d", o=1).to_broadcast((D, HEADS))).then_inc(s.s_load, 16)
            sp.dma_start(b3[:], a["L3_gnn_b"].rearrange("(o k) d -> o (k d)", o=1)).then_inc(s.s_load, 16)
            sp.wait_ge(s.s_z, 2)
            for l in range(3):
                sp.dma_start(K.tab[l][K.E:K.E + 1, :], bsrc[:, l, :]).then_inc(s.s_dma2, 16)
            for t in (K.tabu, *K.tabe, K.taba):
                sp.dma_start(t[K.E:K.E + 1, :], zero[:]).then_inc(s.s_dma2, 16)
            for n in range(3):
                sp.dma_start(K.b3s[n:n + 1, :, :].rearrange("p k d -> p (k d)"), b3p[n][:]).then_inc(s.s_dma2, 16)
            sp.wait_ge(s.s_dma2, 16 * (6 + 2 + len(K.tabe)))

        @block.gpsimd
        def _(g):
            nc.gpsimd.memset(K.ident[:], 0.0)
            nc.gpsimd.memset(K.before[:], 1.0)
            nc.gpsimd.memset(K.carry[:], 1.0)
            nc.gpsimd.memset(K.onesb[:], 1.0)
            nc.gpsimd.iota(iota_i[:], pattern=[[1, LO]], base=0, channel_multiplier=0)
            nc.gpsimd.iota(part_i[:], pattern=[[0, 1]], base=0, channel_multiplier=1)
            g.drain()
            nc.gpsimd.affine_select(out=K.ident[:], in_=K.ident[:], compare_op=ALU.not_equal, fill=1.0,
                                    base=0, pattern=[[-1, D]], channel_multiplier=1)
            nc.gpsimd.affine_select(out=K.before[:], in_=K.before[:], compare_op=ALU.is_gt, fill=0.0,
                                    base=0, pattern=[[-1, D]], channel_multiplier=1)
            nc.gpsimd.affine_select(out=K.carry[:], in_=K.carry[:], compare_op=ALU.is_gt, fill=0.0,
                                    base=0, pattern=[[1, D]], channel_multiplier=-1)
            nc.gpsimd.drain().then_inc(s.s_set, 1)

        @block.vector
        def _(v):
            nc.vector.memset(K.block2[:], 0.0)
            v.drain()
            nc.vector.memset(K.block2[0:64, 0:64], 1.0)
            nc.vector.memset(K.block2[64:128, 64:128], 1.0)
            v.wait_ge(s.s_set, 1)
            nc.vector.tensor_copy(K.identb[:], K.ident[:])
            nc.vector.tensor_copy(K.iota[:], iota_i[:])
            nc.vector.tensor_copy(K.part[:], part_i[:])
            nc.vector.memset(zero[:], 0.0).then_inc(s.s_z, 1)
            v.drain()
            v.wait_ge(s.s_load, 16 * NLOADS)
            for l in range(3):
                nc.vector.tensor_scalar(K.att[:, l, :], K.block2[:], att_c[:, l, :], None, ALU.mult)
            for l in range(2):
                nc.vector.tensor_scalar(bsrc[:, l, :], bsrc[:, l, :], 0.0, None, ALU.max)
            for n in range(3):
                nc.vector.tensor_copy(b3p[n][:], b3[:])
                v.drain()
                if n < 2:
                    nc.vector.tensor_tensor(b3[:], b3[:], b3p[n][:], ALU.subtract)
                    v.drain()
            nc.vector.drain().then_inc(s.s_z, 1)


def ranks(nc, K, a):
    KEYS = ("src", "dst")
    with phase(nc, "rank", ["s_rows", "s_keyb", "s_cast", "s_tp", "s_cols", "s_zero"]
               + [f"{n}_{k}" for n in ("oh", "copied", "looked", "counted", "dotted") for k in KEYS]
               ) as (block, s):
        keyb = {k: s.sb(f"keyb_{k}", [D, K.E], I32) for k in KEYS}
        raw = s.sb("raw", [K.NT, 2, P], I32)
        rowf = s.sb("rowf", [K.NT, 3, P])
        coli = s.sb("coli", [P, K.NT], I32)
        keyi = s.sb("keyi", [P, K.NT], I32)
        colp = {k: s.sb(f"colp_{k}", [P, K.NT]) for k in KEYS}
        colc = {k: s.sb(f"colc_{k}", [P, K.NT]) for k in KEYS}
        pbi = s.sb("pbi", [K.NP, P], I32)
        ohp = {(k, b): s.sb(f"ohp_{k}{b}", [P, K.NP], BF16) for k in KEYS for b in (0, 1)}
        ohc = {(k, b): s.sb(f"ohc_{k}{b}", [P, LO], BF16) for k in KEYS for b in (0, 1)}
        ohpt = {(k, b): s.sb(f"ohpt_{k}{b}", [K.NP, P]) for k in KEYS for b in (0, 1)}
        zb = s.sb("zb", [P, LO], BF16)
        junk = s.sb("junk", [P, LO])
        o0, o1 = s.sb("o0", [P, 1]), s.sb("o1", [P, 1])
        count = {k: s.ps(f"count_{k}", [K.NP, LO]) for k in KEYS}
        look = {(k, b): s.ps(f"look_{k}{b}", [P, LO]) for k in KEYS for b in (0, 1)}
        pt = s.ps("pt", [P, 3, K.NT])

        @block.sync
        def _(sp):
            tiles = lambda x: x.rearrange("(t p) -> t p", p=P)
            sp.dma_start(raw[:, 0, :], tiles(a["src"])).then_inc(s.s_rows, 16)
            sp.dma_start(raw[:, 1, :], tiles(a["dst"])).then_inc(s.s_rows, 16)
            sp.dma_start(rowf[:, 2, :], tiles(a["edge_weight"])).then_inc(s.s_rows, 16)
            for k in KEYS:
                sp.dma_start(keyb[k][:], a[k].rearrange("(o e) -> o e", o=1).to_broadcast((D, K.E))).then_inc(s.s_keyb, 16)

        @block.tensor
        def _(pe):
            pe.wait_ge(s.s_cast, 1)
            for n in range(3):
                last = nc.tensor.transpose(pt[:, n, :], rowf[:, n, :], K.ident[0:K.NT, 0:K.NT])
            last.then_inc(s.s_tp, 1)
            pe.wait_ge(s.s_zero, 1)
            for k in KEYS:
                nc.tensor.matmul(count[k][:], zb[:, 0:K.NP], zb[:], start=True, stop=True).then_inc(s.by_name[f"counted_{k}"], 1)
            for c in peeled(pe, K.NCH):
                for t in range(T):
                    n = c * T + t
                    for k in KEYS:
                        pe.wait_ge(s.by_name[f"oh_{k}"], n + 1)
                        pe.wait_ge(s.by_name[f"copied_{k}"], n + 1)
                        pe.wait_ge(s.by_name[f"dotted_{k}"], c * T + max(t - 1, 0))
                        nc.tensor.matmul(look[k, t % 2][:], ohpt[k, t % 2][:], K.cnt[k][:], start=True,
                                         stop=True).then_inc(s.by_name[f"looked_{k}"], 1)
                        nc.tensor.matmul(count[k][:], ohp[k, t % 2][:], ohc[k, t % 2][:], start=False, stop=True,
                                         skip_group_check=True).then_inc(s.by_name[f"counted_{k}"], 1)

        @block.scalar
        def _(act):
            for c in peeled(act, K.NCH):
                for t in range(T):
                    n = c * T + t
                    for k in KEYS:
                        act.wait_ge(s.by_name[f"counted_{k}"], n + 1)
                        act.wait_ge(s.by_name[f"looked_{k}"], n)
                        nc.scalar.copy(K.cnt[k][:], count[k][:]).then_inc(s.by_name[f"copied_{k}"], 1)
            for k in KEYS:
                act.wait_ge(s.by_name[f"counted_{k}"], K.NT + 1)
                act.wait_ge(s.by_name[f"looked_{k}"], K.NT)
                nc.scalar.copy(K.cnt[k][:], count[k][:])

        @block.vector
        def _(v):
            nc.vector.memset(zb[:], 0.0).then_inc(s.s_zero, 1)
            v.wait_ge(s.s_rows, 48)
            nc.vector.tensor_copy(rowf[:, 0:2, :], raw[:]).then_inc(s.s_cast, 1)
            v.wait_ge(s.s_tp, 1)
            for n, k in enumerate(KEYS):
                nc.vector.tensor_copy(K.col[k][:], pt[:, n, :])
                nc.vector.tensor_copy(keyi[:], pt[:, n, :])
                v.drain()
                nc.vector.tensor_scalar(coli[:], keyi[:], 9, None, ALU.arith_shift_right)
                v.drain()
                nc.vector.tensor_copy(colp[k][:], coli[:])
                v.drain()
                nc.vector.tensor_scalar(coli[:], keyi[:], LO - 1, None, ALU.bitwise_and)
                v.drain()
                nc.vector.tensor_copy(colc[k][:], coli[:])
                v.drain()
            nc.vector.tensor_copy(K.wcol[:], pt[:, 2, :])
            v.drain()
            v.wait_ge(s.s_keyb, 32)

            def onehots(c, t, k):
                n, b = c * T + t, t % 2
                nc.vector.tensor_scalar(pbi[:], keyb[k][0:K.NP, bass.ds(n * P, P)], 9, None, ALU.arith_shift_right)
                v.drain()
                v.wait_ge(s.by_name[f"counted_{k}"], c * T + max(t, 1))
                nc.vector.tensor_scalar(ohpt[k, b][:], pbi[:], K.part[0:K.NP, :], None, ALU.is_equal)
                nc.vector.tensor_scalar(ohp[k, b][:], K.iota[0:P, 0:K.NP], colp[k][:, bass.ds(n, 1)], None, ALU.is_equal)
                nc.vector.tensor_scalar(ohc[k, b][:], K.iota[0:P, :], colc[k][:, bass.ds(n, 1)], None, ALU.is_equal)
                nc.vector.drain().then_inc(s.by_name[f"oh_{k}"], 1)

            def dot(c, t, k):
                n, b = c * T + t, t % 2
                nc.vector.scalar_tensor_tensor(out=junk[:, 0:P], in0=keyb[k][0:P, bass.ds(n * P, P)],
                                               scalar=K.col[k][:, bass.ds(n, 1)], in1=K.before[0:P, 0:P],
                                               op0=ALU.is_equal, op1=ALU.mult, accum_out=o0[:])
                v.drain()
                v.wait_ge(s.by_name[f"looked_{k}"], n + 1)
                nc.vector.scalar_tensor_tensor(out=junk[:], in0=look[k, b][:], scalar=1.0, in1=ohc[k, b][:],
                                               op0=ALU.mult, op1=ALU.mult, accum_out=o1[:])
                v.drain()
                nc.vector.tensor_tensor(K.occ[k][:, bass.ds(n, 1)], o0[:], o1[:], ALU.add)
                nc.vector.drain().then_inc(s.by_name[f"dotted_{k}"], 1)

            for c in peeled(v, K.NCH):
                for k in KEYS:
                    onehots(c, 0, k)
                for t in range(1, T):
                    for k in KEYS:
                        onehots(c, t, k)
                    for k in KEYS:
                        dot(c, t - 1, k)
                for k in KEYS:
                    dot(c, T - 1, k)


def node_table(nc, K):
    with phase(nc, "table", ["s_tot", "s_carry", "s_tab", "s_out"]) as (block, s):
        info = s.sb("info", [K.NP, LO, 4])
        scan = s.sb("scan", [K.NP, 2, LO])
        pc = s.ps("pc", [K.NP, 2])

        @block.vector
        def _(v):
            for n, k in enumerate(("src", "dst")):
                nc.vector.tensor_copy(info[:, :, n], K.cnt[k][:])
                nc.vector.tensor_tensor_scan(scan[:, n, :], K.cnt[k][:], K.cnt[k][:], 0.0, ALU.add, ALU.bypass)
            nc.vector.drain().then_inc(s.s_tot, 1)
            v.wait_ge(s.s_carry, 1)
            for n in range(2):
                nc.vector.tensor_scalar(info[:, :, 2 + n], scan[:, n, :], pc[:, n:n + 1], None, ALU.add)
            nc.vector.drain().then_inc(s.s_tab, 1)

        @block.tensor
        def _(pe):
            pe.wait_ge(s.s_tot, 1)
            for n in range(2):
                last = nc.tensor.matmul(pc[:, n:n + 1], K.carry[0:K.NP, 0:K.NP], scan[:, n, LO - 1:LO], start=True, stop=True)
            last.then_inc(s.s_carry, 1)

        @block.sync
        def _(sp):
            sp.wait_ge(s.s_tab, 1)
            hold(sp, s)
            sp.dma_start(K.info.rearrange("(p c) w -> p c w", c=LO), info[:]).then_inc(s.s_out, 16)
            sp.wait_ge(s.s_out, 16)


def records(nc, K, a):
    with phase(nc, "rec", ["s_idx", "s_arg", "s_root"], ["ea", "info", "made", "used", "sent"]) as (block, s):
        idx = [s.sb(f"idx{u}", [P, 2, T], I32) for u in range(SLOTS)]
        inf = [s.sb(f"inf{u}", [P, 2, T, 4]) for u in range(SLOTS)]
        rec = [s.sb(f"rec{u}", [P, T, REC]) for u in range(SLOTS)]
        recj = [s.sb(f"recj{u}", [P, T, 4]) for u in range(SLOTS)]
        pos = [s.sb(f"pos{u}", [P, 2, T], I32) for u in range(SLOTS)]
        arg = s.sb("arg", [P, 4, T])
        root = s.sb("root", [P, 4, T])
        inv = s.sb("inv", [P, 4, T])
        x = [s.sb(f"x{n}", [P, T]) for n in range(4)]

        @block.sync
        def _(sp):
            for i in peeled(sp, K.NI):
                for u in range(SLOTS):
                    sp.wait_ge(s.sent[u], i * (16 * 2 * T))
                    hold(sp, s)
                    sp.dma_start(rec[u][:, :, R_EA:R_EA + 32],
                                 rows_of(a["edge_attr_32"], i * (SLOTS * CH) + u * CH)).then_inc(s.ea[u], 16)

        @block.gpsimd
        def _(g):
            g.wait_ge(s.s_idx, 1)

            def gather(i, u):
                for n in range(2):
                    for t in range(T):
                        nc.gpsimd.indirect_dma_start(inf[u][:, n, t, :], None, K.info[:, :],
                                                     bass.IndirectOffsetOnAxis(ap=idx[u][:, n, t:t + 1], axis=0)
                                                     ).then_inc(s.info[u], 16)

            def scatter(i, u):
                g.wait_ge(s.made[u], i + 1)
                hold(g, s)
                for t in range(T):
                    nc.gpsimd.indirect_dma_start(K.recd[:, :], bass.IndirectOffsetOnAxis(ap=pos[u][:, 0, t:t + 1], axis=0),
                                                 rec[u][:, t, :], None).then_inc(s.sent[u], 16)
                    nc.gpsimd.indirect_dma_start(K.recj[:, :], bass.IndirectOffsetOnAxis(ap=pos[u][:, 1, t:t + 1], axis=0),
                                                 recj[u][:, t, :], None).then_inc(s.sent[u], 16)

            for i in peeled(g, K.NI):
                for u in range(SLOTS):
                    g.wait_ge(s.s_idx, i * SLOTS + u + 1)
                    hold(g, s)
                    gather(i, u)
                    if u:
                        scatter(i, u - 1)
                scatter(i, SLOTS - 1)
            for u in range(SLOTS):
                g.wait_ge(s.sent[u], K.NI * 16 * 2 * T)

        @block.scalar
        def _(act):
            for i in peeled(act, K.NI):
                for u in range(SLOTS):
                    act.wait_ge(s.s_arg, i * SLOTS + u + 1)
                    nc.scalar.activation(root[:], arg[:], ACT.Sqrt).then_inc(s.s_root, 1)

        @block.vector
        def _(v):
            for i in peeled(v, K.NI):
                for u in range(SLOTS):
                    v.wait_ge(s.info[u], i * (16 * 2 * T))
                    v.wait_ge(s.sent[u], i * (16 * 2 * T))
                    for n, k in enumerate(("src", "dst")):
                        nc.vector.tensor_copy(idx[u][:, n, :], K.col[k][:, bass.ds(i * (SLOTS * T) + u * T, T)])
                    nc.vector.drain().then_inc(s.s_idx, 1)
                for u in range(SLOTS):
                    v.wait_ge(s.info[u], (i + 1) * (16 * 2 * T))
                    v.wait_ge(s.ea[u], (i + 1) * 16)
                    tile = lambda b: b[:, bass.ds(i * (SLOTS * T) + u * T, T)]
                    f = inf[u]
                    outs, ins, ejs, eds = (f[:, 0, :, w] for w in range(4))
                    outd, ind, ejd, edd = (f[:, 1, :, w] for w in range(4))
                    ri = rec[u][:].bitcast(I32)
                    rf = rec[u]
                    ji = recj[u][:].bitcast(I32)
                    TS, TT, STT = nc.vector.tensor_scalar, nc.vector.tensor_tensor, nc.vector.scalar_tensor_tensor
                    occs, occd = tile(K.occ["src"]), tile(K.occ["dst"])
                    TS(arg[:, 0, :], outs, 1.0, None, ALU.add)
                    TS(arg[:, 1, :], outd, 1.0, None, ALU.add)
                    TS(arg[:, 2, :], ins, 1.0, None, ALU.add)
                    TS(arg[:, 3, :], ind, 1.0, None, ALU.add)
                    nc.vector.drain().then_inc(s.s_arg, 1)
                    TS(x[0][:], ins, 1.0, None, ALU.min)
                    TS(x[1][:], outd, 1.0, None, ALU.min)
                    TS(x[2][:], eds, -(K.E + 1.0), None, ALU.add)
                    TS(x[3][:], ejd, -(K.E + 1.0), None, ALU.add)
                    v.drain()
                    TT(x[2][:], x[2][:], x[0][:], ALU.mult)
                    TT(x[3][:], x[3][:], x[1][:], ALU.mult)
                    v.drain()
                    TS(ri[:, :, R_RHO], x[2][:], float(K.E), None, ALU.add)
                    TS(ri[:, :, R_SIGD], x[3][:], float(K.E), None, ALU.add)
                    TS(ji[:, :, J_LINK], x[3][:], float(K.E), None, ALU.add)
                    TS(ri[:, :, R_SIGS], ejs, -1.0, None, ALU.add)
                    nc.vector.tensor_copy(ri[:, :, R_SRC], tile(K.col["src"]))
                    nc.vector.tensor_copy(ri[:, :, R_DST], tile(K.col["dst"]))
                    v.drain()
                    TT(x[1][:], edd, ind, ALU.subtract)
                    TT(x[3][:], ejs, outs, ALU.subtract)
                    v.drain()
                    TT(x[1][:], x[1][:], occd, ALU.add)
                    TT(x[3][:], x[3][:], occs, ALU.add)
                    v.drain()
                    nc.vector.tensor_copy(pos[u][:, 0, :], x[1][:])
                    nc.vector.tensor_copy(pos[u][:, 1, :], x[3][:])
                    nc.vector.tensor_copy(ji[:, :, J_POSD], x[1][:])
                    nc.vector.tensor_copy(recj[u][:, :, J_W], tile(K.wcol))
                    TS(recj[u][:, :, J_NSTART], occs, 1.0, None, ALU.min)
                    TS(rf[:, :, R_NSTART], occd, 1.0, None, ALU.min)
                    v.drain()
                    TT(x[1][:], ind, occd, ALU.subtract)
                    TT(x[2][:], outs, occs, ALU.subtract)
                    v.drain()
                    TS(x[1][:], x[1][:], -1.0, 1.0, ALU.add, ALU.min)
                    TS(x[2][:], x[2][:], -1.0, 1.0, ALU.add, ALU.min)
                    v.drain()
                    nc.vector.tensor_copy(rf[:, :, R_NLAST], x[1][:])
                    TT(x[2][:], x[2][:], x[0][:], ALU.max)
                    v.drain()
                    STT(ri[:, :, R_SIDX], x[2][:], float(FAR), tile(K.col["src"]), ALU.mult, ALU.add)
                    STT(ri[:, :, R_DIDX], x[1][:], float(FAR), tile(K.col["dst"]), ALU.mult, ALU.add)
                    v.wait_ge(s.s_root, i * SLOTS + u + 1)
                    nc.vector.reciprocal(inv[:], root[:])
                    v.drain()
                    TT(rf[:, :, R_CMSG], inv[:, 0, :], inv[:, 1, :], ALU.mult)
                    TT(rf[:, :, R_SELFS], inv[:, 0, :], inv[:, 0, :], ALU.mult)
                    TT(rf[:, :, R_SELFD], inv[:, 1, :], inv[:, 1, :], ALU.mult)
                    TT(rf[:, :, R_CMSG3], inv[:, 2, :], inv[:, 3, :], ALU.mult)
                    TT(rf[:, :, R_SELF3], inv[:, 3, :], inv[:, 3, :], ALU.mult)
                    nc.vector.memset(rf[:, :, R_DST + 1:R_EA], 0.0)
                    nc.vector.drain().then_inc(s.made[u], 1)


def rounds(eng, K, first, body):
    first()
    for i in peeled(eng, K.NI - 1):
        for u in range(SLOTS):
            body(i, u, (i, u + 1) if u < SLOTS - 1 else (i + 1, 0))
    i = K.NI - 1
    for u in range(SLOTS):
        body(i, u, (i, u + 1) if u < SLOTS - 1 else None)


def ahead(eng, K, body):
    for i in peeled(eng, K.NI):
        for u in range(SLOTS):
            body(i, u)


def again(i):
    return not (isinstance(i, int) and i == 0)


def again_step(n):
    return not isinstance(n, int) or n >= DSLOTS


def cnt(i, u):
    return i * SLOTS + u


def span(i, u):
    return bass.ds(i * (SLOTS * CH) + u * CH, CH)


def chunk_steps(eng, K, lag, body):
    def stages(n, u, known):
        def stage(d):
            if known and not 0 <= n - d < K.NCH:
                return None
            return n - d, (u - d) % SLOTS, n * CH - d * CH
        return stage

    peel = min(2, K.NI)
    for n in range(peel * SLOTS):
        body(n, n % SLOTS, stages(n, n % SLOTS, True))
    if K.NI > peel:
        with eng.Fori(peel, K.NI) as i:
            for u in range(SLOTS):
                body(i * SLOTS + u, u, stages(i * SLOTS + u, u, False))
    for n in range(K.NCH, K.NCH + lag):
        body(n, n % SLOTS, stages(n, n % SLOTS, True))


def turn(c, w):
    return (c - w) // SLOTS


def again_chunk(n):
    return not isinstance(n, int) or n >= SLOTS


def flags(nc, K, at, table, words, outs, width):
    with phase(nc, at, ["s_diag", "s_ps", "s_cp"], ["rec"]) as (block, s):
        rec = [s.sb(f"rec{u}", [P, T, width]) for u in range(SLOTS)]
        diag = s.sb("diag", [P, len(words), T, P], BF16)
        ps = [s.ps(f"ps{n}", [D, CH]) for n in range(len(words))]

        @block.sync
        def _(sp):
            for i in peeled(sp, K.NI):
                for u in range(SLOTS):
                    sp.wait_ge(s.s_diag, i * SLOTS)
                    hold(sp, s)
                    sp.dma_start(rec[u][:], rows_of(table, i * (SLOTS * CH) + u * CH)).then_inc(s.rec[u], 16)

        @block.vector
        def _(v):
            for i in peeled(v, K.NI):
                for u in range(SLOTS):
                    v.wait_ge(s.rec[u], (i + 1) * 16)
                    v.wait_ge(s.s_ps, cnt(i, u))
                    for n, w in enumerate(words):
                        nc.vector.tensor_tensor(diag[:, n], K.identb[0:P, 0:P].unsqueeze(1).to_broadcast((P, T, P)),
                                                rec[u][:, :, w:w + 1].to_broadcast((P, T, P)), ALU.mult)
                    nc.vector.drain().then_inc(s.s_diag, 1)

        @block.tensor
        def _(pe):
            for i in peeled(pe, K.NI):
                for u in range(SLOTS):
                    pe.wait_ge(s.s_diag, cnt(i, u) + 1)
                    pe.wait_ge(s.s_cp, cnt(i, u))
                    for n in range(len(words)):
                        last = nc.tensor.matmul(ps[n][:], K.onesb[0:P, :], diag[:, n].rearrange("p t e -> p (t e)"),
                                                start=True, stop=True)
                    last.then_inc(s.s_ps, 1)

        @block.scalar
        def _(act):
            for i in peeled(act, K.NI):
                for u in range(SLOTS):
                    act.wait_ge(s.s_ps, cnt(i, u) + 1)
                    hold(act, s)
                    for n in range(len(words)):
                        last = nc.scalar.copy(outs[n][:, span(i, u)], ps[n][:])
                    nc.scalar.drain().then_inc(s.s_cp, 1)


def spread_back(nc, K, at, x):
    with phase(nc, at, []) as (block, s):
        @block.vector
        def _(v):
            E = K.E
            nc.vector.scalar_tensor_tensor(out=x[:], in0=K.nlast[:], scalar=-1.0, in1=x[:], op0=ALU.add, op1=ALU.mult)
            v.drain()
            nc.vector.tensor_tensor_scan(x[:, E - 1::-1], K.nlast[:, E - 1::-1], x[:, E - 1::-1], 0.0,
                                         ALU.mult, ALU.subtract)


def ln_stats(nc, v, L, x, n):
    for t in range(n):
        nc.vector.bn_stats(L.st[0:x.shape[0], t, :], x[:, t, :])
    v.drain()
    for t in range(n):
        nc.vector.bn_aggr(L.mv[0:x.shape[0], t, :], L.st[0:x.shape[0], t, :])
    v.drain()
    nc.vector.tensor_scalar(L.var[0:x.shape[0], 0:n], L.mv[0:x.shape[0], 0:n, 1], EPS, None, ALU.add)


def ln_scale(nc, v, L, n, np_=P):
    nc.vector.reciprocal(L.rstd[0:np_, 0:n], L.sd[0:np_, 0:n])
    v.drain()
    nc.vector.scalar_tensor_tensor(out=L.shift[0:np_, 0:n], in0=L.mv[0:np_, 0:n, 0], scalar=-1.0,
                                   in1=L.rstd[0:np_, 0:n], op0=ALU.mult, op1=ALU.mult)


def ln_bufs(s, n, name="ln", np_=P):
    L = Box()
    L.st = s.sb(name + "st", [np_, n, 6])
    L.mv = s.sb(name + "mv", [np_, n, 2])
    L.var, L.sd = s.sb(name + "var", [np_, n]), s.sb(name + "sd", [np_, n])
    L.rstd, L.shift = s.sb(name + "rstd", [np_, n]), s.sb(name + "shift", [np_, n])
    return L


def gat(nc, K, a, l):
    names = ["s_var", "s_sd", "s_sc", "s_ln", "s_xp", "s_in", "s_e", "s_er", "s_el", "s_l", "s_xj", "s_arg",
             "s_pj", "s_ex", "s_den", "s_num", "s_dt", "s_rd", "s_rw", "s_rb", "s_o", "s_h", "s_tr", "s_row", "s_st"]
    first_layer = l == 0
    NG = 2 if first_layer else 1
    with phase(nc, f"gat{l}", names, ["rec", "gat", "keep"]) as (block, s):
        rec = [s.sb(f"rec{u}", [P, T, REC]) for u in range(SLOTS)]
        g = [s.sb(f"g{u}", [P, NG * T, D]) for u in range(SLOTS)]
        if first_layer:
            L = ln_bufs(s, 2 * T)
            h = s.sb("h", [P, 2 * T, D])
            hdt = s.sb("hdt", [D, T, P])
        hst = [s.sb(f"hst{u}", [D, T, P]) for u in range(SLOTS)]
        eat = s.sb("eat", [32, T, P])
        er, el = s.sb("er", [D, CH]), s.sb("el", [D, CH])
        m = s.sb("m", [D, CH + 1])
        ta, tp = s.sb("ta", [D, CH]), s.sb("tp", [D, CH])
        xa, xp = s.sb("xa", [D, CH]), s.sb("xp", [D, CH])
        den, num = s.sb("den", [D, CH + 1]), s.sb("num", [D, CH + 1])
        rden = s.sb("rden", [P, T, 2])
        rwide = s.sb("rwide", [P, T, 2, 64])
        wx = s.sb("wx", [D, CH])
        o = s.sb("o", [D, CH])
        ht = s.sb("ht", [D, T, P])
        orow = s.sb("orow", [P, T, D])
        ps_s = s.ps("s", [D, T, P])
        ps_d = s.ps("d", [D, T, P]) if first_layer else None
        ps_ea = s.ps("ea", [32, T, P])
        ps_xj, ps_e, ps_l = s.ps("xj", [D, CH]), s.ps("e", [D, CH]), s.ps("l", [D, CH])
        ps_o = s.ps("o", [P, T, D])
        ps_r = s.ps("r", [D, 512])
        ps_den = ps_r[0:P, CH:CH + 2 * T].rearrange("p (t k) -> p t k", k=2)
        flat = lambda b: b[:].rearrange("p t e -> p (t e)")

        @block.sync
        def _(sp):
            def body(n, u, stage):
                if c := stage(0):
                    c, w, at = c
                    if again_chunk(n):
                        sp.wait_ge(s.s_xp, c - SLOTS + 1)
                        hold(sp, s)
                    sp.dma_start(rec[w][:], rows_of(K.recd, at)).then_inc(s.rec[w], 16)
                if first_layer and (c := stage(2)):
                    c, w, at = c
                    sp.wait_ge(s.gat[w], turn(c, w) * (16 * NG * T) + 16 * NG * T)
                    hold(sp, s)
                    sp.dma_start(rows_of(K.xs, at), g[w][:, 0:T, :]).then_inc(s.keep[w], 16)
                    sp.dma_start(rows_of(K.xd, at), g[w][:, T:2 * T, :]).then_inc(s.keep[w], 16)
                if c := stage(6):
                    c, w, at = c
                    sp.wait_ge(s.s_row, c + 1)
                    hold(sp, s)
                    sp.dma_start(rows_of(K.tab[l], at), orow[:]).then_inc(s.s_st, 16)

            chunk_steps(sp, K, 6, body)
            sp.wait_ge(s.s_st, 16 * K.NCH)
            if first_layer:
                for u in range(SLOTS):
                    sp.wait_ge(s.keep[u], 32 * K.NI)

        @block.gpsimd
        def _(gp):
            src = K.x if first_layer else K.tab[l - 1]
            words = (R_SRC, R_DST) if first_layer else (R_RHO,)

            def body(n, u, stage):
                if c := stage(0):
                    c, w, at = c
                    gp.wait_ge(s.rec[w], turn(c, w) * 16 + 16)
                    if again_chunk(n):
                        gp.wait_ge(s.s_xp, c - SLOTS + 1)
                        if first_layer:
                            gp.wait_ge(s.s_ln, c - SLOTS + 1)
                            gp.wait_ge(s.keep[w], turn(c, w) * 32)
                    hold(gp, s)
                    for k, word in enumerate(words):
                        for t in range(T):
                            nc.gpsimd.indirect_dma_start(
                                g[w][:, k * T + t, :], None, src[:, :],
                                bass.IndirectOffsetOnAxis(ap=rec[w][:].bitcast(I32)[:, t, word:word + 1], axis=0)
                            ).then_inc(s.gat[w], 16)

            chunk_steps(gp, K, 0, body)

        @block.tensor
        def _(pe):
            def body(n, u, stage):
                c1, c2, c3, c4 = (stage(d) for d in range(1, 5))
                if c2:
                    c, w, at = c2
                    pe.wait_ge(s.s_el, c + 1)
                    pe.wait_ge(s.s_arg, c)
                    nc.tensor.matmul(ps_l[:], K.att[:, l, :], el[:], start=True, stop=True).then_inc(s.s_l, 1)
                if c1:
                    c, w, at = c1
                    rows = h if first_layer else g[w]
                    if first_layer:
                        pe.wait_ge(s.s_ln, c + 1)
                    else:
                        pe.wait_ge(s.gat[w], turn(c, w) * (16 * NG * T) + 16 * NG * T)
                    pe.wait_ge(s.rec[w], turn(c, w) * 16 + 16)
                    pe.wait_ge(s.s_in, c)
                    for t in range(T):
                        nc.tensor.transpose(ps_s[:, t, :], rows[:, t, :], K.ident[0:P, 0:P])
                        if first_layer:
                            nc.tensor.transpose(ps_d[:, t, :], rows[:, T + t, :], K.ident[0:P, 0:P])
                        last = nc.tensor.transpose(ps_ea[:, t, :], rec[w][:, t, R_EA:R_EA + 32], K.ident[0:P, 0:P])
                    last.then_inc(s.s_xp, 1)
                if c4:
                    c, w, at = c4
                    pe.wait_ge(s.s_h, c + 1)
                    pe.wait_ge(s.s_row, c)
                    for t in range(T):
                        last = nc.tensor.transpose(ps_o[:, t, :], ht[:, t, :], K.ident[:])
                    last.then_inc(s.s_tr, 1)
                if c2:
                    c, w, at = c2
                    pe.wait_ge(s.s_pj, c)
                    nc.tensor.matmul(ps_xj[:], K.wl[:, l, :], flat(hst[w]), start=True, stop=True).then_inc(s.s_xj, 1)
                if c1:
                    c, w, at = c1
                    pe.wait_ge(s.s_in, c + 1)
                    pe.wait_ge(s.s_el, c)
                    nc.tensor.matmul(ps_e[:], K.wl[:, l, :], flat(hst[w]), start=True, stop=False)
                    hd = flat(hdt) if first_layer else K.hd[:, bass.ds(at, CH)]
                    nc.tensor.matmul(ps_e[:], K.wr[:, l, :], hd, start=False, stop=False)
                    nc.tensor.matmul(ps_e[:], K.we[:, l, :], flat(eat), start=False, stop=True).then_inc(s.s_e, 1)
                if c3:
                    c, w, at = c3
                    pe.wait_ge(s.s_den, c + 1)
                    for t in range(T):
                        last = nc.tensor.matmul(ps_den[:, t, :], den[:, 1 + t * P:1 + (t + 1) * P], K.ident[:, 0::64],
                                                start=True, stop=True)
                    last.then_inc(s.s_dt, 1)
                    pe.wait_ge(s.s_rw, c + 1)
                    for t in range(T):
                        last = nc.tensor.matmul(ps_r[:, t * P:(t + 1) * P],
                                                rwide[:, t, :, :].rearrange("p k d -> p (k d)"), K.ident[0:P, 0:P],
                                                start=True, stop=True)
                    last.then_inc(s.s_rb, 1)

            chunk_steps(pe, K, 4, body)

        @block.scalar
        def _(act):
            def body(n, u, stage):
                c0, c1, c2, c3, c4 = (stage(d) for d in range(5))
                if c1:
                    c, w, at = c1
                    act.wait_ge(s.s_xp, c + 1)
                    act.wait_ge(s.s_e, c)
                    if again_chunk(n):
                        act.wait_ge(s.s_xj, c - SLOTS + 1)
                    nc.scalar.copy(hst[w][:], ps_s[:])
                    if first_layer:
                        nc.scalar.copy(hdt[:], ps_d[:])
                    nc.scalar.copy(eat[:], ps_ea[:])
                    nc.scalar.drain().then_inc(s.s_in, 1)
                if c4:
                    c, w, at = c4
                    act.wait_ge(s.s_o, c + 1)
                    act.wait_ge(s.s_tr, c)
                    fn = ACT.Relu if l < 2 else ACT.Identity
                    nc.scalar.activation(flat(ht), o[:], fn, bias=K.bcol[:, l:l + 1])
                    nc.scalar.activation(K.hd[:, bass.ds(at, CH)], o[:], fn, bias=K.bcol[:, l:l + 1])
                    nc.scalar.drain().then_inc(s.s_h, 1)
                if c2:
                    c, w, at = c2
                    act.wait_ge(s.s_arg, c + 1)
                    act.wait_ge(s.s_num, c)
                    nc.scalar.activation(xa[:], ta[:], ACT.Exp)
                    nc.scalar.activation(xp[:], tp[:], ACT.Exp)
                    nc.scalar.drain().then_inc(s.s_ex, 1)
                if c1:
                    c, w, at = c1
                    act.wait_ge(s.s_e, c + 1)
                    act.wait_ge(s.s_el, c)
                    nc.scalar.activation(er[:], ps_e[:], ACT.Relu, scale=0.8).then_inc(s.s_er, 1)
                if c3:
                    c, w, at = c3
                    act.wait_ge(s.s_rd, c + 1)
                    act.wait_ge(s.s_rb, c)
                    nc.scalar.copy(rwide[:], rden[:].unsqueeze(3).to_broadcast((P, T, 2, 64))).then_inc(s.s_rw, 1)
                if c4:
                    c, w, at = c4
                    act.wait_ge(s.s_tr, c + 1)
                    act.wait_ge(s.s_st, c * 16)
                    nc.scalar.copy(orow[:], ps_o[:]).then_inc(s.s_row, 1)
                if c0 and first_layer:
                    c, w, at = c0
                    act.wait_ge(s.s_var, c + 1)
                    nc.scalar.activation(L.sd[:], L.var[:], ACT.Sqrt).then_inc(s.s_sd, 1)
                    act.wait_ge(s.s_sc, c + 1)
                    act.wait_ge(s.s_xp, c)
                    for t in range(2 * T):
                        nc.scalar.activation(h[:, t, :], g[w][:, t, :], ACT.Relu, bias=L.shift[:, t:t + 1],
                                             scale=L.rstd[:, t:t + 1])
                    nc.scalar.drain().then_inc(s.s_ln, 1)

            chunk_steps(act, K, 4, body)

        @block.vector
        def _(v):
            for b in (m, den, num):
                nc.vector.memset(b[:, CH:CH + 1], 0.0)
            v.drain()

            def body(n, u, stage):
                c0, c1, c2, c3, c4 = (stage(d) for d in range(5))
                if c4:
                    c, w, at = c4
                    v.wait_ge(s.s_rb, c + 1)
                    v.wait_ge(s.s_h, c)
                    nc.vector.tensor_tensor(o[:], num[:, 1:CH + 1], ps_r[:, 0:CH], ALU.mult)
                    nc.vector.drain().then_inc(s.s_o, 1)
                if c2:
                    c, w, at = c2
                    low = K.nstart[:, bass.ds(at, CH)]
                    nc.vector.tensor_copy(m[:, 0:1], m[:, CH:CH + 1])
                    v.drain()
                    v.wait_ge(s.s_l, c + 1)
                    nc.vector.tensor_tensor_scan(m[:, 1:CH + 1], low, ps_l[:], m[:, 0:1], ALU.min, ALU.max)
                    v.drain()
                    v.wait_ge(s.s_ex, c)
                    nc.vector.tensor_tensor(ta[:], m[:, 0:CH], m[:, 1:CH + 1], ALU.subtract)
                    nc.vector.tensor_tensor(tp[:], ps_l[:], m[:, 1:CH + 1], ALU.subtract)
                    v.drain()
                    nc.vector.tensor_tensor(ta[:], ta[:], low, ALU.min)
                    nc.vector.drain().then_inc(s.s_arg, 1)
                if c3:
                    c, w, at = c3
                    v.wait_ge(s.s_ex, c + 1)
                    v.wait_ge(s.s_xj, c + 1)
                    nc.vector.tensor_tensor(wx[:], xp[:], ps_xj[:], ALU.mult).then_inc(s.s_pj, 1)
                    for b in (den, num):
                        nc.vector.tensor_copy(b[:, 0:1], b[:, CH:CH + 1])
                    v.drain()
                    nc.vector.tensor_tensor_scan(den[:, 1:CH + 1], xa[:], xp[:], den[:, 0:1], ALU.mult,
                                                 ALU.add).then_inc(s.s_den, 1)
                    nc.vector.tensor_tensor_scan(num[:, 1:CH + 1], xa[:], wx[:], num[:, 0:1], ALU.mult, ALU.add)
                    nc.vector.drain().then_inc(s.s_num, 1)
                if c0 and first_layer:
                    c, w, at = c0
                    v.wait_ge(s.gat[w], turn(c, w) * (16 * NG * T) + 16 * NG * T)
                    v.wait_ge(s.s_ln, c)
                    ln_stats(nc, v, L, g[w], 2 * T)
                    nc.vector.drain().then_inc(s.s_var, 1)
                if c3:
                    c, w, at = c3
                    v.wait_ge(s.s_dt, c + 1)
                    v.wait_ge(s.s_rw, c)
                    nc.vector.tensor_scalar(rden[:], ps_den, 1e-16, None, ALU.add)
                    v.drain()
                    nc.vector.reciprocal(rden[:], rden[:])
                    nc.vector.drain().then_inc(s.s_rd, 1)
                if c1:
                    c, w, at = c1
                    v.wait_ge(s.s_er, c + 1)
                    v.wait_ge(s.s_l, c)
                    nc.vector.scalar_tensor_tensor(out=el[:], in0=ps_e[:], scalar=0.2, in1=er[:], op0=ALU.mult,
                                                   op1=ALU.add).then_inc(s.s_el, 1)
                if c0 and first_layer:
                    c, w, at = c0
                    v.wait_ge(s.s_sd, c + 1)
                    ln_scale(nc, v, L, 2 * T)
                    nc.vector.drain().then_inc(s.s_sc, 1)

            chunk_steps(v, K, 4, body)


def start_form(nc, K, at, bounds):
    with phase(nc, at, []) as (block, s):
        @block.vector
        def _(v):
            if bounds:
                nc.vector.tensor_scalar(K.nstart[:], K.nstart[:], 2 * BIG, -BIG, ALU.mult, ALU.add)
            else:
                nc.vector.tensor_scalar(K.nstart[:], K.nstart[:], 0.0, None, ALU.is_gt)


def gcn_messages(nc, K):
    names = ["s_hc", "s_dt", "s_x1", "s_sd", "s_sc", "s_h", "s_tm", "s_sum", "s_tr", "s_row",
             "s_st", "s_sv"]
    with phase(nc, "msg", names, ["rec", "ld", "gat", "stx"]) as (block, s):
        rec = [s.sb(f"rec{u}", [P, T, REC]) for u in range(SLOTS)]
        g = [s.sb(f"g{u}", [P, T, D]) for u in range(SLOTS)]
        x = [s.sb(f"x{u}", [P, 2 * T, D]) for u in range(SLOTS)]
        L = ln_bufs(s, 2 * T)
        sc, sh = s.sb("sc", [P, 3 * T]), s.sb("sh", [P, 3 * T])
        hc = s.sb("hc", [D, T, P])
        h = s.sb("h", [P, 3 * T, D])
        us = s.sb("us", [D, CH + 1])
        urow = s.sb("urow", [P, T, D])
        ps_d, ps_m, ps_u = s.ps("d", [P, T, D]), s.ps("m", [D, T, P]), s.ps("u", [P, T, D])

        @block.sync
        def _(sp):
            def loads(i, u):
                at = i * (SLOTS * CH) + u * CH
                if again(i):
                    prev = cnt(i - 1, u) + 1
                    sp.wait_ge(s.s_sc, prev)
                    hold(sp, s)
                    sp.wait_ge(s.s_h, prev)
                    hold(sp, s)
                    sp.wait_ge(s.stx[u], 32 * i)
                    hold(sp, s)
                    sp.wait_ge(s.gat[u], i * (16 * T))
                    hold(sp, s)
                sp.dma_start(rec[u][:], rows_of(K.recd, at)).then_inc(s.rec[u], 16)
                sp.dma_start(x[u][:, 0:T, :], rows_of(K.xs, at)).then_inc(s.ld[u], 16)
                sp.dma_start(x[u][:, T:2 * T, :], rows_of(K.xd, at)).then_inc(s.ld[u], 16)

            ahead(sp, K, loads)

        @block.gpsimd
        def _(gp):
            def gathers(i, u):
                gp.wait_ge(s.rec[u], (i + 1) * 16)
                if again(i):
                    gp.wait_ge(s.s_x1, cnt(i - 1, u) + 1)
                hold(gp, s)
                for t in range(T):
                    nc.gpsimd.indirect_dma_start(
                        g[u][:, t, :], None, K.tab[2][:, :],
                        bass.IndirectOffsetOnAxis(ap=rec[u][:].bitcast(I32)[:, t, R_RHO:R_RHO + 1], axis=0)
                    ).then_inc(s.gat[u], 16)

            ahead(gp, K, gathers)

        @block.tensor
        def _(pe):
            for i in peeled(pe, K.NI):
                for u in range(SLOTS):
                    c = cnt(i, u)
                    pe.wait_ge(s.s_hc, c + 1)
                    pe.wait_ge(s.s_x1, c)
                    for t in range(T):
                        last = nc.tensor.transpose(ps_d[:, t, :], hc[:, t, :], K.ident[:])
                    last.then_inc(s.s_dt, 1)
                    pe.wait_ge(s.s_h, c + 1)
                    pe.wait_ge(s.s_sum, c)
                    for t in range(T):
                        last = nc.tensor.transpose(ps_m[:, t, :], h[:, t, :], K.ident[0:P, 0:P])
                    last.then_inc(s.s_tm, 1)
                    pe.wait_ge(s.s_sum, c + 1)
                    pe.wait_ge(s.s_row, c)
                    for t in range(T):
                        last = nc.tensor.transpose(ps_u[:, t, :], us[:, 1 + t * P:1 + (t + 1) * P], K.ident[:])
                    last.then_inc(s.s_tr, 1)

        @block.scalar
        def _(act):
            for i in peeled(act, K.NI):
                for u in range(SLOTS):
                    c, at = cnt(i, u), i * (SLOTS * CH) + u * CH
                    act.wait_ge(s.s_dt, c)
                    hold(act, s)
                    nc.scalar.copy(hc[:].rearrange("p t e -> p (t e)"), K.hd[:, span(i, u)]).then_inc(s.s_hc, 1)
                    act.wait_ge(s.s_x1, c + 1)
                    act.dma_start(rows_of(K.xs, at), x[u][:, 0:T, :]).then_inc(s.stx[u], 16)
                    act.dma_start(rows_of(K.xd, at), x[u][:, T:2 * T, :]).then_inc(s.stx[u], 16)
                    nc.scalar.activation(L.sd[:], L.var[:], ACT.Sqrt).then_inc(s.s_sd, 1)
                    act.wait_ge(s.s_sc, c + 1)
                    act.wait_ge(s.s_tm, c)
                    act.wait_ge(s.s_sv, 32 * c)
                    for n in range(3):
                        for t in range(T):
                            nc.scalar.activation(h[:, n * T + t, :], x[u][:, (0, 0, T)[n] + t, :], ACT.Relu,
                                                 bias=sh[:, n * T + t:n * T + t + 1],
                                                 scale=sc[:, n * T + t:n * T + t + 1])
                    nc.scalar.drain().then_inc(s.s_h, 1)
                    act.wait_ge(s.s_h, c + 1)
                    act.dma_start(rows_of(K.vs, at), h[:, T:2 * T, :]).then_inc(s.s_sv, 16)
                    act.dma_start(rows_of(K.vd, at), h[:, 2 * T:3 * T, :]).then_inc(s.s_sv, 16)
                    act.wait_ge(s.s_tr, c + 1)
                    hold(act, s)
                    nc.scalar.copy(K.u[:, span(i, u)], us[:, 1:CH + 1])
                    act.wait_ge(s.s_st, 16 * c)
                    nc.scalar.copy(urow[:], ps_u[:])
                    nc.scalar.drain().then_inc(s.s_row, 1)
                    act.wait_ge(s.s_row, c + 1)
                    act.dma_start(rows_of(K.tabu, at), urow[:]).then_inc(s.s_st, 16)
            act.wait_ge(s.s_st, 16 * K.NCH)
            act.wait_ge(s.s_sv, 32 * K.NCH)
            for u in range(SLOTS):
                act.wait_ge(s.stx[u], 32 * K.NI)

        @block.vector
        def _(v):
            nc.vector.memset(us[:, CH:CH + 1], 0.0)
            v.drain()
            for i in peeled(v, K.NI):
                for u in range(SLOTS):
                    c = cnt(i, u)
                    v.wait_ge(s.gat[u], (i + 1) * (16 * T))
                    v.wait_ge(s.ld[u], (i + 1) * 32)
                    v.wait_ge(s.rec[u], (i + 1) * 16)
                    nc.vector.tensor_tensor(x[u][:, 0:T, :], x[u][:, 0:T, :], g[u][:], ALU.add)
                    v.wait_ge(s.s_dt, c + 1)
                    nc.vector.tensor_tensor(x[u][:, T:2 * T, :], x[u][:, T:2 * T, :], ps_d[:], ALU.add)
                    v.drain()
                    v.wait_ge(s.s_h, c)
                    ln_stats(nc, v, L, x[u], 2 * T)
                    nc.vector.drain().then_inc(s.s_x1, 1)
                    v.wait_ge(s.s_sd, c + 1)
                    ln_scale(nc, v, L, 2 * T)
                    v.drain()
                    for n, (w, t0) in enumerate(((R_CMSG, 0), (R_SELFS, 0), (R_SELFD, T))):
                        nc.vector.tensor_tensor(sc[:, n * T:(n + 1) * T], L.rstd[:, t0:t0 + T], rec[u][:, :, w], ALU.mult)
                        nc.vector.tensor_tensor(sh[:, n * T:(n + 1) * T], L.shift[:, t0:t0 + T], rec[u][:, :, w], ALU.mult)
                    nc.vector.drain().then_inc(s.s_sc, 1)
                    v.wait_ge(s.s_tr, c)
                    v.wait_ge(s.s_row, c)
                    nc.vector.tensor_copy(us[:, 0:1], us[:, CH:CH + 1])
                    v.drain()
                    v.wait_ge(s.s_tm, c + 1)
                    nc.vector.tensor_tensor_scan(us[:, 1:CH + 1], K.nstart[:, span(i, u)],
                                                 ps_m[:].rearrange("p t e -> p (t e)"), us[:, 0:1],
                                                 ALU.mult, ALU.add).then_inc(s.s_sum, 1)


def gcn_update(nc, K):
    names = ["s_y", "s_xp", "s_ys", "s_yt", "s_mm", "s_x2", "s_sd", "s_sc", "s_h", "s_sth"]
    with phase(nc, "upd", names, ["rec", "ld", "gat", "stx"]) as (block, s):
        rec = [s.sb(f"rec{u}", [P, T, REC]) for u in range(SLOTS)]
        g = [s.sb(f"g{u}", [P, T, D]) for u in range(SLOTS)]
        x = [s.sb(f"x{u}", [P, 2 * T, D]) for u in range(SLOTS)]
        vv = [s.sb(f"vv{u}", [P, 2 * T, D]) for u in range(SLOTS)]
        L = ln_bufs(s, T)
        yst, ydt = s.sb("yst", [D, T, P]), s.sb("ydt", [D, T, P])
        h = s.sb("h", [P, T, D])
        ps_s, ps_d = s.ps("s", [D, T, P]), s.ps("d", [D, T, P])
        ps_y = s.ps("y", [P, 2 * T, D])

        @block.sync
        def _(sp):
            def loads(i, u):
                at = i * (SLOTS * CH) + u * CH
                if again(i):
                    prev = cnt(i - 1, u) + 1
                    sp.wait_ge(s.s_h, prev)
                    hold(sp, s)
                    sp.wait_ge(s.s_xp, prev)
                    hold(sp, s)
                    sp.wait_ge(s.stx[u], 32 * i)
                    hold(sp, s)
                sp.dma_start(rec[u][:], rows_of(K.recd, at)).then_inc(s.rec[u], 16)
                sp.dma_start(x[u][:, 0:T, :], rows_of(K.xs, at)).then_inc(s.ld[u], 16)
                sp.dma_start(x[u][:, T:2 * T, :], rows_of(K.xd, at)).then_inc(s.ld[u], 16)
                sp.dma_start(vv[u][:, 0:T, :], rows_of(K.vs, at)).then_inc(s.ld[u], 16)
                sp.dma_start(vv[u][:, T:2 * T, :], rows_of(K.vd, at)).then_inc(s.ld[u], 16)

            ahead(sp, K, loads)

        @block.gpsimd
        def _(gp):
            def gathers(i, u):
                gp.wait_ge(s.rec[u], (i + 1) * 16)
                if again(i):
                    gp.wait_ge(s.s_y, cnt(i - 1, u) + 1)
                hold(gp, s)
                for t in range(T):
                    nc.gpsimd.indirect_dma_start(
                        g[u][:, t, :], None, K.tabu[:, :],
                        bass.IndirectOffsetOnAxis(ap=rec[u][:].bitcast(I32)[:, t, R_RHO:R_RHO + 1], axis=0)
                    ).then_inc(s.gat[u], 16)

            ahead(gp, K, gathers)

        @block.tensor
        def _(pe):
            for i in peeled(pe, K.NI):
                for u in range(SLOTS):
                    c = cnt(i, u)
                    pe.wait_ge(s.s_y, c + 1)
                    pe.wait_ge(s.s_yt, c)
                    for t in range(T):
                        nc.tensor.transpose(ps_s[:, t, :], vv[u][:, t, :], K.ident[0:P, 0:P])
                        last = nc.tensor.transpose(ps_d[:, t, :], vv[u][:, T + t, :], K.ident[0:P, 0:P])
                    last.then_inc(s.s_xp, 1)
                    pe.wait_ge(s.s_ys, c + 1)
                    pe.wait_ge(s.s_yt, c + 1)
                    pe.wait_ge(s.s_x2, c)
                    for t in range(T):
                        nc.tensor.matmul(ps_y[:, t, :], yst[:, t, :], K.w1[:], start=True, stop=True)
                        last = nc.tensor.matmul(ps_y[:, T + t, :], ydt[:, t, :], K.w1[:], start=True, stop=True)
                    last.then_inc(s.s_mm, 1)

        @block.scalar
        def _(act):
            for i in peeled(act, K.NI):
                for u in range(SLOTS):
                    c, at = cnt(i, u), i * (SLOTS * CH) + u * CH
                    act.wait_ge(s.s_xp, c + 1)
                    act.wait_ge(s.s_mm, c)
                    nc.scalar.copy(yst[:], ps_s[:]).then_inc(s.s_ys, 1)
                    act.wait_ge(s.s_x2, c + 1)
                    act.dma_start(rows_of(K.xs, at), x[u][:, 0:T, :]).then_inc(s.stx[u], 16)
                    act.dma_start(rows_of(K.xd, at), x[u][:, T:2 * T, :]).then_inc(s.stx[u], 16)
                    nc.scalar.activation(L.sd[:], L.var[:], ACT.Sqrt).then_inc(s.s_sd, 1)
                    act.wait_ge(s.s_sc, c + 1)
                    act.wait_ge(s.s_sth, 16 * c)
                    for t in range(T):
                        nc.scalar.activation(h[:, t, :], x[u][:, T + t, :], ACT.Relu, bias=L.shift[:, t:t + 1],
                                             scale=L.rstd[:, t:t + 1])
                    nc.scalar.drain().then_inc(s.s_h, 1)
                    act.wait_ge(s.s_h, c + 1)
                    act.dma_start(rows_of(K.h2, at), h[:]).then_inc(s.s_sth, 16)
            act.wait_ge(s.s_sth, 16 * K.NCH)
            for u in range(SLOTS):
                act.wait_ge(s.stx[u], 32 * K.NI)

        @block.vector
        def _(v):
            for i in peeled(v, K.NI):
                for u in range(SLOTS):
                    c = cnt(i, u)
                    v.wait_ge(s.gat[u], (i + 1) * (16 * T))
                    v.wait_ge(s.ld[u], (i + 1) * 64)
                    nc.vector.tensor_tensor(vv[u][:, 0:T, :], vv[u][:, 0:T, :], g[u][:], ALU.add)
                    bias = K.b1row[0:P, :].unsqueeze(1).to_broadcast((P, 2 * T, D))
                    nc.vector.tensor_tensor(x[u][:], x[u][:], bias, ALU.add)
                    nc.vector.drain().then_inc(s.s_y, 1)
                    v.wait_ge(s.s_xp, c + 1)
                    v.wait_ge(s.s_mm, c)
                    nc.vector.tensor_tensor(ydt[:].rearrange("p t e -> p (t e)"), ps_d[:].rearrange("p t e -> p (t e)"),
                                            K.u[:, span(i, u)], ALU.add)
                    v.wait_ge(s.s_ys, c + 1)
                    hold(v, s)
                    nc.vector.drain().then_inc(s.s_yt, 1)
                    v.wait_ge(s.s_mm, c + 1)
                    nc.vector.tensor_tensor(x[u][:], x[u][:], ps_y[:], ALU.add)
                    v.drain()
                    v.wait_ge(s.s_h, c)
                    ln_stats(nc, v, L, x[u][:, T:2 * T, :], T)
                    nc.vector.drain().then_inc(s.s_x2, 1)
                    v.wait_ge(s.s_sd, c + 1)
                    ln_scale(nc, v, L, T)
                    nc.vector.drain().then_inc(s.s_sc, 1)


def hop(nc, K, n):
    source = K.h2 if n == 0 else K.tabe[n - 1]
    word = J_POSD if n == 0 else J_LINK
    out = K.tabe[n] if n < 2 else K.taba
    names = ["s_m", "s_tm", "s_sum", "s_tr", "s_row", "s_st"]
    with phase(nc, f"hop{n}", names, ["rec", "gat"]) as (block, s):
        rec = [s.sb(f"rec{u}", [P, T, 4]) for u in range(SLOTS)]
        g = [s.sb(f"g{u}", [P, T, D]) for u in range(SLOTS)]
        m = s.sb("m", [P, T, D])
        es = s.sb("es", [D, CH + 1])
        ac = s.sb("ac", [D, CH])
        orow = s.sb("orow", [P, T, D])
        ps_m, ps_o = s.ps("m", [D, T, P]), s.ps("o", [P, T, D])

        @block.sync
        def _(sp):
            def loads(i, u):
                if again(i):
                    sp.wait_ge(s.s_m, cnt(i - 1, u) + 1)
                    hold(sp, s)
                sp.dma_start(rec[u][:], rows_of(K.recj, i * (SLOTS * CH) + u * CH)).then_inc(s.rec[u], 16)

            ahead(sp, K, loads)

        @block.gpsimd
        def _(gp):
            def gathers(i, u):
                gp.wait_ge(s.rec[u], (i + 1) * 16)
                hold(gp, s)
                for t in range(T):
                    nc.gpsimd.indirect_dma_start(
                        g[u][:, t, :], None, source[:, :],
                        bass.IndirectOffsetOnAxis(ap=rec[u][:].bitcast(I32)[:, t, word:word + 1], axis=0)
                    ).then_inc(s.gat[u], 16)

            ahead(gp, K, gathers)

        @block.scalar
        def _(act):
            for i in peeled(act, K.NI):
                for u in range(SLOTS):
                    c = cnt(i, u)
                    act.wait_ge(s.s_tr, c + 1)
                    act.wait_ge(s.s_st, 16 * c)
                    nc.scalar.copy(orow[:], ps_o[:]).then_inc(s.s_row, 1)
                    act.wait_ge(s.s_row, c + 1)
                    act.dma_start(rows_of(out, i * (SLOTS * CH) + u * CH), orow[:]).then_inc(s.s_st, 16)
            act.wait_ge(s.s_st, 16 * K.NCH)

        @block.tensor
        def _(pe):
            for i in peeled(pe, K.NI):
                for u in range(SLOTS):
                    c = cnt(i, u)
                    pe.wait_ge(s.s_m, c + 1)
                    for t in range(T):
                        last = nc.tensor.transpose(ps_m[:, t, :], m[:, t, :], K.ident[0:P, 0:P])
                    last.then_inc(s.s_tm, 1)
                    pe.wait_ge(s.s_sum, c + 1)
                    pe.wait_ge(s.s_row, c)
                    cols = es[:, 1:CH + 1] if n < 2 else ac[:]
                    for t in range(T):
                        last = nc.tensor.transpose(ps_o[:, t, :], cols[:, t * P:(t + 1) * P], K.ident[:])
                    last.then_inc(s.s_tr, 1)

        @block.vector
        def _(v):
            nc.vector.memset(es[:, CH:CH + 1], 0.0)
            v.drain()
            for i in peeled(v, K.NI):
                for u in range(SLOTS):
                    c = cnt(i, u)
                    v.wait_ge(s.gat[u], (i + 1) * (16 * T))
                    v.wait_ge(s.rec[u], (i + 1) * 16)
                    v.wait_ge(s.s_tm, c)
                    nc.vector.tensor_tensor(m[:], g[u][:], rec[u][:, :, J_W:J_W + 1].to_broadcast((P, T, D)), ALU.mult)
                    nc.vector.drain().then_inc(s.s_m, 1)
                    v.wait_ge(s.s_tr, c)
                    nc.vector.tensor_copy(es[:, 0:1], es[:, CH:CH + 1])
                    v.drain()
                    v.wait_ge(s.s_tm, c + 1)
                    nc.vector.tensor_tensor_scan(es[:, 1:CH + 1], K.nstart[:, span(i, u)],
                                                 ps_m[:].rearrange("p t e -> p (t e)"), es[:, 0:1], ALU.mult, ALU.add)
                    v.drain()
                    if n == 0:
                        nc.vector.tensor_copy(K.u[:, span(i, u)], es[:, 1:CH + 1])
                    elif n == 1:
                        nc.vector.tensor_tensor(K.u[:, span(i, u)], K.u[:, span(i, u)], es[:, 1:CH + 1], ALU.add)
                    else:
                        nc.vector.tensor_tensor(ac[:], K.u[:, span(i, u)], es[:, 1:CH + 1], ALU.add)
                    nc.vector.drain().then_inc(s.s_sum, 1)


def gate_messages(nc, K):
    names = ["s_var", "s_sd", "s_sc", "s_h2", "s_h3", "s_msg", "s_tm", "s_th", "s_ht", "s_lg", "s_sum", "s_ms", "s_tr",
             "s_made", "s_x3"]
    with phase(nc, "gate", names, ["rec", "ld", "gat", "sent"]) as (block, s):
        rec = [s.sb(f"rec{u}", [P, T, REC]) for u in range(SLOTS)]
        g = [s.sb(f"g{u}", [P, 2 * T, D]) for u in range(SLOTS)]
        x = [s.sb(f"x{u}", [P, 2 * T, D]) for u in range(SLOTS)]
        row = [s.sb(f"row{u}", [P, 2 * T, ROW]) for u in range(SLOTS)]
        L = ln_bufs(s, 2 * T)
        h = s.sb("h", [P, 2 * T, D])
        msg = s.sb("msg", [P, T, D])
        ht = s.sb("ht", [D, 2 * T, D])
        ms = s.sb("ms", [D, CH + 1])
        ps_m, ps_u = s.ps("m", [D, T, P]), s.ps("u", [P, T, D])
        ps_h = s.ps("h", [D, 2 * T, D])
        ps_g = s.ps("g", [P, 2 * T, HEADS])

        @block.sync
        def _(sp):
            def loads(i, u):
                at = i * (SLOTS * CH) + u * CH
                if again(i):
                    sp.wait_ge(s.sent[u], i * (16 * 2 * T))
                    hold(sp, s)
                sp.dma_start(rec[u][:], rows_of(K.recd, at)).then_inc(s.rec[u], 16)
                sp.dma_start(x[u][:, 0:T, :], rows_of(K.xs, at)).then_inc(s.ld[u], 16)
                sp.dma_start(x[u][:, T:2 * T, :], rows_of(K.xd, at)).then_inc(s.ld[u], 16)

            ahead(sp, K, loads)

        @block.gpsimd
        def _(gp):
            def gathers(i, u):
                gp.wait_ge(s.rec[u], (i + 1) * 16)
                hold(gp, s)
                for n, w in enumerate((R_SIGS, R_SIGD)):
                    for t in range(T):
                        nc.gpsimd.indirect_dma_start(
                            g[u][:, n * T + t, :], None, K.taba[:, :],
                            bass.IndirectOffsetOnAxis(ap=rec[u][:].bitcast(I32)[:, t, w:w + 1], axis=0)
                        ).then_inc(s.gat[u], 16)

            def scatters(i, u):
                gp.wait_ge(s.s_made, cnt(i, u) + 1)
                hold(gp, s)
                for n, w in enumerate((R_SIDX, R_DIDX)):
                    for t in range(T):
                        nc.gpsimd.indirect_dma_start(
                            K.rows[:, :],
                            bass.IndirectOffsetOnAxis(ap=rec[u][:].bitcast(I32)[:, t, w:w + 1], axis=0),
                            row[u][:, n * T + t, :], None, bounds_check=K.N - 1, oob_is_err=False
                        ).then_inc(s.sent[u], 16)

            def body(i, u, nxt):
                if nxt:
                    gathers(*nxt)
                scatters(i, u)

            rounds(gp, K, lambda: gathers(0, 0), body)
            for u in range(SLOTS):
                gp.wait_ge(s.sent[u], K.NI * (16 * 2 * T))

        @block.tensor
        def _(pe):
            for i in peeled(pe, K.NI):
                for u in range(SLOTS):
                    c = cnt(i, u)
                    pe.wait_ge(s.s_h3, c + 1)
                    pe.wait_ge(s.s_msg, c + 1)
                    pe.wait_ge(s.s_sum, c)
                    for t in range(T):
                        last = nc.tensor.transpose(ps_m[:, t, :], msg[:, t, :], K.ident[0:P, 0:P])
                    last.then_inc(s.s_tm, 1)
                    pe.wait_ge(s.s_ht, c)
                    for t in range(2 * T):
                        last = nc.tensor.transpose(ps_h[:, t, 0:P], h[:, t, :], K.ident[0:P, 0:P])
                    last.then_inc(s.s_th, 1)
                    pe.wait_ge(s.s_ht, c + 1)
                    pe.wait_ge(s.s_made, c)
                    for t in range(2 * T):
                        last = nc.tensor.matmul(ps_g[:, t, :], ht[:, t, 0:P], K.wd[:], start=True, stop=True)
                    last.then_inc(s.s_lg, 1)
                    pe.wait_ge(s.s_sum, c + 1)
                    for t in range(T):
                        last = nc.tensor.transpose(ps_u[:, t, :], ms[:, 1 + t * P:1 + (t + 1) * P], K.ident[:])
                    last.then_inc(s.s_tr, 1)

        @block.scalar
        def _(act):
            for i in peeled(act, K.NI):
                for u in range(SLOTS):
                    c = cnt(i, u)
                    for half in (0, 1):
                        act.wait_ge(s.s_var, 2 * c + half + 1)
                        nc.scalar.activation(L.sd[:], L.var[:], ACT.Sqrt).then_inc(s.s_sd, 1)
                        act.wait_ge(s.s_sc, 2 * c + half + 1)
                        if half == 0:
                            act.wait_ge(s.s_th, c)
                            act.wait_ge(s.s_made, c)
                        src = x[u] if half == 0 else row[u]
                        for t in range(2 * T):
                            nc.scalar.activation(h[:, t, :], src[:, t, 0:D], ACT.Relu, bias=L.shift[:, t:t + 1],
                                                 scale=L.rstd[:, t:t + 1])
                        nc.scalar.drain().then_inc((s.s_h2, s.s_h3)[half], 1)
                    act.wait_ge(s.s_th, c + 1)
                    act.wait_ge(s.s_lg, c)
                    nc.scalar.copy(ht[:, :, 0:P], ps_h[:, :, 0:P]).then_inc(s.s_ht, 1)

        @block.vector
        def _(v):
            nc.vector.memset(ms[:, CH:CH + 1], 0.0)
            v.drain()
            for i in peeled(v, K.NI):
                for u in range(SLOTS):
                    c = cnt(i, u)
                    v.wait_ge(s.ld[u], (i + 1) * 32)
                    v.wait_ge(s.s_h3, c)
                    ln_stats(nc, v, L, x[u], 2 * T)
                    nc.vector.drain().then_inc(s.s_var, 1)
                    v.wait_ge(s.s_sd, 2 * c + 1)
                    ln_scale(nc, v, L, 2 * T)
                    nc.vector.drain().then_inc(s.s_sc, 1)
                    v.wait_ge(s.s_h2, c + 1)
                    v.wait_ge(s.gat[u], (i + 1) * (16 * 2 * T))
                    nc.vector.tensor_tensor(g[u][:], g[u][:], h[:], ALU.add)
                    v.drain()
                    nc.vector.scalar_tensor_tensor(out=row[u][:, :, 0:D], in0=g[u][:], scalar=0.25, in1=x[u][:],
                                                   op0=ALU.mult, op1=ALU.add)
                    v.drain()
                    ln_stats(nc, v, L, row[u][:, :, 0:D], 2 * T)
                    nc.vector.drain().then_inc(s.s_var, 1)
                    v.wait_ge(s.s_sd, 2 * c + 2)
                    ln_scale(nc, v, L, 2 * T)
                    nc.vector.drain().then_inc(s.s_sc, 1)
                    v.wait_ge(s.rec[u], (i + 1) * 16)
                    v.wait_ge(s.s_h3, c + 1)
                    nc.vector.tensor_tensor(msg[:], h[:, 0:T, :], rec[u][:, :, R_CMSG3:R_CMSG3 + 1].to_broadcast((P, T, D)),
                                            ALU.mult)
                    nc.vector.drain().then_inc(s.s_msg, 1)
                    nc.vector.tensor_copy(row[u][:, 0:T, D:2 * D], h[:, 0:T, :])
                    nc.vector.tensor_tensor(row[u][:, T:2 * T, D:2 * D], h[:, T:2 * T, :],
                                            rec[u][:, :, R_SELF3:R_SELF3 + 1].to_broadcast((P, T, D)), ALU.mult)
                    v.wait_ge(s.s_tr, c)
                    nc.vector.tensor_copy(ms[:, 0:1], ms[:, CH:CH + 1])
                    v.drain()
                    v.wait_ge(s.s_tm, c + 1)
                    nc.vector.tensor_tensor_scan(ms[:, 1:CH + 1], K.nstart[:, span(i, u)],
                                                 ps_m[:].rearrange("p t e -> p (t e)"), ms[:, 0:1],
                                                 ALU.mult, ALU.add).then_inc(s.s_sum, 1)
                    v.wait_ge(s.s_lg, c + 1)
                    nc.vector.tensor_tensor(row[u][:, :, 2 * D:ROW], ps_g[:],
                                            K.bdrow[0:P, :].unsqueeze(1).to_broadcast((P, 2 * T, HEADS)), ALU.add)
                    v.wait_ge(s.s_tr, c + 1)
                    nc.vector.tensor_tensor(row[u][:, T:2 * T, D:2 * D], row[u][:, T:2 * T, D:2 * D], ps_u[:], ALU.add)
                    nc.vector.drain().then_inc(s.s_made, 1)


def steps(eng, K, lag, body):
    full = K.NGI * DSLOTS
    last = full + (1 if K.REM else 0)

    def stages(s, u, known):
        def stage(d):
            if known and not 0 <= s - d < last:
                return None
            q = K.REM if known and s - d == full else D
            return s - d, (u - d) % DSLOTS, q, s * (GT * D) - d * (GT * D)
        return stage

    peel = min(2, K.NGI)
    for n in range(peel * DSLOTS):
        body(n, n % DSLOTS, stages(n, n % DSLOTS, True))
    if K.NGI > peel:
        with eng.Fori(peel, K.NGI) as i:
            for u in range(DSLOTS):
                body(i * DSLOTS + u, u, stages(i * DSLOTS + u, u, False))
    for n in range(full, last + lag):
        body(n, n % DSLOTS, stages(n, n % DSLOTS, True))


def uses(K, c, u):
    return (c - u) // DSLOTS


def node_rows(dram, q, at):
    return dram[bass.ds(at, q * GT), :].rearrange("(p t) d -> p t d", t=GT)


def dense_first(nc, K):
    names = ["s_in", "s_x1", "s_h2", "s_h1", "s_h3", "s_t1", "s_c1", "s_m1", "s_x2", "s_x3", "s_t3", "s_c3", "s_m3",
             "s_row", "s_b12"] + [f"s_{n}{j}" for n in ("var", "sd", "sc") for j in range(3)]
    with phase(nc, "first", names, ["ld", "st"], DSLOTS) as (block, s):
        var, sd, sc = ([s.by_name[f"s_{n}{j}"] for j in range(3)] for n in ("var", "sd", "sc"))
        x = [s.sb(f"x{u}", [D, GT, D]) for u in range(DSLOTS)]
        xa = [s.sb(f"xa{u}", [D, GT, D]) for u in range(DSLOTS)]
        xb = [s.sb(f"xb{u}", [D, GT, D]) for u in range(DSLOTS)]
        row = [s.sb(f"row{u}", [D, GT, ROW]) for u in range(DSLOTS)]
        b12 = s.sb("b12", [D, D])
        h1, h2 = s.sb("h1", [D, GT, D]), s.sb("h2", [D, GT, D])
        ht1, ht3 = s.sb("ht1", [D, GT, D]), s.sb("ht3", [D, GT, D])
        L = [[ln_bufs(s, GT, f"ln{j}{u}", D) for u in range(DSLOTS)] for j in range(3)]
        ps_t1, ps_t3, ps_y = s.ps("t1", [D, 8, D]), s.ps("t3", [D, 8, D]), s.ps("y", [D, 8, D])
        ps_g = s.ps("g", [D, GT, HEADS])

        @block.sync
        def _(sp):
            def body(n, u, stage):
                if g := stage(0):
                    c, u0, q, at = g
                    sp.wait_ge(s.s_in, n - DSLOTS + 1) if again_step(n) else None
                    hold(sp, s)
                    sp.dma_start(x[u0][0:q], node_rows(K.x, q, at)).then_inc(s.ld[u0], 16)
                if g := stage(4):
                    c, u4, q, at = g
                    sp.wait_ge(s.s_row, c + 1)
                    hold(sp, s)
                    sp.dma_start(node_rows(K.rows, q, at), row[u4][0:q]).then_inc(s.st[u4], 16)

            steps(sp, K, 4, body)
            for u in range(DSLOTS):
                sp.wait_ge(s.st[u], 16 * (K.NGI + (1 if K.REM and u == 0 else 0)))

        @block.gpsimd
        def _(g_):
            g_.wait_ge(s.s_b12, 1)

            def body(n, u, stage):
                if g := stage(0):
                    c, u0, q, at = g
                    g_.wait_ge(s.ld[u0], uses(K, c, u0) * 16 + 16)
                    if again_step(n):
                        g_.wait_ge(s.s_h1, c - DSLOTS + 1)
                        g_.wait_ge(s.s_x3, c - DSLOTS + 1)
                    hold(g_, s)
                    wide = lambda b: b[0:q, :].unsqueeze(1).to_broadcast((q, GT, D))
                    nc.gpsimd.tensor_tensor(xa[u0][0:q], x[u0][0:q], wide(K.b2row), ALU.add)
                    nc.gpsimd.tensor_tensor(xb[u0][0:q], x[u0][0:q], wide(b12), ALU.add).then_inc(s.s_in, 1)

            steps(g_, K, 0, body)

        @block.vector
        def _(v):
            nc.vector.tensor_tensor(b12[:], K.b1row[:], K.b2row[:], ALU.add).then_inc(s.s_b12, 1)

            def scale(j, g):
                if g:
                    c, w, q, at = g
                    v.wait_ge(sd[j], c + 1)
                    ln_scale(nc, v, L[j][w], GT, q)
                    nc.vector.drain().then_inc(sc[j], 1)

            def body(n, u, stage):
                g0, g1, g2, g3 = (stage(d) for d in range(4))
                if g0:
                    c, w, q, at = g0
                    v.wait_ge(s.s_in, c + 1)
                    if again_step(n):
                        v.wait_ge(s.s_h1, c - DSLOTS + 1)
                    ln_stats(nc, v, L[0][w], xa[w][0:q], GT)
                    nc.vector.drain().then_inc(var[0], 1)
                if g1:
                    c, w, q, at = g1
                    v.wait_ge(s.s_m1, c + 1)
                    nc.vector.tensor_tensor(xb[w][0:q], xb[w][0:q], ps_y[0:q, 0:GT, :], ALU.add)
                    v.drain()
                    ln_stats(nc, v, L[1][w], xb[w][0:q], GT)
                    nc.vector.drain().then_inc(var[1], 1)
                scale(0, g0)
                if g2:
                    c, w, q, at = g2
                    v.wait_ge(s.s_h2, c + 1)
                    v.wait_ge(s.st[w], uses(K, c, w) * 16)
                    nc.vector.scalar_tensor_tensor(out=row[w][0:q, :, 0:D], in0=h2[0:q], scalar=0.25, in1=xb[w][0:q],
                                                   op0=ALU.mult, op1=ALU.add)
                    nc.vector.drain().then_inc(s.s_x3, 1)
                    if again_step(c):
                        v.wait_ge(s.s_h3, c - DSLOTS + 1)
                    ln_stats(nc, v, L[2][w], row[w][0:q, :, 0:D], GT)
                    nc.vector.drain().then_inc(var[2], 1)
                scale(1, g1)
                scale(2, g2)
                if g3:
                    c, w, q, at = g3
                    v.wait_ge(s.s_m3, c + 1)
                    nc.vector.tensor_tensor(row[w][0:q, :, 2 * D:ROW], ps_g[0:q],
                                            K.bdrow[0:q, :].unsqueeze(1).to_broadcast((q, GT, HEADS)), ALU.add)
                    nc.vector.drain().then_inc(s.s_row, 1)

            steps(v, K, 3, body)

        @block.scalar
        def _(act):
            def root(j, g):
                if g:
                    c, w, q, at = g
                    act.wait_ge(var[j], c + 1)
                    nc.scalar.activation(L[j][w].sd[0:q], L[j][w].var[0:q], ACT.Sqrt).then_inc(sd[j], 1)

            def relus(j, g, out, src, done):
                c, w, q, at = g
                act.wait_ge(sc[j], c + 1)
                for t in range(GT):
                    nc.scalar.activation(out[0:q, t, :], src[0:q, t, 0:D], ACT.Relu, bias=L[j][w].shift[0:q, t:t + 1],
                                         scale=L[j][w].rstd[0:q, t:t + 1])
                nc.scalar.drain().then_inc(done, 1)

            def body(n, u, stage):
                g0, g1, g2, g3 = (stage(d) for d in range(4))
                if g3:
                    c, w, q, at = g3
                    act.wait_ge(s.s_t3, c + 1)
                    act.wait_ge(s.s_m3, c)
                    nc.scalar.copy(ht3[:, :, 0:q], ps_t3[:, 0:GT, 0:q]).then_inc(s.s_c3, 1)
                root(0, g0)
                root(1, g1)
                if g0:
                    act.wait_ge(s.s_t1, g0[0])
                    relus(0, g0, h1, xa[g0[1]], s.s_h1)
                root(2, g2)
                if g1:
                    act.wait_ge(s.s_x3, g1[0])
                    relus(1, g1, h2, xb[g1[1]], s.s_h2)
                if g0:
                    c, w, q, at = g0
                    act.wait_ge(s.s_t1, c + 1)
                    act.wait_ge(s.s_m1, c)
                    nc.scalar.copy(ht1[:, :, 0:q], ps_t1[:, 0:GT, 0:q]).then_inc(s.s_c1, 1)
                if g2:
                    relus(2, g2, row[g2[1]][:, :, D:2 * D], row[g2[1]], s.s_h3)

            steps(act, K, 3, body)

        @block.tensor
        def _(pe):
            def body(n, u, stage):
                g0, g2, g3 = stage(0), stage(2), stage(3)
                if g3:
                    c, w, q, at = g3
                    pe.wait_ge(s.s_c3, c + 1)
                    pe.wait_ge(s.s_row, c)
                    for t in range(GT):
                        last = nc.tensor.matmul(ps_g[0:q, t, :], ht3[:, t, 0:q], K.wd[:], start=True, stop=True)
                    last.then_inc(s.s_m3, 1)
                if g0:
                    c, w, q, at = g0
                    pe.wait_ge(s.s_h1, c + 1)
                    pe.wait_ge(s.s_c1, c)
                    for t in range(GT):
                        last = nc.tensor.transpose(ps_t1[:, t, 0:q], h1[0:q, t, :], K.ident[0:q, 0:q])
                    last.then_inc(s.s_t1, 1)
                    pe.wait_ge(s.s_c1, c + 1)
                    pe.wait_ge(var[1], c)
                    for t in range(GT):
                        last = nc.tensor.matmul(ps_y[0:q, t, :], ht1[:, t, 0:q], K.w1[:], start=True, stop=True)
                    last.then_inc(s.s_m1, 1)
                if g2:
                    c, w, q, at = g2
                    pe.wait_ge(s.s_h3, c + 1)
                    pe.wait_ge(s.s_c3, c)
                    for t in range(GT):
                        last = nc.tensor.transpose(ps_t3[:, t, 0:q], row[w][0:q, t, D:2 * D], K.ident[0:q, 0:q])
                    last.then_inc(s.s_t3, 1)

            steps(pe, K, 3, body)


def dense_last(nc, K):
    ZB = DSLOTS
    names = ["s_tp", "s_ct", "s_mx", "s_exp", "s_x3"]
    with phase(nc, "last", names, ["ld", "st", "comb", "zdone", "zread"], DSLOTS) as (block, s):
        row = [s.sb(f"row{u}", [D, GT, ROW]) for u in range(DSLOTS)]
        res = [s.sb(f"res{u}", [D, GT, D]) for u in range(DSLOTS)]
        at_ = [s.sb(f"at{u}", [D, GT, D]) for u in range(DSLOTS)]
        z = [s.sb(f"z{u}", [D, GT, HEADS, D]) for u in range(DSLOTS)]
        gate = [s.sb(f"gate{u}", [D, GT, HEADS]) for u in range(DSLOTS)]
        sm, rs = s.sb("sm", [D, GT]), s.sb("rs", [D, GT])
        ps_t = s.ps("t", [D, 8, D])
        ps_z = [s.ps(f"z{n}", [D, HEADS, D]) for n in range(ZB)]

        def tile(c, w, t):
            j = w * GT + t
            return j % ZB, uses(K, c, w) * (DSLOTS * GT // ZB) + j // ZB

        @block.sync
        def _(sp):
            def body(n, u, stage):
                if g := stage(0):
                    c, w, q, at = g
                    if again_step(n):
                        sp.wait_ge(s.s_x3, c - DSLOTS + 1)
                        hold(sp, s)
                    sp.dma_start(row[w][0:q], node_rows(K.rows, q, at)).then_inc(s.ld[w], 16)

            steps(sp, K, 0, body)

        @block.gpsimd
        def _(gp):
            def body(n, u, stage):
                if g := stage(2):
                    c, w, q, at = g
                    gp.wait_ge(s.comb[w], uses(K, c, w) + 1)
                    hold(gp, s)
                    gp.dma_start(node_rows(K.out, q, at), res[w][0:q]).then_inc(s.st[w], 16)

            steps(gp, K, 2, body)
            for u in range(DSLOTS):
                gp.wait_ge(s.st[u], 16 * (K.NGI + (1 if K.REM and u == 0 else 0)))

        @block.tensor
        def _(pe):
            def body(n, u, stage):
                if g := stage(0):
                    c, w, q, at = g
                    pe.wait_ge(s.ld[w], uses(K, c, w) * 16 + 16)
                    pe.wait_ge(s.s_ct, c)
                    for t in range(GT):
                        last = nc.tensor.transpose(ps_t[:, t, 0:q], row[w][0:q, t, D:2 * D], K.ident[0:q, 0:q])
                    last.then_inc(s.s_tp, 1)
                if g := stage(1):
                    c, w, q, at = g
                    pe.wait_ge(s.s_ct, c + 1)
                    for t in range(GT):
                        b, before = tile(c, w, t)
                        pe.wait_ge(s.zread[b], before)
                        for half in (0, 1):
                            hs = slice(half * 4, half * 4 + 4)
                            nc.tensor.matmul(ps_z[b][0:q, hs, :], at_[w][:, t, 0:q], K.w3[:, hs, :], start=True, stop=False)
                            last = nc.tensor.matmul(ps_z[b][0:q, hs, :], K.onesb[0:3, 0:q], K.b3s[:, hs, :],
                                                    start=False, stop=True)
                        last.then_inc(s.zdone[b], 1)

            steps(pe, K, 1, body)

        @block.scalar
        def _(act):
            def body(n, u, stage):
                if g := stage(0):
                    c, w, q, at = g
                    act.wait_ge(s.s_tp, c + 1)
                    nc.scalar.copy(at_[w][:, :, 0:q], ps_t[:, 0:GT, 0:q]).then_inc(s.s_ct, 1)
                    act.wait_ge(s.s_mx, c + 1)
                    nc.scalar.activation(gate[w][0:q], gate[w][0:q], ACT.Exp).then_inc(s.s_exp, 1)
                if g := stage(1):
                    c, w, q, at = g
                    act.wait_ge(s.comb[w], uses(K, c, w))
                    for t in range(GT):
                        b, before = tile(c, w, t)
                        act.wait_ge(s.zdone[b], before + 1)
                        nc.scalar.activation(z[w][0:q, t], ps_z[b][0:q], ACT.Relu).then_inc(s.zread[b], 1)

            steps(act, K, 1, body)

        @block.vector
        def _(v):
            def body(n, u, stage):
                if g := stage(0):
                    c, w, q, at = g
                    lg = row[w][0:q, :, 2 * D:ROW]
                    v.wait_ge(s.ld[w], uses(K, c, w) * 16 + 16)
                    nc.vector.tensor_reduce(out=sm[0:q], in_=lg, axis=mybir.AxisListType.X, op=ALU.max)
                    v.drain()
                    nc.vector.tensor_tensor(gate[w][0:q], lg, sm[0:q].unsqueeze(2).to_broadcast((q, GT, HEADS)), ALU.subtract)
                    nc.vector.drain().then_inc(s.s_mx, 1)
                if g := stage(2):
                    c, w, q, at = g
                    v.wait_ge(s.s_exp, c + 1)
                    nc.vector.tensor_reduce(out=sm[0:q], in_=gate[w][0:q], axis=mybir.AxisListType.X, op=ALU.add)
                    v.drain()
                    nc.vector.reciprocal(rs[0:q], sm[0:q])
                    v.drain()
                    nc.vector.tensor_tensor(gate[w][0:q], gate[w][0:q], rs[0:q].unsqueeze(2).to_broadcast((q, GT, HEADS)), ALU.mult)
                    v.drain()
                    for t in range(GT):
                        b, before = tile(c, w, t)
                        v.wait_ge(s.zread[b], before + 1)
                    v.wait_ge(s.st[w], uses(K, c, w) * 16)
                    for k in range(HEADS):
                        for t in range(GT):
                            before = row[w][0:q, t, 0:D] if k == 0 else res[w][0:q, t, :]
                            nc.vector.scalar_tensor_tensor(out=res[w][0:q, t, :], in0=z[w][0:q, t, k, :],
                                                           scalar=gate[w][0:q, t, k:k + 1], in1=before,
                                                           op0=ALU.mult, op1=ALU.add)
                        drained = nc.vector.drain()
                        if k == 0:
                            drained.then_inc(s.s_x3, 1)
                    drained.then_inc(s.comb[w], 1)

            steps(v, K, 2, body)


def build(nc, a, out):
    K = Box()
    K.N, K.E = a["x"].shape[0], a["src"].shape[0]
    K.NT, K.NCH = K.E // P, K.E // CH
    K.NI = K.NCH // SLOTS
    assert K.E == K.NI * SLOTS * CH and K.NT <= D
    K.NP = -(-K.N // LO)
    K.NGI, rest = divmod(K.N, DSLOTS * GT * D)
    K.REM = rest // GT
    assert rest == K.REM * GT and K.REM <= D
    K.x, K.out = a["x"], out
    dram = lambda name, shape: nc.dram_tensor(name, shape, F32, kind="Internal").ap()
    K.info = dram("node_info", (K.NP * LO, 4))
    K.recd, K.recj = dram("records_d", (K.E, REC)), dram("records_j", (K.E, 4))
    K.tab = [dram(f"gat_out{l}", (K.E + 1, D)) for l in range(3)]
    K.tabu, K.taba = dram("gcn_sum", (K.E + 1, D)), dram("hops_sum", (K.E + 1, D))
    K.tabe = [dram(f"hop{n}", (K.E + 1, D)) for n in range(2)]
    K.xs, K.xd, K.vs, K.vd, K.h2 = (dram(n, (K.E, D)) for n in ("x_src", "x_dst", "self_src", "self_dst", "h2_dst"))
    K.rows = dram("node_rows", (K.N, ROW))
    with ExitStack() as ctx:
        sb = lambda c, n, shape, dt=F32: c.enter_context(nc.sbuf_tensor("k_" + n, shape, dt))
        K.wl, K.wr, K.we = sb(ctx, "wl", [D, 3, D]), sb(ctx, "wr", [D, 3, D]), sb(ctx, "we", [32, 3, D])
        K.att, K.bcol = sb(ctx, "att", [D, 3, D]), sb(ctx, "bcol", [D, 3])
        K.w1, K.w3, K.wd = sb(ctx, "w1", [D, D]), sb(ctx, "w3", [D, HEADS, D]), sb(ctx, "wd", [D, HEADS])
        K.b1row, K.b2row, K.bdrow = sb(ctx, "b1row", [D, D]), sb(ctx, "b2row", [D, D]), sb(ctx, "bdrow", [D, HEADS])
        K.b3s = sb(ctx, "b3s", [3, HEADS, D], BF16)
        K.ident, K.identb = sb(ctx, "ident", [D, D]), sb(ctx, "identb", [D, D], BF16)
        K.onesb = sb(ctx, "onesb", [D, D], BF16)
        with ExitStack() as c1:
            K.before, K.carry, K.block2 = sb(c1, "before", [D, D]), sb(c1, "carry", [D, D]), sb(c1, "block2", [D, D])
            K.iota, K.part = sb(c1, "iota", [D, LO]), sb(c1, "part", [D, 1])
            K.cnt = {k: sb(c1, f"cnt_{k}", [K.NP, LO]) for k in ("src", "dst")}
            K.col = {k: sb(c1, f"col_{k}", [P, K.NT]) for k in ("src", "dst")}
            K.occ = {k: sb(c1, f"occ_{k}", [P, K.NT]) for k in ("src", "dst")}
            K.wcol = sb(c1, "wcol", [P, K.NT])
            constants(nc, K, a)
            dense_first(nc, K)
            ranks(nc, K, a)
            node_table(nc, K)
            records(nc, K, a)
        with ExitStack() as c2:
            K.nstart = sb(c2, "nstart", [D, K.E], BF16)
            K.nlast = sb(c2, "nlast", [D, K.E], BF16)
            K.hd = K.u = sb(c2, "hd", [D, K.E])
            flags(nc, K, "flags_d", K.recd, (R_NSTART, R_NLAST), (K.nstart, K.nlast), REC)
            start_form(nc, K, "bounds", True)
            for l in range(3):
                gat(nc, K, a, l)
                spread_back(nc, K, f"spread{l}", K.hd)
            start_form(nc, K, "factors", False)
            gcn_messages(nc, K)
            spread_back(nc, K, "spread_u", K.u)
            gcn_update(nc, K)
            flags(nc, K, "flags_j", K.recj, (J_NSTART,), (K.nstart,), 4)
            for n in range(3):
                hop(nc, K, n)
        with ExitStack() as c2:
            K.nstart = sb(c2, "nstart2", [D, K.E], BF16)
            flags(nc, K, "flags_3", K.recd, (R_NSTART,), (K.nstart,), REC)
            gate_messages(nc, K)
        dense_last(nc, K)


_INS = ["x", "src", "dst", "edge_attr_32", "edge_weight"] + [
    f"L0_gnn_{w}{l}" for l in range(3) for w in ("Wl", "Wr", "We", "att", "b")] + [
    "L1_gnn_weight", "L1_gnn_bias", "L3_gnn_W", "L3_gnn_b", "L3_gnn_W_dict", "L3_gnn_b_dict"]


def kernel(**inputs):
    import numpy as _np
    import concourse.bacc as _bacc
    from concourse.bass_utils import run_bass_kernel_spmd as _run

    nc = _bacc.Bacc("TRN2", target_bir_lowering=False, num_devices=1)
    arrays, args = {}, {}
    for name in _INS:
        v = _np.ascontiguousarray(inputs[name])
        arrays[f"in_{name}"] = v
        args[name] = nc.dram_tensor(f"in_{name}", v.shape, mybir.dt.from_np(v.dtype), kind="ExternalInput").ap()
    shape = inputs["x"].shape
    out = nc.dram_tensor("out", shape, F32, kind="ExternalOutput").ap()
    build(nc, args, out)
    return _run(nc, [arrays], core_ids=[0]).results[0]["out"]
```

```python
import concourse.bass as bass
from concourse import mybir
from contextlib import ExitStack, contextmanager

F32, I32, BF16 = mybir.dt.float32, mybir.dt.int32, mybir.dt.bfloat16
ALU, ACT = mybir.AluOpType, mybir.ActivationFunctionType
D = 128
P = 125
T = 4
CH = P * T
SLOTS = 5
REC = 48
LO = 512
BIG = 1e30
FAR = 1 << 20
EPS = 1e-5
GT = 5
DSLOTS = 3
ROW = 2 * D + 8
HEADS = 8
R_RHO, R_SIGS, R_SIGD, R_SIDX, R_DIDX = 0, 1, 2, 3, 4
R_CMSG, R_SELFS, R_SELFD, R_CMSG3, R_SELF3, R_NSTART, R_NLAST = 5, 6, 7, 8, 9, 10, 11
R_SRC, R_DST = 12, 13
R_EA = 16
J_LINK, J_POSD, J_W, J_NSTART = 0, 1, 2, 3


class Box:
    pass


@contextmanager
def phase(nc, at, names, slots=(), each=SLOTS):
    one = {name: nc.alloc_semaphore(f"{at}_{name}") for name in ("s_held", *names)}
    many = {name: [nc.alloc_semaphore(f"{at}_{name}{u}") for u in range(each)] for name in slots}
    every = [*one.values(), *(h for hs in many.values() for h in hs)]
    s = type("Semaphores", (), {**one, **many, "by_name": one})()
    with ExitStack() as bufs:
        s.sb = lambda name, shape, dt=F32: bufs.enter_context(nc.sbuf_tensor(f"{at}_{name}", shape, dt))
        s.ps = lambda name, shape, dt=F32: bufs.enter_context(nc.psum_tensor(f"{at}_ps_{name}", shape, dt))
        with nc.Block() as block:
            yield block, s
    nc.clear_and_free_semaphores(every)
    nc.all_engine_barrier()


def hold(eng, s):
    eng.sem_inc(s.s_held, 1)


def peeled(eng, n):
    if n > 0:
        yield 0
    if n > 1:
        with eng.Fori(1, n) as i:
            yield i


def rows_of(dram, start, n=CH):
    return dram[bass.ds(start, n), :].rearrange("(t p) d -> p t d", p=P)


def constants(nc, K, a):
    with phase(nc, "const", ["s_load", "s_set", "s_sel", "s_dma2", "s_z"]) as (block, s):
        att_c = s.sb("att_c", [D, 3, 1])
        bsrc = s.sb("bsrc", [1, 4, D])
        zero = s.sb("zero", [1, D])
        iota_i = s.sb("iota_i", [D, LO], I32)
        part_i = s.sb("part_i", [D, 1], I32)
        b3 = s.sb("b3", [1, HEADS * D])
        b3p = [s.sb(f"b3p{n}", [1, HEADS * D], BF16) for n in range(3)]
        NLOADS = 3 * 5 + 10

        @block.sync
        def _(sp):
            for l in range(3):
                sp.dma_start(K.wl[:, l, :], a[f"L0_gnn_Wl{l}"][:, :]).then_inc(s.s_load, 16)
                sp.dma_start(K.wr[:, l, :], a[f"L0_gnn_Wr{l}"][:, :]).then_inc(s.s_load, 16)
                sp.dma_start(K.we[:, l, :], a[f"L0_gnn_We{l}"][:, :]).then_inc(s.s_load, 16)
                sp.dma_start(att_c[:, l, :], a[f"L0_gnn_att{l}"].rearrange("h (c o) -> (h c) o", o=1)).then_inc(s.s_load, 16)
                sp.dma_start(K.bcol[:, l:l + 1], a[f"L0_gnn_b{l}"].rearrange("(p o) -> p o", o=1)).then_inc(s.s_load, 16)
            for l in range(3):
                sp.dma_start(bsrc[:, l, :], a[f"L0_gnn_b{l}"].rearrange("(o d) -> o d", o=1)).then_inc(s.s_load, 16)
            sp.dma_start(K.w1[:], a["L1_gnn_weight"][:, :]).then_inc(s.s_load, 16)
            sp.dma_start(K.w3[:], a["L3_gnn_W"].rearrange("k i o -> i k o")).then_inc(s.s_load, 16)
            sp.dma_start(K.wd[:], a["L3_gnn_W_dict"][:, :]).then_inc(s.s_load, 16)
            sp.dma_start(K.b2row[:], a["L0_gnn_b2"].rearrange("(o d) -> o d", o=1).to_broadcast((D, D))).then_inc(s.s_load, 16)
            sp.dma_start(K.b1row[:], a["L1_gnn_bias"].rearrange("(o d) -> o d", o=1).to_broadcast((D, D))).then_inc(s.s_load, 16)
            sp.dma_start(K.bdrow[:], a["L3_gnn_b_dict"].rearrange("(o d) -> o d", o=1).to_broadcast((D, HEADS))).then_inc(s.s_load, 16)
            sp.dma_start(b3[:], a["L3_gnn_b"].rearrange("(o k) d -> o (k d)", o=1)).then_inc(s.s_load, 16)
            sp.wait_ge(s.s_z, 2)
            for l in range(3):
                sp.dma_start(K.tab[l][K.E:K.E + 1, :], bsrc[:, l, :]).then_inc(s.s_dma2, 16)
            for t in (K.tabu, *K.tabe, K.taba):
                sp.dma_start(t[K.E:K.E + 1, :], zero[:]).then_inc(s.s_dma2, 16)
            for n in range(3):
                sp.dma_start(K.b3s[n:n + 1, :, :].rearrange("p k d -> p (k d)"), b3p[n][:]).then_inc(s.s_dma2, 16)
            sp.wait_ge(s.s_dma2, 16 * (6 + 2 + len(K.tabe)))

        @block.gpsimd
        def _(g):
            nc.gpsimd.memset(K.ident[:], 0.0)
            nc.gpsimd.memset(K.before[:], 1.0)
            nc.gpsimd.memset(K.carry[:], 1.0)
            nc.gpsimd.memset(K.onesb[:], 1.0)
            nc.gpsimd.iota(iota_i[:], pattern=[[1, LO]], base=0, channel_multiplier=0)
            nc.gpsimd.iota(part_i[:], pattern=[[0, 1]], base=0, channel_multiplier=1)
            g.drain()
            nc.gpsimd.affine_select(out=K.ident[:], in_=K.ident[:], compare_op=ALU.not_equal, fill=1.0,
                                    base=0, pattern=[[-1, D]], channel_multiplier=1)
            nc.gpsimd.affine_select(out=K.before[:], in_=K.before[:], compare_op=ALU.is_gt, fill=0.0,
                                    base=0, pattern=[[-1, D]], channel_multiplier=1)
            nc.gpsimd.affine_select(out=K.carry[:], in_=K.carry[:], compare_op=ALU.is_gt, fill=0.0,
                                    base=0, pattern=[[1, D]], channel_multiplier=-1)
            nc.gpsimd.drain().then_inc(s.s_set, 1)

        @block.vector
        def _(v):
            nc.vector.memset(K.block2[:], 0.0)
            v.drain()
            nc.vector.memset(K.block2[0:64, 0:64], 1.0)
            nc.vector.memset(K.block2[64:128, 64:128], 1.0)
            v.wait_ge(s.s_set, 1)
            nc.vector.tensor_copy(K.identb[:], K.ident[:])
            nc.vector.tensor_copy(K.iota[:], iota_i[:])
            nc.vector.tensor_copy(K.part[:], part_i[:])
            nc.vector.memset(zero[:], 0.0).then_inc(s.s_z, 1)
            v.drain()
            v.wait_ge(s.s_load, 16 * NLOADS)
            for l in range(3):
                nc.vector.tensor_scalar(K.att[:, l, :], K.block2[:], att_c[:, l, :], None, ALU.mult)
            for l in range(2):
                nc.vector.tensor_scalar(bsrc[:, l, :], bsrc[:, l, :], 0.0, None, ALU.max)
            for n in range(3):
                nc.vector.tensor_copy(b3p[n][:], b3[:])
                v.drain()
                if n < 2:
                    nc.vector.tensor_tensor(b3[:], b3[:], b3p[n][:], ALU.subtract)
                    v.drain()
            nc.vector.drain().then_inc(s.s_z, 1)


def ranks(nc, K, a):
    KEYS = ("src", "dst")
    with phase(nc, "rank", ["s_rows", "s_keyb", "s_cast", "s_tp", "s_zero"]
               + [f"{n}_{k}" for n in ("part", "down", "along", "copied", "looked", "counted", "dotted") for k in KEYS]
               ) as (block, s):
        keyb = {k: s.sb(f"keyb_{k}", [D, K.E], I32) for k in KEYS}
        raw = s.sb("raw", [K.NT, 2, P], I32)
        rowf = s.sb("rowf", [K.NT, 3, P])
        coli = s.sb("coli", [P, K.NT], I32)
        keyi = s.sb("keyi", [P, K.NT], I32)
        colp = {k: s.sb(f"colp_{k}", [P, K.NT]) for k in KEYS}
        colc = {k: s.sb(f"colc_{k}", [P, K.NT]) for k in KEYS}
        pbi = {(k, b): s.sb(f"pbi_{k}{b}", [K.NP, P], I32) for k in KEYS for b in (0, 1)}
        ohp = {(k, b): s.sb(f"ohp_{k}{b}", [P, K.NP], BF16) for k in KEYS for b in (0, 1)}
        ohc = {(k, b): s.sb(f"ohc_{k}{b}", [P, LO], BF16) for k in KEYS for b in (0, 1)}
        ohpt = {(k, b): s.sb(f"ohpt_{k}{b}", [K.NP, P]) for k in KEYS for b in (0, 1)}
        zb = s.sb("zb", [P, LO], BF16)
        junk = {(k, n): s.sb(f"junk_{k}{n}", [P, (P, LO)[n]]) for k in KEYS for n in (0, 1)}
        earlier = {k: s.sb(f"earlier_{k}", [P, K.NT]) for k in KEYS}
        count = {k: s.ps(f"count_{k}", [K.NP, LO]) for k in KEYS}
        look = {(k, b): s.ps(f"look_{k}{b}", [P, LO]) for k in KEYS for b in (0, 1)}
        pt = s.ps("pt", [P, 3, K.NT])

        @block.sync
        def _(sp):
            tiles = lambda x: x.rearrange("(t p) -> t p", p=P)
            sp.dma_start(raw[:, 0, :], tiles(a["src"])).then_inc(s.s_rows, 16)
            sp.dma_start(raw[:, 1, :], tiles(a["dst"])).then_inc(s.s_rows, 16)
            sp.dma_start(rowf[:, 2, :], tiles(a["edge_weight"])).then_inc(s.s_rows, 16)
            for k in KEYS:
                sp.dma_start(keyb[k][:], a[k].rearrange("(o e) -> o e", o=1).to_broadcast((D, K.E))).then_inc(s.s_keyb, 16)

        @block.tensor
        def _(pe):
            pe.wait_ge(s.s_cast, 1)
            for n in range(3):
                last = nc.tensor.transpose(pt[:, n, :], rowf[:, n, :], K.ident[0:K.NT, 0:K.NT])
            last.then_inc(s.s_tp, 1)
            pe.wait_ge(s.s_zero, 1)
            for k in KEYS:
                nc.tensor.matmul(count[k][:], zb[:, 0:K.NP], zb[:], start=True, stop=True).then_inc(s.by_name[f"counted_{k}"], 1)
            for c in peeled(pe, K.NCH):
                for t in range(T):
                    n = c * T + t
                    for k in KEYS:
                        pe.wait_ge(s.by_name[f"down_{k}"], n + 1)
                        pe.wait_ge(s.by_name[f"along_{k}"], 2 * n + 2)
                        pe.wait_ge(s.by_name[f"copied_{k}"], n + 1)
                        if again(c) or t > 1:
                            pe.wait_ge(s.by_name[f"dotted_{k}"], 2 * n - 2)
                        nc.tensor.matmul(look[k, t % 2][:], ohpt[k, t % 2][:], K.cnt[k][:], start=True,
                                         stop=True).then_inc(s.by_name[f"looked_{k}"], 1)
                        nc.tensor.matmul(count[k][:], ohp[k, t % 2][:], ohc[k, t % 2][:], start=False, stop=True,
                                         skip_group_check=True).then_inc(s.by_name[f"counted_{k}"], 1)

        @block.scalar
        def _(act):
            for c in peeled(act, K.NCH):
                for t in range(T):
                    n = c * T + t
                    for k in KEYS:
                        act.wait_ge(s.by_name[f"counted_{k}"], n + 1)
                        act.wait_ge(s.by_name[f"looked_{k}"], n)
                        nc.scalar.copy(K.cnt[k][:], count[k][:]).then_inc(s.by_name[f"copied_{k}"], 1)
            for k in KEYS:
                act.wait_ge(s.by_name[f"counted_{k}"], K.NT + 1)
                act.wait_ge(s.by_name[f"looked_{k}"], K.NT)
                nc.scalar.copy(K.cnt[k][:], count[k][:])

        @block.vector
        def _(v):
            nc.vector.memset(zb[:], 0.0).then_inc(s.s_zero, 1)
            v.wait_ge(s.s_rows, 48)
            nc.vector.tensor_copy(rowf[:, 0:2, :], raw[:]).then_inc(s.s_cast, 1)
            v.wait_ge(s.s_tp, 1)
            for n, k in enumerate(KEYS):
                nc.vector.tensor_copy(K.col[k][:], pt[:, n, :])
                nc.vector.tensor_copy(keyi[:], pt[:, n, :])
                v.drain()
                nc.vector.tensor_scalar(coli[:], keyi[:], 9, None, ALU.arith_shift_right)
                v.drain()
                nc.vector.tensor_copy(colp[k][:], coli[:])
                v.drain()
                nc.vector.tensor_scalar(coli[:], keyi[:], LO - 1, None, ALU.bitwise_and)
                v.drain()
                nc.vector.tensor_copy(colc[k][:], coli[:])
                v.drain()
            nc.vector.tensor_copy(K.wcol[:], pt[:, 2, :])
            v.wait_ge(s.s_keyb, 32)
            v.drain()

            def onehot(c, t, k):
                n, b = c * T + t, t % 2
                if again(c) or t > 1:
                    v.wait_ge(s.by_name[f"down_{k}"], n - 1)
                nc.vector.tensor_scalar(pbi[k, b][:], keyb[k][0:K.NP, bass.ds(n * P, P)], 9, None,
                                        ALU.arith_shift_right).then_inc(s.by_name[f"part_{k}"], 1)
                v.wait_ge(s.by_name[f"counted_{k}"], c * T + max(t, 1))
                if again(c) or t > 1:
                    v.wait_ge(s.by_name[f"dotted_{k}"], 2 * n - 2)
                nc.vector.tensor_scalar(ohp[k, b][:], K.iota[0:P, 0:K.NP], colp[k][:, bass.ds(n, 1)], None,
                                        ALU.is_equal).then_inc(s.by_name[f"along_{k}"], 1)
                nc.vector.tensor_scalar(ohc[k, b][:], K.iota[0:P, :], colc[k][:, bass.ds(n, 1)], None,
                                        ALU.is_equal).then_inc(s.by_name[f"along_{k}"], 1)

            def dot(n, b, k, known):
                dotted = s.by_name[f"dotted_{k}"]
                if not known or n:
                    v.wait_ge(dotted, 2 * n)
                nc.vector.scalar_tensor_tensor(out=junk[k, 0][:], in0=keyb[k][0:P, bass.ds(n * P, P)],
                                               scalar=K.col[k][:, bass.ds(n, 1)], in1=K.before[0:P, 0:P],
                                               op0=ALU.is_equal, op1=ALU.mult,
                                               accum_out=K.occ[k][:, bass.ds(n, 1)]).then_inc(dotted, 1)
                v.wait_ge(s.by_name[f"looked_{k}"], n + 1)
                v.wait_ge(s.by_name[f"along_{k}"], 2 * n + 2)
                nc.vector.scalar_tensor_tensor(out=junk[k, 1][:], in0=look[k, b][:], scalar=1.0, in1=ohc[k, b][:],
                                               op0=ALU.mult, op1=ALU.mult,
                                               accum_out=earlier[k][:, bass.ds(n, 1)]).then_inc(dotted, 1)

            for c in peeled(v, K.NCH):
                for t in range(T):
                    for k in KEYS:
                        onehot(c, t, k)
                    if again(c) or t:
                        for k in KEYS:
                            dot(c * T + t - 1, (t - 1) % 2, k, not again(c))
            for k in KEYS:
                dot(K.NT - 1, (T - 1) % 2, k, True)
            v.drain()
            for k in KEYS:
                nc.vector.tensor_tensor(K.occ[k][:], K.occ[k][:], earlier[k][:], ALU.add)

        @block.gpsimd
        def _(gp):
            for c in peeled(gp, K.NCH):
                for t in range(T):
                    n, b = c * T + t, t % 2
                    for k in KEYS:
                        gp.wait_ge(s.by_name[f"counted_{k}"], c * T + max(t, 1))
                        gp.wait_ge(s.by_name[f"part_{k}"], n + 1)
                        hold(gp, s)
                        nc.gpsimd.tensor_scalar(ohpt[k, b][:], pbi[k, b][:], K.part[0:K.NP, :], None,
                                                ALU.is_equal).then_inc(s.by_name[f"down_{k}"], 1)


def node_table(nc, K):
    with phase(nc, "table", ["s_tot", "s_carry", "s_tab", "s_out"]) as (block, s):
        info = s.sb("info", [K.NP, LO, 4])
        scan = s.sb("scan", [K.NP, 2, LO])
        pc = s.ps("pc", [K.NP, 2])

        @block.vector
        def _(v):
            for n, k in enumerate(("src", "dst")):
                nc.vector.tensor_copy(info[:, :, n], K.cnt[k][:])
                nc.vector.tensor_tensor_scan(scan[:, n, :], K.cnt[k][:], K.cnt[k][:], 0.0, ALU.add, ALU.bypass)
            nc.vector.drain().then_inc(s.s_tot, 1)
            v.wait_ge(s.s_carry, 1)
            for n in range(2):
                nc.vector.tensor_scalar(info[:, :, 2 + n], scan[:, n, :], pc[:, n:n + 1], None, ALU.add)
            nc.vector.drain().then_inc(s.s_tab, 1)

        @block.tensor
        def _(pe):
            pe.wait_ge(s.s_tot, 1)
            for n in range(2):
                last = nc.tensor.matmul(pc[:, n:n + 1], K.carry[0:K.NP, 0:K.NP], scan[:, n, LO - 1:LO], start=True, stop=True)
            last.then_inc(s.s_carry, 1)

        @block.sync
        def _(sp):
            sp.wait_ge(s.s_tab, 1)
            hold(sp, s)
            sp.dma_start(K.info.rearrange("(p c) w -> p c w", c=LO), info[:]).then_inc(s.s_out, 16)
            sp.wait_ge(s.s_out, 16)


REC_NAMES = ["rec_ea", "rec_idx", "rec_info", "rec_arg", "rec_root", "rec_made", "rec_sent"]


def record_bufs(s):
    R = Box()
    R.idx = s.sb("recidx", [P, 2, T], I32)
    R.inf = s.sb("recinf", [P, 2, T, 4])
    R.rec, R.recj = s.sb("rec", [P, T, REC]), s.sb("recj", [P, T, 4])
    R.pos = s.sb("recpos", [P, 2, T], I32)
    R.arg, R.root, R.inv = (s.sb("rec" + n, [P, 4, T]) for n in ("arg", "root", "inv"))
    R.x = [s.sb(f"recx{n}", [P, T]) for n in range(4)]
    return R


def record_of(K, n, u):
    assert K.NCH == K.NGI - 1
    if isinstance(n, int) and not 0 < n // DSLOTS <= K.NCH:
        return None
    return (n - u - DSLOTS) // DSLOTS


def record_load(sp, s, R, K, a, r):
    if again(r):
        sp.wait_ge(s.rec_sent, r * (16 * 2 * T))
        hold(sp, s)
    sp.dma_start(R.rec[:, :, R_EA:R_EA + 32], rows_of(a["edge_attr_32"], r * CH)).then_inc(s.rec_ea, 16)


def record_gathers(nc, gp, s, R, K, r):
    gp.wait_ge(s.rec_idx, r + 1)
    if again(r):
        gp.wait_ge(s.rec_made, r)
    hold(gp, s)
    for n in range(2):
        for t in range(T):
            nc.gpsimd.indirect_dma_start(R.inf[:, n, t, :], None, K.info[:, :],
                                         bass.IndirectOffsetOnAxis(ap=R.idx[:, n, t:t + 1], axis=0)
                                         ).then_inc(s.rec_info, 16)


def record_scatters(nc, gp, s, R, K, r):
    gp.wait_ge(s.rec_made, r + 1)
    hold(gp, s)
    for t in range(T):
        nc.gpsimd.indirect_dma_start(K.recd[:, :], bass.IndirectOffsetOnAxis(ap=R.pos[:, 0, t:t + 1], axis=0),
                                     R.rec[:, t, :], None).then_inc(s.rec_sent, 16)
        nc.gpsimd.indirect_dma_start(K.recj[:, :], bass.IndirectOffsetOnAxis(ap=R.pos[:, 1, t:t + 1], axis=0),
                                     R.recj[:, t, :], None).then_inc(s.rec_sent, 16)


def record_indices(nc, v, s, R, K, r):
    if again(r):
        v.wait_ge(s.rec_info, r * (16 * 2 * T))
    for n, k in enumerate(("src", "dst")):
        nc.vector.tensor_copy(R.idx[:, n, :], K.col[k][:, bass.ds(r * T, T)])
    nc.vector.drain().then_inc(s.rec_idx, 1)


def record_make(nc, v, s, R, K, r):
    v.wait_ge(s.rec_info, r * (16 * 2 * T) + 16 * 2 * T)
    v.wait_ge(s.rec_ea, r * 16 + 16)
    if again(r):
        v.wait_ge(s.rec_sent, r * (16 * 2 * T))
    tile = lambda b: b[:, bass.ds(r * T, T)]
    f = R.inf
    outs, ins, ejs, eds = (f[:, 0, :, w] for w in range(4))
    outd, ind, ejd, edd = (f[:, 1, :, w] for w in range(4))
    ri = R.rec[:].bitcast(I32)
    rf = R.rec
    ji = R.recj[:].bitcast(I32)
    TS, TT, STT = nc.vector.tensor_scalar, nc.vector.tensor_tensor, nc.vector.scalar_tensor_tensor
    occs, occd = tile(K.occ["src"]), tile(K.occ["dst"])
    TS(R.arg[:, 0, :], outs, 1.0, None, ALU.add)
    TS(R.arg[:, 1, :], outd, 1.0, None, ALU.add)
    TS(R.arg[:, 2, :], ins, 1.0, None, ALU.add)
    TS(R.arg[:, 3, :], ind, 1.0, None, ALU.add)
    nc.vector.drain().then_inc(s.rec_arg, 1)
    TS(R.x[0][:], ins, 1.0, None, ALU.min)
    TS(R.x[1][:], outd, 1.0, None, ALU.min)
    TS(R.x[2][:], eds, -(K.E + 1.0), None, ALU.add)
    TS(R.x[3][:], ejd, -(K.E + 1.0), None, ALU.add)
    v.drain()
    TT(R.x[2][:], R.x[2][:], R.x[0][:], ALU.mult)
    TT(R.x[3][:], R.x[3][:], R.x[1][:], ALU.mult)
    v.drain()
    TS(ri[:, :, R_RHO], R.x[2][:], float(K.E), None, ALU.add)
    TS(ri[:, :, R_SIGD], R.x[3][:], float(K.E), None, ALU.add)
    TS(ji[:, :, J_LINK], R.x[3][:], float(K.E), None, ALU.add)
    TS(ri[:, :, R_SIGS], ejs, -1.0, None, ALU.add)
    nc.vector.tensor_copy(ri[:, :, R_SRC], tile(K.col["src"]))
    nc.vector.tensor_copy(ri[:, :, R_DST], tile(K.col["dst"]))
    v.drain()
    TT(R.x[1][:], edd, ind, ALU.subtract)
    TT(R.x[3][:], ejs, outs, ALU.subtract)
    v.drain()
    TT(R.x[1][:], R.x[1][:], occd, ALU.add)
    TT(R.x[3][:], R.x[3][:], occs, ALU.add)
    v.drain()
    nc.vector.tensor_copy(R.pos[:, 0, :], R.x[1][:])
    nc.vector.tensor_copy(R.pos[:, 1, :], R.x[3][:])
    nc.vector.tensor_copy(ji[:, :, J_POSD], R.x[1][:])
    nc.vector.tensor_copy(R.recj[:, :, J_W], tile(K.wcol))
    TS(R.recj[:, :, J_NSTART], occs, 1.0, None, ALU.min)
    TS(rf[:, :, R_NSTART], occd, 1.0, None, ALU.min)
    v.drain()
    TT(R.x[1][:], ind, occd, ALU.subtract)
    TT(R.x[2][:], outs, occs, ALU.subtract)
    v.drain()
    TS(R.x[1][:], R.x[1][:], -1.0, 1.0, ALU.add, ALU.min)
    TS(R.x[2][:], R.x[2][:], -1.0, 1.0, ALU.add, ALU.min)
    v.drain()
    nc.vector.tensor_copy(rf[:, :, R_NLAST], R.x[1][:])
    TT(R.x[2][:], R.x[2][:], R.x[0][:], ALU.max)
    v.drain()
    STT(ri[:, :, R_SIDX], R.x[2][:], float(FAR), tile(K.col["src"]), ALU.mult, ALU.add)
    STT(ri[:, :, R_DIDX], R.x[1][:], float(FAR), tile(K.col["dst"]), ALU.mult, ALU.add)
    v.wait_ge(s.rec_root, r + 1)
    nc.vector.reciprocal(R.inv[:], R.root[:])
    v.drain()
    TT(rf[:, :, R_CMSG], R.inv[:, 0, :], R.inv[:, 1, :], ALU.mult)
    TT(rf[:, :, R_SELFS], R.inv[:, 0, :], R.inv[:, 0, :], ALU.mult)
    TT(rf[:, :, R_SELFD], R.inv[:, 1, :], R.inv[:, 1, :], ALU.mult)
    TT(rf[:, :, R_CMSG3], R.inv[:, 2, :], R.inv[:, 3, :], ALU.mult)
    TT(rf[:, :, R_SELF3], R.inv[:, 3, :], R.inv[:, 3, :], ALU.mult)
    nc.vector.memset(rf[:, :, R_DST + 1:R_EA], 0.0)
    nc.vector.drain().then_inc(s.rec_made, 1)


def ahead(eng, K, body):
    for i in peeled(eng, K.NI):
        for u in range(SLOTS):
            body(i, u)


def again(i):
    return not (isinstance(i, int) and i == 0)


def again_step(n):
    return not isinstance(n, int) or n >= DSLOTS


def cnt(i, u):
    return i * SLOTS + u


def span(i, u):
    return bass.ds(i * (SLOTS * CH) + u * CH, CH)


def chunk_steps(eng, K, lag, body):
    def stages(n, u, known):
        def stage(d):
            if known and not 0 <= n - d < K.NCH:
                return None
            return n - d, (u - d) % SLOTS, n * CH - d * CH
        return stage

    peel = min(2, K.NI)
    for n in range(peel * SLOTS):
        body(n, n % SLOTS, stages(n, n % SLOTS, True))
    if K.NI > peel:
        with eng.Fori(peel, K.NI) as i:
            for u in range(SLOTS):
                body(i * SLOTS + u, u, stages(i * SLOTS + u, u, False))
    for n in range(K.NCH, K.NCH + lag):
        body(n, n % SLOTS, stages(n, n % SLOTS, True))


def turn(c, w):
    return (c - w) // SLOTS


def again_chunk(n):
    return not isinstance(n, int) or n >= SLOTS


def flags(nc, K, at, table, words, outs, width):
    with phase(nc, at, ["s_diag", "s_ps", "s_cp"], ["rec"]) as (block, s):
        rec = [s.sb(f"rec{u}", [P, T, width]) for u in range(SLOTS)]
        diag = s.sb("diag", [P, len(words), T, P], BF16)
        ps = [s.ps(f"ps{n}", [D, CH]) for n in range(len(words))]

        @block.sync
        def _(sp):
            for i in peeled(sp, K.NI):
                for u in range(SLOTS):
                    sp.wait_ge(s.s_diag, i * SLOTS)
                    hold(sp, s)
                    sp.dma_start(rec[u][:], rows_of(table, i * (SLOTS * CH) + u * CH)).then_inc(s.rec[u], 16)

        @block.vector
        def _(v):
            for i in peeled(v, K.NI):
                for u in range(SLOTS):
                    v.wait_ge(s.rec[u], (i + 1) * 16)
                    v.wait_ge(s.s_ps, cnt(i, u))
                    for n, w in enumerate(words):
                        nc.vector.tensor_tensor(diag[:, n], K.identb[0:P, 0:P].unsqueeze(1).to_broadcast((P, T, P)),
                                                rec[u][:, :, w:w + 1].to_broadcast((P, T, P)), ALU.mult)
                    nc.vector.drain().then_inc(s.s_diag, 1)

        @block.tensor
        def _(pe):
            for i in peeled(pe, K.NI):
                for u in range(SLOTS):
                    pe.wait_ge(s.s_diag, cnt(i, u) + 1)
                    pe.wait_ge(s.s_cp, cnt(i, u))
                    for n in range(len(words)):
                        last = nc.tensor.matmul(ps[n][:], K.onesb[0:P, :], diag[:, n].rearrange("p t e -> p (t e)"),
                                                start=True, stop=True)
                    last.then_inc(s.s_ps, 1)

        @block.scalar
        def _(act):
            for i in peeled(act, K.NI):
                for u in range(SLOTS):
                    act.wait_ge(s.s_ps, cnt(i, u) + 1)
                    hold(act, s)
                    for n in range(len(words)):
                        last = nc.scalar.copy(outs[n][:, span(i, u)], ps[n][:])
                    nc.scalar.drain().then_inc(s.s_cp, 1)


def spread_back(nc, K, at, x):
    with phase(nc, at, []) as (block, s):
        @block.vector
        def _(v):
            E = K.E
            nc.vector.scalar_tensor_tensor(out=x[:], in0=K.nlast[:], scalar=-1.0, in1=x[:], op0=ALU.add, op1=ALU.mult)
            v.drain()
            nc.vector.tensor_tensor_scan(x[:, E - 1::-1], K.nlast[:, E - 1::-1], x[:, E - 1::-1], 0.0,
                                         ALU.mult, ALU.subtract)


def ln_stats(nc, v, L, x, n):
    for t in range(n):
        nc.vector.bn_stats(L.st[0:x.shape[0], t, :], x[:, t, :])
    v.drain()
    for t in range(n):
        nc.vector.bn_aggr(L.mv[0:x.shape[0], t, :], L.st[0:x.shape[0], t, :])
    v.drain()
    nc.vector.tensor_scalar(L.var[0:x.shape[0], 0:n], L.mv[0:x.shape[0], 0:n, 1], EPS, None, ALU.add)


def ln_scale(nc, v, L, n, np_=P):
    nc.vector.reciprocal(L.rstd[0:np_, 0:n], L.sd[0:np_, 0:n])
    v.drain()
    nc.vector.scalar_tensor_tensor(out=L.shift[0:np_, 0:n], in0=L.mv[0:np_, 0:n, 0], scalar=-1.0,
                                   in1=L.rstd[0:np_, 0:n], op0=ALU.mult, op1=ALU.mult)


def ln_bufs(s, n, name="ln", np_=P):
    L = Box()
    L.st = s.sb(name + "st", [np_, n, 6])
    L.mv = s.sb(name + "mv", [np_, n, 2])
    L.var, L.sd = s.sb(name + "var", [np_, n]), s.sb(name + "sd", [np_, n])
    L.rstd, L.shift = s.sb(name + "rstd", [np_, n]), s.sb(name + "shift", [np_, n])
    return L


def gat(nc, K, a, l):
    names = ["s_var", "s_sd", "s_sc", "s_ln", "s_xp", "s_in", "s_e", "s_er", "s_el", "s_l", "s_xj", "s_arg",
             "s_pj", "s_ex", "s_den", "s_num", "s_dt", "s_rd", "s_rw", "s_rb", "s_o", "s_h", "s_tr", "s_row", "s_st"]
    first_layer = l == 0
    NG = 2 if first_layer else 1
    with phase(nc, f"gat{l}", names, ["rec", "gat", "keep"]) as (block, s):
        rec = [s.sb(f"rec{u}", [P, T, REC]) for u in range(SLOTS)]
        g = [s.sb(f"g{u}", [P, NG * T, D]) for u in range(SLOTS)]
        if first_layer:
            L = ln_bufs(s, 2 * T)
            h = s.sb("h", [P, 2 * T, D])
            hdt = s.sb("hdt", [D, T, P])
        hst = [s.sb(f"hst{u}", [D, T, P]) for u in range(SLOTS)]
        eat = s.sb("eat", [32, T, P])
        er, el = s.sb("er", [D, CH]), s.sb("el", [D, CH])
        m = s.sb("m", [D, CH + 1])
        ta, tp = s.sb("ta", [D, CH]), s.sb("tp", [D, CH])
        xa, xp = s.sb("xa", [D, CH]), s.sb("xp", [D, CH])
        den = s.sb("den", [D, CH + 1])
        num = [s.sb(f"num{u}", [D, CH + 1]) for u in range(SLOTS)]
        rden = s.sb("rden", [P, T, 2])
        rwide = s.sb("rwide", [P, T, 2, 64])
        wx = s.sb("wx", [D, CH])
        o = s.sb("o", [D, CH])
        ht = s.sb("ht", [D, T, P])
        orow = s.sb("orow", [P, T, D])
        ps_s = s.ps("s", [D, T, P])
        ps_d = s.ps("d", [D, T, P]) if first_layer else None
        ps_ea = s.ps("ea", [32, T, P])
        ps_xj, ps_e, ps_l = s.ps("xj", [D, CH]), s.ps("e", [D, CH]), s.ps("l", [D, CH])
        ps_o = s.ps("o", [P, T, D])
        ps_r = s.ps("r", [D, 512])
        ps_den = ps_r[0:P, CH:CH + 2 * T].rearrange("p (t k) -> p t k", k=2)
        flat = lambda b: b[:].rearrange("p t e -> p (t e)")

        @block.sync
        def _(sp):
            def body(n, u, stage):
                if c := stage(0):
                    c, w, at = c
                    if again_chunk(n):
                        sp.wait_ge(s.s_xp, c - SLOTS + 1)
                        hold(sp, s)
                    sp.dma_start(rec[w][:], rows_of(K.recd, at)).then_inc(s.rec[w], 16)
                if first_layer and (c := stage(2)):
                    c, w, at = c
                    sp.wait_ge(s.gat[w], turn(c, w) * (16 * NG * T) + 16 * NG * T)
                    hold(sp, s)
                    sp.dma_start(rows_of(K.xs, at), g[w][:, 0:T, :]).then_inc(s.keep[w], 16)
                    sp.dma_start(rows_of(K.xd, at), g[w][:, T:2 * T, :]).then_inc(s.keep[w], 16)
                if c := stage(6):
                    c, w, at = c
                    sp.wait_ge(s.s_row, c + 1)
                    hold(sp, s)
                    sp.dma_start(rows_of(K.tab[l], at), orow[:]).then_inc(s.s_st, 16)

            chunk_steps(sp, K, 6, body)
            sp.wait_ge(s.s_st, 16 * K.NCH)
            if first_layer:
                for u in range(SLOTS):
                    sp.wait_ge(s.keep[u], 32 * K.NI)

        @block.gpsimd
        def _(gp):
            src = K.x if first_layer else K.tab[l - 1]
            words = (R_SRC, R_DST) if first_layer else (R_RHO,)

            def body(n, u, stage):
                if c := stage(0):
                    c, w, at = c
                    gp.wait_ge(s.rec[w], turn(c, w) * 16 + 16)
                    if again_chunk(n):
                        gp.wait_ge(s.s_xp, c - SLOTS + 1)
                        if first_layer:
                            gp.wait_ge(s.s_ln, c - SLOTS + 1)
                            gp.wait_ge(s.keep[w], turn(c, w) * 32)
                    hold(gp, s)
                    for k, word in enumerate(words):
                        for t in range(T):
                            nc.gpsimd.indirect_dma_start(
                                g[w][:, k * T + t, :], None, src[:, :],
                                bass.IndirectOffsetOnAxis(ap=rec[w][:].bitcast(I32)[:, t, word:word + 1], axis=0)
                            ).then_inc(s.gat[w], 16)

            chunk_steps(gp, K, 0, body)

        @block.tensor
        def _(pe):
            def body(n, u, stage):
                c1, c2, c4, c5 = (stage(d) for d in (1, 2, 4, 5))
                if c2:
                    c, w, at = c2
                    pe.wait_ge(s.s_el, c + 1)
                    pe.wait_ge(s.s_arg, c)
                    nc.tensor.matmul(ps_l[:], K.att[:, l, :], el[:], start=True, stop=True).then_inc(s.s_l, 1)
                if c4:
                    c, w, at = c4
                    pe.wait_ge(s.s_den, c + 1)
                    pe.wait_ge(s.s_rd, c)
                    pe.wait_ge(s.s_o, c)
                    for t in range(T):
                        last = nc.tensor.matmul(ps_den[:, t, :], den[:, 1 + t * P:1 + (t + 1) * P], K.ident[:, 0::64],
                                                start=True, stop=True)
                    last.then_inc(s.s_dt, 1)
                if c1:
                    c, w, at = c1
                    rows = h if first_layer else g[w]
                    if first_layer:
                        pe.wait_ge(s.s_ln, c + 1)
                    else:
                        pe.wait_ge(s.gat[w], turn(c, w) * (16 * NG * T) + 16 * NG * T)
                    pe.wait_ge(s.rec[w], turn(c, w) * 16 + 16)
                    pe.wait_ge(s.s_in, c)
                    for t in range(T):
                        nc.tensor.transpose(ps_s[:, t, :], rows[:, t, :], K.ident[0:P, 0:P])
                        if first_layer:
                            nc.tensor.transpose(ps_d[:, t, :], rows[:, T + t, :], K.ident[0:P, 0:P])
                        last = nc.tensor.transpose(ps_ea[:, t, :], rec[w][:, t, R_EA:R_EA + 32], K.ident[0:P, 0:P])
                    last.then_inc(s.s_xp, 1)
                if c5:
                    c, w, at = c5
                    pe.wait_ge(s.s_h, c + 1)
                    pe.wait_ge(s.s_row, c)
                    for t in range(T):
                        last = nc.tensor.transpose(ps_o[:, t, :], ht[:, t, :], K.ident[:])
                    last.then_inc(s.s_tr, 1)
                if c1:
                    c, w, at = c1
                    pe.wait_ge(s.s_in, c + 1)
                    pe.wait_ge(s.s_el, c)
                    nc.tensor.matmul(ps_e[:], K.wl[:, l, :], flat(hst[w]), start=True, stop=False)
                    hd = flat(hdt) if first_layer else K.hd[:, bass.ds(at, CH)]
                    nc.tensor.matmul(ps_e[:], K.wr[:, l, :], hd, start=False, stop=False)
                    nc.tensor.matmul(ps_e[:], K.we[:, l, :], flat(eat), start=False, stop=True).then_inc(s.s_e, 1)
                if c4:
                    c, w, at = c4
                    pe.wait_ge(s.s_rw, c + 1)
                    for t in range(T):
                        last = nc.tensor.matmul(ps_r[:, t * P:(t + 1) * P],
                                                rwide[:, t, :, :].rearrange("p k d -> p (k d)"), K.ident[0:P, 0:P],
                                                start=True, stop=True)
                    last.then_inc(s.s_rb, 1)
                if c2:
                    c, w, at = c2
                    pe.wait_ge(s.s_pj, c)
                    nc.tensor.matmul(ps_xj[:], K.wl[:, l, :], flat(hst[w]), start=True, stop=True).then_inc(s.s_xj, 1)

            chunk_steps(pe, K, 5, body)

        @block.scalar
        def _(act):
            def body(n, u, stage):
                c0, c1, c2, c3, c4, c5 = (stage(d) for d in range(6))
                if c5:
                    c, w, at = c5
                    act.wait_ge(s.s_o, c + 1)
                    act.wait_ge(s.s_tr, c)
                    fn = ACT.Relu if l < 2 else ACT.Identity
                    nc.scalar.activation(flat(ht), o[:], fn, bias=K.bcol[:, l:l + 1])
                    nc.scalar.activation(K.hd[:, bass.ds(at, CH)], o[:], fn, bias=K.bcol[:, l:l + 1])
                    nc.scalar.drain().then_inc(s.s_h, 1)
                if c0 and first_layer:
                    c, w, at = c0
                    act.wait_ge(s.s_var, c + 1)
                    nc.scalar.activation(L.sd[:], L.var[:], ACT.Sqrt).then_inc(s.s_sd, 1)
                if c1:
                    c, w, at = c1
                    act.wait_ge(s.s_xp, c + 1)
                    act.wait_ge(s.s_e, c)
                    if again_chunk(n):
                        act.wait_ge(s.s_xj, c - SLOTS + 1)
                    nc.scalar.copy(hst[w][:], ps_s[:])
                    if first_layer:
                        nc.scalar.copy(hdt[:], ps_d[:])
                    nc.scalar.copy(eat[:], ps_ea[:])
                    nc.scalar.drain().then_inc(s.s_in, 1)
                if c0 and first_layer:
                    c, w, at = c0
                    act.wait_ge(s.s_sc, c + 1)
                    act.wait_ge(s.s_xp, c)
                    for t in range(2 * T):
                        nc.scalar.activation(h[:, t, :], g[w][:, t, :], ACT.Relu, bias=L.shift[:, t:t + 1],
                                             scale=L.rstd[:, t:t + 1])
                    nc.scalar.drain().then_inc(s.s_ln, 1)
                if c5:
                    c, w, at = c5
                    act.wait_ge(s.s_tr, c + 1)
                    act.wait_ge(s.s_st, c * 16)
                    nc.scalar.copy(orow[:], ps_o[:]).then_inc(s.s_row, 1)
                if c4:
                    c, w, at = c4
                    act.wait_ge(s.s_rd, c + 1)
                    act.wait_ge(s.s_rb, c)
                    nc.scalar.copy(rwide[:], rden[:].unsqueeze(3).to_broadcast((P, T, 2, 64))).then_inc(s.s_rw, 1)
                if c1:
                    c, w, at = c1
                    act.wait_ge(s.s_e, c + 1)
                    act.wait_ge(s.s_el, c)
                    nc.scalar.activation(er[:], ps_e[:], ACT.Relu, scale=0.8).then_inc(s.s_er, 1)
                if c2:
                    c, w, at = c2
                    act.wait_ge(s.s_arg, c + 1)
                    act.wait_ge(s.s_num, c)
                    nc.scalar.activation(xa[:], ta[:], ACT.Exp)
                    nc.scalar.activation(xp[:], tp[:], ACT.Exp)
                    nc.scalar.drain().then_inc(s.s_ex, 1)

            chunk_steps(act, K, 5, body)

        @block.vector
        def _(v):
            for b in (m, den, num[SLOTS - 1]):
                nc.vector.memset(b[:, CH:CH + 1], 0.0)
            v.drain()

            def body(n, u, stage):
                c0, c1, c2, c3, c4, c5 = (stage(d) for d in range(6))
                if c5:
                    c, w, at = c5
                    v.wait_ge(s.s_rb, c + 1)
                    v.wait_ge(s.s_h, c)
                    nc.vector.tensor_tensor(o[:], num[w][:, 1:CH + 1], ps_r[:, 0:CH], ALU.mult).then_inc(s.s_o, 1)
                if c0 and first_layer:
                    c, w, at = c0
                    v.wait_ge(s.gat[w], turn(c, w) * (16 * NG * T) + 16 * NG * T)
                    v.wait_ge(s.s_ln, c)
                    ln_stats(nc, v, L, g[w], 2 * T)
                    nc.vector.drain().then_inc(s.s_var, 1)
                if c2:
                    c, w, at = c2
                    low = K.nstart[:, bass.ds(at, CH)]
                    nc.vector.tensor_copy(m[:, 0:1], m[:, CH:CH + 1])
                    v.drain()
                    v.wait_ge(s.s_l, c + 1)
                    nc.vector.tensor_tensor_scan(m[:, 1:CH + 1], low, ps_l[:], m[:, 0:1], ALU.min, ALU.max)
                    v.drain()
                    v.wait_ge(s.s_ex, c)
                    nc.vector.tensor_tensor(ta[:], m[:, 0:CH], m[:, 1:CH + 1], ALU.subtract)
                    nc.vector.tensor_tensor(tp[:], ps_l[:], m[:, 1:CH + 1], ALU.subtract)
                    v.drain()
                    nc.vector.tensor_tensor(ta[:], ta[:], low, ALU.min)
                    nc.vector.drain().then_inc(s.s_arg, 1)
                if c0 and first_layer:
                    c, w, at = c0
                    v.wait_ge(s.s_sd, c + 1)
                    ln_scale(nc, v, L, 2 * T)
                    nc.vector.drain().then_inc(s.s_sc, 1)
                if c4:
                    c, w, at = c4
                    v.wait_ge(s.s_dt, c + 1)
                    v.wait_ge(s.s_rw, c)
                    nc.vector.tensor_scalar(rden[:], ps_den, 1e-16, None, ALU.add)
                    v.drain()
                    nc.vector.reciprocal(rden[:], rden[:])
                    nc.vector.drain().then_inc(s.s_rd, 1)
                if c3:
                    c, w, at = c3
                    before = num[(w - 1) % SLOTS]
                    v.wait_ge(s.s_ex, c + 1)
                    v.wait_ge(s.s_xj, c + 1)
                    nc.vector.tensor_tensor(wx[:], xp[:], ps_xj[:], ALU.mult).then_inc(s.s_pj, 1)
                    nc.vector.tensor_copy(num[w][:, 0:1], before[:, CH:CH + 1])
                    v.wait_ge(s.s_dt, c)
                    nc.vector.tensor_copy(den[:, 0:1], den[:, CH:CH + 1])
                    v.drain()
                    nc.vector.tensor_tensor_scan(den[:, 1:CH + 1], xa[:], xp[:], den[:, 0:1], ALU.mult,
                                                 ALU.add).then_inc(s.s_den, 1)
                    nc.vector.tensor_tensor_scan(num[w][:, 1:CH + 1], xa[:], wx[:], num[w][:, 0:1], ALU.mult, ALU.add)
                    nc.vector.drain().then_inc(s.s_num, 1)
                if c1:
                    c, w, at = c1
                    v.wait_ge(s.s_er, c + 1)
                    v.wait_ge(s.s_l, c)
                    nc.vector.scalar_tensor_tensor(out=el[:], in0=ps_e[:], scalar=0.2, in1=er[:], op0=ALU.mult,
                                                   op1=ALU.add).then_inc(s.s_el, 1)

            chunk_steps(v, K, 5, body)


def start_form(nc, K, at, bounds):
    with phase(nc, at, []) as (block, s):
        @block.vector
        def _(v):
            if bounds:
                nc.vector.tensor_scalar(K.nstart[:], K.nstart[:], 2 * BIG, -BIG, ALU.mult, ALU.add)
            else:
                nc.vector.tensor_scalar(K.nstart[:], K.nstart[:], 0.0, None, ALU.is_gt)


def gcn_messages(nc, K):
    names = ["s_hc", "s_dt", "s_x1", "s_sd", "s_sc", "s_h", "s_tm", "s_sum", "s_tr", "s_row",
             "s_st"]
    with phase(nc, "msg", names, ["rec", "ld", "gat", "stx", "sv"]) as (block, s):
        rec = [s.sb(f"rec{u}", [P, T, REC]) for u in range(SLOTS)]
        g = [s.sb(f"g{u}", [P, T, D]) for u in range(SLOTS)]
        x = [s.sb(f"x{u}", [P, 2 * T, D]) for u in range(SLOTS)]
        L = ln_bufs(s, 2 * T)
        sc, sh = s.sb("sc", [P, 3 * T]), s.sb("sh", [P, 3 * T])
        hc = s.sb("hc", [D, T, P])
        h = [s.sb(f"h{u}", [P, 3 * T, D]) for u in range(SLOTS)]
        us = s.sb("us", [D, CH + 1])
        urow = s.sb("urow", [P, T, D])
        ps_d, ps_m, ps_u = s.ps("d", [P, T, D]), s.ps("m", [D, T, P]), s.ps("u", [P, T, D])

        @block.sync
        def _(sp):
            def body(n, u, stage):
                if c := stage(0):
                    c, w, at = c
                    if again_chunk(n):
                        sp.wait_ge(s.s_h, c - SLOTS + 1)
                        hold(sp, s)
                        sp.wait_ge(s.s_sc, c - SLOTS + 1)
                        hold(sp, s)
                        sp.wait_ge(s.stx[w], 32 * turn(c, w))
                        hold(sp, s)
                        sp.wait_ge(s.gat[w], turn(c, w) * (16 * T))
                        hold(sp, s)
                    sp.dma_start(rec[w][:], rows_of(K.recd, at)).then_inc(s.rec[w], 16)
                    sp.dma_start(x[w][:, 0:T, :], rows_of(K.xs, at)).then_inc(s.ld[w], 16)
                    sp.dma_start(x[w][:, T:2 * T, :], rows_of(K.xd, at)).then_inc(s.ld[w], 16)

            chunk_steps(sp, K, 0, body)

        @block.gpsimd
        def _(gp):
            def body(n, u, stage):
                if c := stage(0):
                    c, w, at = c
                    gp.wait_ge(s.rec[w], turn(c, w) * 16 + 16)
                    if again_chunk(n):
                        gp.wait_ge(s.s_x1, c - SLOTS + 1)
                    hold(gp, s)
                    for t in range(T):
                        nc.gpsimd.indirect_dma_start(
                            g[w][:, t, :], None, K.tab[2][:, :],
                            bass.IndirectOffsetOnAxis(ap=rec[w][:].bitcast(I32)[:, t, R_RHO:R_RHO + 1], axis=0)
                        ).then_inc(s.gat[w], 16)

            chunk_steps(gp, K, 0, body)

        @block.tensor
        def _(pe):
            def body(n, u, stage):
                c0, c2 = stage(0), stage(2)
                if c2:
                    c, w, at = c2
                    pe.wait_ge(s.s_h, c + 1)
                    pe.wait_ge(s.s_sum, c)
                    for t in range(T):
                        last = nc.tensor.transpose(ps_m[:, t, :], h[w][:, t, :], K.ident[0:P, 0:P])
                    last.then_inc(s.s_tm, 1)
                if c0:
                    c, w, at = c0
                    pe.wait_ge(s.s_hc, c + 1)
                    pe.wait_ge(s.s_x1, c)
                    for t in range(T):
                        last = nc.tensor.transpose(ps_d[:, t, :], hc[:, t, :], K.ident[:])
                    last.then_inc(s.s_dt, 1)
                if c2:
                    c, w, at = c2
                    pe.wait_ge(s.s_sum, c + 1)
                    pe.wait_ge(s.s_row, c)
                    for t in range(T):
                        last = nc.tensor.transpose(ps_u[:, t, :], us[:, 1 + t * P:1 + (t + 1) * P], K.ident[:])
                    last.then_inc(s.s_tr, 1)

            chunk_steps(pe, K, 2, body)

        @block.scalar
        def _(act):
            def body(n, u, stage):
                c0, c1, c2, c3 = (stage(d) for d in range(4))
                if c2:
                    c, w, at = c2
                    act.wait_ge(s.s_h, c + 1)
                    act.dma_start(rows_of(K.vs, at), h[w][:, T:2 * T, :]).then_inc(s.sv[w], 16)
                    act.dma_start(rows_of(K.vd, at), h[w][:, 2 * T:3 * T, :]).then_inc(s.sv[w], 16)
                if c3:
                    c, w, at = c3
                    act.wait_ge(s.s_row, c + 1)
                    act.dma_start(rows_of(K.tabu, at), urow[:]).then_inc(s.s_st, 16)
                if c0:
                    c, w, at = c0
                    act.wait_ge(s.s_dt, c)
                    hold(act, s)
                    nc.scalar.copy(hc[:].rearrange("p t e -> p (t e)"), K.hd[:, bass.ds(at, CH)]).then_inc(s.s_hc, 1)
                if c1:
                    c, w, at = c1
                    act.wait_ge(s.s_x1, c + 1)
                    nc.scalar.activation(L.sd[:], L.var[:], ACT.Sqrt).then_inc(s.s_sd, 1)
                    act.dma_start(rows_of(K.xs, at), x[w][:, 0:T, :]).then_inc(s.stx[w], 16)
                    act.dma_start(rows_of(K.xd, at), x[w][:, T:2 * T, :]).then_inc(s.stx[w], 16)
                    act.wait_ge(s.s_sc, c + 1)
                    if again_chunk(n):
                        act.wait_ge(s.s_tm, c - SLOTS + 1)
                    act.wait_ge(s.sv[w], 32 * turn(c, w))
                    for k in range(3):
                        for t in range(T):
                            nc.scalar.activation(h[w][:, k * T + t, :], x[w][:, (0, 0, T)[k] + t, :], ACT.Relu,
                                                 bias=sh[:, k * T + t:k * T + t + 1],
                                                 scale=sc[:, k * T + t:k * T + t + 1])
                    nc.scalar.drain().then_inc(s.s_h, 1)
                if c2:
                    c, w, at = c2
                    act.wait_ge(s.s_tr, c + 1)
                    act.wait_ge(s.s_st, 16 * c)
                    nc.scalar.copy(urow[:], ps_u[:])
                    nc.scalar.copy(K.u[:, bass.ds(at, CH)], us[:, 1:CH + 1])
                    nc.scalar.drain().then_inc(s.s_row, 1)

            chunk_steps(act, K, 3, body)
            act.wait_ge(s.s_st, 16 * K.NCH)
            for u in range(SLOTS):
                act.wait_ge(s.sv[u], 32 * K.NI)
                act.wait_ge(s.stx[u], 32 * K.NI)

        @block.vector
        def _(v):
            nc.vector.memset(us[:, CH:CH + 1], 0.0)
            v.drain()

            def body(n, u, stage):
                c1, c2 = stage(1), stage(2)
                if c1:
                    c, w, at = c1
                    v.wait_ge(s.gat[w], turn(c, w) * (16 * T) + 16 * T)
                    v.wait_ge(s.ld[w], turn(c, w) * 32 + 32)
                    v.wait_ge(s.rec[w], turn(c, w) * 16 + 16)
                    nc.vector.tensor_tensor(x[w][:, 0:T, :], x[w][:, 0:T, :], g[w][:], ALU.add)
                    v.wait_ge(s.s_dt, c + 1)
                    nc.vector.tensor_tensor(x[w][:, T:2 * T, :], x[w][:, T:2 * T, :], ps_d[:], ALU.add)
                    v.drain()
                    ln_stats(nc, v, L, x[w], 2 * T)
                    nc.vector.drain().then_inc(s.s_x1, 1)
                if c2:
                    c, w, at = c2
                    v.wait_ge(s.s_tr, c)
                    v.wait_ge(s.s_row, c)
                    nc.vector.tensor_copy(us[:, 0:1], us[:, CH:CH + 1])
                    v.drain()
                    v.wait_ge(s.s_tm, c + 1)
                    nc.vector.tensor_tensor_scan(us[:, 1:CH + 1], K.nstart[:, bass.ds(at, CH)],
                                                 ps_m[:].rearrange("p t e -> p (t e)"), us[:, 0:1],
                                                 ALU.mult, ALU.add).then_inc(s.s_sum, 1)
                if c1:
                    c, w, at = c1
                    v.wait_ge(s.s_sd, c + 1)
                    ln_scale(nc, v, L, 2 * T)
                    v.drain()
                    v.wait_ge(s.s_h, c)
                    for k, (word, t0) in enumerate(((R_CMSG, 0), (R_SELFS, 0), (R_SELFD, T))):
                        nc.vector.tensor_tensor(sc[:, k * T:(k + 1) * T], L.rstd[:, t0:t0 + T], rec[w][:, :, word], ALU.mult)
                        nc.vector.tensor_tensor(sh[:, k * T:(k + 1) * T], L.shift[:, t0:t0 + T], rec[w][:, :, word], ALU.mult)
                    nc.vector.drain().then_inc(s.s_sc, 1)

            chunk_steps(v, K, 2, body)


def gcn_update(nc, K):
    names = ["s_y", "s_xp", "s_ys", "s_yt", "s_mm", "s_x2", "s_sd", "s_sc", "s_h", "s_sth"]
    with phase(nc, "upd", names, ["rec", "ld", "gat", "stx"]) as (block, s):
        rec = [s.sb(f"rec{u}", [P, T, REC]) for u in range(SLOTS)]
        g = [s.sb(f"g{u}", [P, T, D]) for u in range(SLOTS)]
        x = [s.sb(f"x{u}", [P, 2 * T, D]) for u in range(SLOTS)]
        vv = [s.sb(f"vv{u}", [P, 2 * T, D]) for u in range(SLOTS)]
        L = ln_bufs(s, T)
        yst, ydt = s.sb("yst", [D, T, P]), s.sb("ydt", [D, T, P])
        h = s.sb("h", [P, T, D])
        ps_s, ps_d = s.ps("s", [D, T, P]), s.ps("d", [D, T, P])
        ps_y = s.ps("y", [P, 2 * T, D])

        @block.sync
        def _(sp):
            def body(n, u, stage):
                if c := stage(0):
                    c, w, at = c
                    if again_chunk(n):
                        sp.wait_ge(s.s_h, c - SLOTS + 1)
                        hold(sp, s)
                        sp.wait_ge(s.stx[w], 32 * turn(c, w))
                        hold(sp, s)
                    sp.dma_start(rec[w][:], rows_of(K.recd, at)).then_inc(s.rec[w], 16)
                    sp.dma_start(x[w][:, 0:T, :], rows_of(K.xs, at)).then_inc(s.ld[w], 16)
                    sp.dma_start(x[w][:, T:2 * T, :], rows_of(K.xd, at)).then_inc(s.ld[w], 16)
                    sp.dma_start(vv[w][:, 0:T, :], rows_of(K.vs, at)).then_inc(s.ld[w], 16)
                    sp.dma_start(vv[w][:, T:2 * T, :], rows_of(K.vd, at)).then_inc(s.ld[w], 16)

            chunk_steps(sp, K, 0, body)

        @block.gpsimd
        def _(gp):
            def body(n, u, stage):
                if c := stage(0):
                    c, w, at = c
                    gp.wait_ge(s.rec[w], turn(c, w) * 16 + 16)
                    if again_chunk(n):
                        gp.wait_ge(s.s_y, c - SLOTS + 1)
                    hold(gp, s)
                    for t in range(T):
                        nc.gpsimd.indirect_dma_start(
                            g[w][:, t, :], None, K.tabu[:, :],
                            bass.IndirectOffsetOnAxis(ap=rec[w][:].bitcast(I32)[:, t, R_RHO:R_RHO + 1], axis=0)
                        ).then_inc(s.gat[w], 16)

            chunk_steps(gp, K, 0, body)

        @block.tensor
        def _(pe):
            def body(n, u, stage):
                if c := stage(2):
                    c, w, at = c
                    pe.wait_ge(s.s_y, c + 1)
                    pe.wait_ge(s.s_yt, c)
                    pe.wait_ge(s.s_ys, c)
                    for t in range(T):
                        nc.tensor.transpose(ps_s[:, t, :], vv[w][:, t, :], K.ident[0:P, 0:P])
                        last = nc.tensor.transpose(ps_d[:, t, :], vv[w][:, T + t, :], K.ident[0:P, 0:P])
                    last.then_inc(s.s_xp, 1)
                    pe.wait_ge(s.s_ys, c + 1)
                    pe.wait_ge(s.s_yt, c + 1)
                    pe.wait_ge(s.s_x2, c)
                    for t in range(T):
                        nc.tensor.matmul(ps_y[:, t, :], yst[:, t, :], K.w1[:], start=True, stop=True)
                        last = nc.tensor.matmul(ps_y[:, T + t, :], ydt[:, t, :], K.w1[:], start=True, stop=True)
                    last.then_inc(s.s_mm, 1)

            chunk_steps(pe, K, 2, body)

        @block.scalar
        def _(act):
            def body(n, u, stage):
                c2, c3, c4 = (stage(d) for d in (2, 3, 4))
                if c4:
                    c, w, at = c4
                    act.wait_ge(s.s_h, c + 1)
                    act.dma_start(rows_of(K.h2, at), h[:]).then_inc(s.s_sth, 16)
                if c2:
                    c, w, at = c2
                    act.wait_ge(s.s_xp, c + 1)
                    act.wait_ge(s.s_mm, c)
                    nc.scalar.copy(yst[:], ps_s[:]).then_inc(s.s_ys, 1)
                if c3:
                    c, w, at = c3
                    act.wait_ge(s.s_x2, c + 1)
                    nc.scalar.activation(L.sd[:], L.var[:], ACT.Sqrt).then_inc(s.s_sd, 1)
                    act.dma_start(rows_of(K.xs, at), x[w][:, 0:T, :]).then_inc(s.stx[w], 16)
                    act.dma_start(rows_of(K.xd, at), x[w][:, T:2 * T, :]).then_inc(s.stx[w], 16)
                    act.wait_ge(s.s_sc, c + 1)
                    act.wait_ge(s.s_sth, 16 * c)
                    for t in range(T):
                        nc.scalar.activation(h[:, t, :], x[w][:, T + t, :], ACT.Relu, bias=L.shift[:, t:t + 1],
                                             scale=L.rstd[:, t:t + 1])
                    nc.scalar.drain().then_inc(s.s_h, 1)

            chunk_steps(act, K, 4, body)
            act.wait_ge(s.s_sth, 16 * K.NCH)
            for u in range(SLOTS):
                act.wait_ge(s.stx[u], 32 * K.NI)

        @block.vector
        def _(v):
            def body(n, u, stage):
                c1, c2, c3 = (stage(d) for d in (1, 2, 3))
                if c3:
                    c, w, at = c3
                    v.wait_ge(s.s_mm, c + 1)
                    nc.vector.tensor_tensor(x[w][:], x[w][:], ps_y[:], ALU.add)
                    v.drain()
                    v.wait_ge(s.s_h, c)
                    ln_stats(nc, v, L, x[w][:, T:2 * T, :], T)
                    nc.vector.drain().then_inc(s.s_x2, 1)
                if c2:
                    c, w, at = c2
                    v.wait_ge(s.s_xp, c + 1)
                    v.wait_ge(s.s_mm, c)
                    nc.vector.tensor_tensor(ydt[:].rearrange("p t e -> p (t e)"), ps_d[:].rearrange("p t e -> p (t e)"),
                                            K.u[:, bass.ds(at, CH)], ALU.add).then_inc(s.s_yt, 1)
                if c3:
                    c, w, at = c3
                    v.wait_ge(s.s_sd, c + 1)
                    ln_scale(nc, v, L, T)
                    nc.vector.drain().then_inc(s.s_sc, 1)
                if c1:
                    c, w, at = c1
                    v.wait_ge(s.gat[w], turn(c, w) * (16 * T) + 16 * T)
                    v.wait_ge(s.ld[w], turn(c, w) * 64 + 64)
                    nc.vector.tensor_tensor(vv[w][:, 0:T, :], vv[w][:, 0:T, :], g[w][:], ALU.add)
                    bias = K.b1row[0:P, :].unsqueeze(1).to_broadcast((P, 2 * T, D))
                    nc.vector.tensor_tensor(x[w][:], x[w][:], bias, ALU.add)
                    nc.vector.drain().then_inc(s.s_y, 1)

            chunk_steps(v, K, 3, body)


def hop(nc, K, n):
    source = K.h2 if n == 0 else K.tabe[n - 1]
    word = J_POSD if n == 0 else J_LINK
    out = K.tabe[n] if n < 2 else K.taba
    names = ["s_m", "s_tm", "s_sum", "s_tr", "s_row", "s_st"]
    with phase(nc, f"hop{n}", names, ["rec", "gat"]) as (block, s):
        rec = [s.sb(f"rec{u}", [P, T, 4]) for u in range(SLOTS)]
        g = [s.sb(f"g{u}", [P, T, D]) for u in range(SLOTS)]
        m = s.sb("m", [P, T, D])
        es = s.sb("es", [D, CH + 1])
        ac = s.sb("ac", [D, CH])
        orow = s.sb("orow", [P, T, D])
        ps_m, ps_o = s.ps("m", [D, T, P]), s.ps("o", [P, T, D])

        @block.sync
        def _(sp):
            def loads(i, u):
                if again(i):
                    sp.wait_ge(s.s_m, cnt(i - 1, u) + 1)
                    hold(sp, s)
                sp.dma_start(rec[u][:], rows_of(K.recj, i * (SLOTS * CH) + u * CH)).then_inc(s.rec[u], 16)

            ahead(sp, K, loads)

        @block.gpsimd
        def _(gp):
            def gathers(i, u):
                gp.wait_ge(s.rec[u], (i + 1) * 16)
                hold(gp, s)
                for t in range(T):
                    nc.gpsimd.indirect_dma_start(
                        g[u][:, t, :], None, source[:, :],
                        bass.IndirectOffsetOnAxis(ap=rec[u][:].bitcast(I32)[:, t, word:word + 1], axis=0)
                    ).then_inc(s.gat[u], 16)

            ahead(gp, K, gathers)

        @block.scalar
        def _(act):
            for i in peeled(act, K.NI):
                for u in range(SLOTS):
                    c = cnt(i, u)
                    act.wait_ge(s.s_tr, c + 1)
                    act.wait_ge(s.s_st, 16 * c)
                    nc.scalar.copy(orow[:], ps_o[:]).then_inc(s.s_row, 1)
                    act.wait_ge(s.s_row, c + 1)
                    act.dma_start(rows_of(out, i * (SLOTS * CH) + u * CH), orow[:]).then_inc(s.s_st, 16)
            act.wait_ge(s.s_st, 16 * K.NCH)

        @block.tensor
        def _(pe):
            for i in peeled(pe, K.NI):
                for u in range(SLOTS):
                    c = cnt(i, u)
                    pe.wait_ge(s.s_m, c + 1)
                    for t in range(T):
                        last = nc.tensor.transpose(ps_m[:, t, :], m[:, t, :], K.ident[0:P, 0:P])
                    last.then_inc(s.s_tm, 1)
                    pe.wait_ge(s.s_sum, c + 1)
                    pe.wait_ge(s.s_row, c)
                    cols = es[:, 1:CH + 1] if n < 2 else ac[:]
                    for t in range(T):
                        last = nc.tensor.transpose(ps_o[:, t, :], cols[:, t * P:(t + 1) * P], K.ident[:])
                    last.then_inc(s.s_tr, 1)

        @block.vector
        def _(v):
            nc.vector.memset(es[:, CH:CH + 1], 0.0)
            v.drain()
            for i in peeled(v, K.NI):
                for u in range(SLOTS):
                    c = cnt(i, u)
                    v.wait_ge(s.gat[u], (i + 1) * (16 * T))
                    v.wait_ge(s.rec[u], (i + 1) * 16)
                    v.wait_ge(s.s_tm, c)
                    nc.vector.tensor_tensor(m[:], g[u][:], rec[u][:, :, J_W:J_W + 1].to_broadcast((P, T, D)), ALU.mult)
                    nc.vector.drain().then_inc(s.s_m, 1)
                    v.wait_ge(s.s_tr, c)
                    nc.vector.tensor_copy(es[:, 0:1], es[:, CH:CH + 1])
                    v.drain()
                    v.wait_ge(s.s_tm, c + 1)
                    nc.vector.tensor_tensor_scan(es[:, 1:CH + 1], K.nstart[:, span(i, u)],
                                                 ps_m[:].rearrange("p t e -> p (t e)"), es[:, 0:1], ALU.mult, ALU.add)
                    v.drain()
                    if n == 0:
                        nc.vector.tensor_copy(K.u[:, span(i, u)], es[:, 1:CH + 1])
                    elif n == 1:
                        nc.vector.tensor_tensor(K.u[:, span(i, u)], K.u[:, span(i, u)], es[:, 1:CH + 1], ALU.add)
                    else:
                        nc.vector.tensor_tensor(ac[:], K.u[:, span(i, u)], es[:, 1:CH + 1], ALU.add)
                    nc.vector.drain().then_inc(s.s_sum, 1)


def gate_messages(nc, K):
    names = ["s_var2", "s_sd2", "s_sc2", "s_var3", "s_sd3", "s_sc3", "s_g", "s_h2", "s_h3", "s_msg", "s_tm", "s_th", "s_ht", "s_lg", "s_sum", "s_ms", "s_tr",
             "s_made", "s_x3"]
    with phase(nc, "gate", names, ["rec", "ld", "gat", "sent"]) as (block, s):
        rec = [s.sb(f"rec{u}", [P, T, REC]) for u in range(SLOTS)]
        g = [s.sb(f"g{u}", [P, 2 * T, D]) for u in range(SLOTS)]
        x = [s.sb(f"x{u}", [P, 2 * T, D]) for u in range(SLOTS)]
        row = [s.sb(f"row{u}", [P, 2 * T, ROW]) for u in range(SLOTS)]
        L2, L3 = ln_bufs(s, 2 * T, "ln2"), ln_bufs(s, 2 * T, "ln3")
        h2, h3 = s.sb("h2", [P, 2 * T, D]), s.sb("h3", [P, 2 * T, D])
        msg = s.sb("msg", [P, T, D])
        ht = s.sb("ht", [D, 2 * T, D])
        ms = s.sb("ms", [D, CH + 1])
        ps_m, ps_u = s.ps("m", [D, T, P]), s.ps("u", [P, T, D])
        ps_h = s.ps("h", [D, 2 * T, D])
        ps_g = s.ps("g", [P, 2 * T, HEADS])

        @block.sync
        def _(sp):
            def body(n, u, stage):
                if c := stage(0):
                    c, w, at = c
                    if again_chunk(n):
                        sp.wait_ge(s.sent[w], turn(c, w) * (16 * 2 * T))
                        hold(sp, s)
                    sp.dma_start(rec[w][:], rows_of(K.recd, at)).then_inc(s.rec[w], 16)
                    sp.dma_start(x[w][:, 0:T, :], rows_of(K.xs, at)).then_inc(s.ld[w], 16)
                    sp.dma_start(x[w][:, T:2 * T, :], rows_of(K.xd, at)).then_inc(s.ld[w], 16)

            chunk_steps(sp, K, 0, body)

        @block.gpsimd
        def _(gp):
            def body(n, u, stage):
                if c := stage(4):
                    c, w, at = c
                    gp.wait_ge(s.s_made, c + 1)
                    hold(gp, s)
                    for k, word in enumerate((R_SIDX, R_DIDX)):
                        for t in range(T):
                            nc.gpsimd.indirect_dma_start(
                                K.rows[:, :],
                                bass.IndirectOffsetOnAxis(ap=rec[w][:].bitcast(I32)[:, t, word:word + 1], axis=0),
                                row[w][:, k * T + t, :], None, bounds_check=K.N - 1, oob_is_err=False
                            ).then_inc(s.sent[w], 16)
                if c := stage(0):
                    c, w, at = c
                    gp.wait_ge(s.rec[w], turn(c, w) * 16 + 16)
                    hold(gp, s)
                    for k, word in enumerate((R_SIGS, R_SIGD)):
                        for t in range(T):
                            nc.gpsimd.indirect_dma_start(
                                g[w][:, k * T + t, :], None, K.taba[:, :],
                                bass.IndirectOffsetOnAxis(ap=rec[w][:].bitcast(I32)[:, t, word:word + 1], axis=0)
                            ).then_inc(s.gat[w], 16)

            chunk_steps(gp, K, 4, body)
            for u in range(SLOTS):
                gp.wait_ge(s.sent[u], K.NI * (16 * 2 * T))

        @block.tensor
        def _(pe):
            def body(n, u, stage):
                if c := stage(3):
                    c, w, at = c
                    pe.wait_ge(s.s_h3, c + 1)
                    pe.wait_ge(s.s_ht, c)
                    for t in range(2 * T):
                        last = nc.tensor.transpose(ps_h[:, t, 0:P], h3[:, t, :], K.ident[0:P, 0:P])
                    last.then_inc(s.s_th, 1)
                    pe.wait_ge(s.s_msg, c + 1)
                    pe.wait_ge(s.s_sum, c)
                    for t in range(T):
                        last = nc.tensor.transpose(ps_m[:, t, :], msg[:, t, :], K.ident[0:P, 0:P])
                    last.then_inc(s.s_tm, 1)
                    pe.wait_ge(s.s_ht, c + 1)
                    pe.wait_ge(s.s_made, c)
                    for t in range(2 * T):
                        last = nc.tensor.matmul(ps_g[:, t, :], ht[:, t, 0:P], K.wd[:], start=True, stop=True)
                    last.then_inc(s.s_lg, 1)
                    pe.wait_ge(s.s_sum, c + 1)
                    for t in range(T):
                        last = nc.tensor.transpose(ps_u[:, t, :], ms[:, 1 + t * P:1 + (t + 1) * P], K.ident[:])
                    last.then_inc(s.s_tr, 1)

            chunk_steps(pe, K, 3, body)

        @block.scalar
        def _(act):
            def relus(L, out, src, done):
                for t in range(2 * T):
                    nc.scalar.activation(out[:, t, :], src[:, t, 0:D], ACT.Relu, bias=L.shift[:, t:t + 1],
                                         scale=L.rstd[:, t:t + 1])
                nc.scalar.drain().then_inc(done, 1)

            def body(n, u, stage):
                c1, c2, c3 = (stage(d) for d in (1, 2, 3))
                if c1:
                    act.wait_ge(s.s_var2, c1[0] + 1)
                    nc.scalar.activation(L2.sd[:], L2.var[:], ACT.Sqrt).then_inc(s.s_sd2, 1)
                if c2:
                    act.wait_ge(s.s_var3, c2[0] + 1)
                    nc.scalar.activation(L3.sd[:], L3.var[:], ACT.Sqrt).then_inc(s.s_sd3, 1)
                if c3:
                    c, w, at = c3
                    act.wait_ge(s.s_th, c + 1)
                    act.wait_ge(s.s_lg, c)
                    nc.scalar.copy(ht[:, :, 0:P], ps_h[:, :, 0:P]).then_inc(s.s_ht, 1)
                if c1:
                    c, w, at = c1
                    act.wait_ge(s.s_sc2, c + 1)
                    act.wait_ge(s.s_g, c)
                    relus(L2, h2, x[w], s.s_h2)
                if c2:
                    c, w, at = c2
                    act.wait_ge(s.s_sc3, c + 1)
                    act.wait_ge(s.s_th, c)
                    act.wait_ge(s.s_msg, c)
                    relus(L3, h3, row[w], s.s_h3)

            chunk_steps(act, K, 3, body)

        @block.vector
        def _(v):
            nc.vector.memset(ms[:, CH:CH + 1], 0.0)
            v.drain()

            def body(n, u, stage):
                c1, c2, c3 = (stage(d) for d in (1, 2, 3))
                if c1:
                    c, w, at = c1
                    v.wait_ge(s.ld[w], turn(c, w) * 32 + 32)
                    v.wait_ge(s.s_h2, c)
                    ln_stats(nc, v, L2, x[w], 2 * T)
                    nc.vector.drain().then_inc(s.s_var2, 1)
                if c2:
                    c, w, at = c2
                    v.wait_ge(s.s_h2, c + 1)
                    v.wait_ge(s.gat[w], turn(c, w) * (16 * 2 * T) + 16 * 2 * T)
                    nc.vector.tensor_tensor(g[w][:], g[w][:], h2[:], ALU.add)
                    nc.vector.drain().then_inc(s.s_g, 1)
                    nc.vector.scalar_tensor_tensor(out=row[w][:, :, 0:D], in0=g[w][:], scalar=0.25, in1=x[w][:],
                                                   op0=ALU.mult, op1=ALU.add)
                    v.drain()
                    v.wait_ge(s.s_h3, c)
                    ln_stats(nc, v, L3, row[w][:, :, 0:D], 2 * T)
                    nc.vector.drain().then_inc(s.s_var3, 1)
                if c1:
                    v.wait_ge(s.s_sd2, c1[0] + 1)
                    ln_scale(nc, v, L2, 2 * T)
                    nc.vector.drain().then_inc(s.s_sc2, 1)
                if c3:
                    c, w, at = c3
                    v.wait_ge(s.rec[w], turn(c, w) * 16 + 16)
                    v.wait_ge(s.s_h3, c + 1)
                    v.wait_ge(s.s_tm, c)
                    nc.vector.tensor_tensor(msg[:], h3[:, 0:T, :], rec[w][:, :, R_CMSG3:R_CMSG3 + 1].to_broadcast((P, T, D)),
                                            ALU.mult)
                    nc.vector.tensor_copy(row[w][:, 0:T, D:2 * D], h3[:, 0:T, :])
                    nc.vector.tensor_tensor(row[w][:, T:2 * T, D:2 * D], h3[:, T:2 * T, :],
                                            rec[w][:, :, R_SELF3:R_SELF3 + 1].to_broadcast((P, T, D)), ALU.mult)
                    nc.vector.drain().then_inc(s.s_msg, 1)
                if c2:
                    v.wait_ge(s.s_sd3, c2[0] + 1)
                    ln_scale(nc, v, L3, 2 * T)
                    nc.vector.drain().then_inc(s.s_sc3, 1)
                if c3:
                    c, w, at = c3
                    v.wait_ge(s.s_tr, c)
                    nc.vector.tensor_copy(ms[:, 0:1], ms[:, CH:CH + 1])
                    v.drain()
                    v.wait_ge(s.s_tm, c + 1)
                    nc.vector.tensor_tensor_scan(ms[:, 1:CH + 1], K.nstart[:, bass.ds(at, CH)],
                                                 ps_m[:].rearrange("p t e -> p (t e)"), ms[:, 0:1],
                                                 ALU.mult, ALU.add).then_inc(s.s_sum, 1)
                    v.wait_ge(s.s_lg, c + 1)
                    nc.vector.tensor_tensor(row[w][:, :, 2 * D:ROW], ps_g[:],
                                            K.bdrow[0:P, :].unsqueeze(1).to_broadcast((P, 2 * T, HEADS)), ALU.add)
                    v.wait_ge(s.s_tr, c + 1)
                    nc.vector.tensor_tensor(row[w][:, T:2 * T, D:2 * D], row[w][:, T:2 * T, D:2 * D], ps_u[:], ALU.add)
                    nc.vector.drain().then_inc(s.s_made, 1)

            chunk_steps(v, K, 3, body)


def steps(eng, K, lag, body):
    full = K.NGI * DSLOTS
    last = full + (1 if K.REM else 0)

    def stages(s, u, known):
        def stage(d):
            if known and not 0 <= s - d < last:
                return None
            q = K.REM if known and s - d == full else D
            return s - d, (u - d) % DSLOTS, q, s * (GT * D) - d * (GT * D)
        return stage

    peel = min(2, K.NGI)
    for n in range(peel * DSLOTS):
        body(n, n % DSLOTS, stages(n, n % DSLOTS, True))
    if K.NGI > peel:
        with eng.Fori(peel, K.NGI) as i:
            for u in range(DSLOTS):
                body(i * DSLOTS + u, u, stages(i * DSLOTS + u, u, False))
    for n in range(full, last + lag):
        body(n, n % DSLOTS, stages(n, n % DSLOTS, True))


def uses(K, c, u):
    return (c - u) // DSLOTS


def node_rows(dram, q, at):
    return dram[bass.ds(at, q * GT), :].rearrange("(p t) d -> p t d", t=GT)


def dense_first(nc, K, a):
    names = ["s_xa", "s_xb", "s_h2", "s_h1", "s_h3", "s_t1", "s_c1", "s_m1", "s_x2", "s_x3", "s_t3", "s_c3", "s_m3",
             "s_row", "s_b12"] + [f"s_{n}{j}" for n in ("var", "sd", "sc") for j in range(3)] + REC_NAMES
    with phase(nc, "first", names, ["ld", "st"], DSLOTS) as (block, s):
        var, sd, sc = ([s.by_name[f"s_{n}{j}"] for j in range(3)] for n in ("var", "sd", "sc"))
        x = [s.sb(f"x{u}", [D, GT, D]) for u in range(DSLOTS)]
        xa = [s.sb(f"xa{u}", [D, GT, D]) for u in range(DSLOTS)]
        xb = [s.sb(f"xb{u}", [D, GT, D]) for u in range(DSLOTS)]
        row = [s.sb(f"row{u}", [D, GT, ROW]) for u in range(DSLOTS)]
        R = record_bufs(s)
        b12 = s.sb("b12", [D, D])
        h1, h2 = s.sb("h1", [D, GT, D]), s.sb("h2", [D, GT, D])
        ht1, ht3 = s.sb("ht1", [D, GT, D]), s.sb("ht3", [D, GT, D])
        L = [[ln_bufs(s, GT, f"ln{j}{u}", D) for u in range(DSLOTS)] for j in range(3)]
        ps_t1, ps_t3, ps_y = s.ps("t1", [D, 8, D]), s.ps("t3", [D, 8, D]), s.ps("y", [D, 8, D])
        ps_g = s.ps("g", [D, GT, HEADS])

        @block.sync
        def _(sp):
            def body(n, u, stage):
                if g := stage(0):
                    c, w, q, at = g
                    if again_step(n):
                        sp.wait_ge(s.s_xb, c - DSLOTS + 1)
                        hold(sp, s)
                    sp.dma_start(x[w][0:q], node_rows(K.x, q, at)).then_inc(s.ld[w], 16)
                if u == 0 and (r := record_of(K, n, u)) is not None:
                    record_load(sp, s, R, K, a, r)
                if g := stage(5):
                    c, w, q, at = g
                    sp.wait_ge(s.s_row, c + 1)
                    hold(sp, s)
                    sp.dma_start(node_rows(K.rows, q, at), row[w][0:q]).then_inc(s.st[w], 16)

            steps(sp, K, 5, body)
            for u in range(DSLOTS):
                sp.wait_ge(s.st[u], 16 * (K.NGI + (1 if K.REM and u == 0 else 0)))

        @block.gpsimd
        def _(gp):
            wide = lambda b, q: b[0:q, :].unsqueeze(1).to_broadcast((q, GT, D))
            gp.wait_ge(s.s_b12, 1)

            def body(n, u, stage):
                if g := stage(1):
                    c, w, q, at = g
                    if again_step(c):
                        gp.wait_ge(s.s_x3, c - DSLOTS + 1)
                        hold(gp, s)
                    nc.gpsimd.tensor_tensor(xb[w][0:q], x[w][0:q], wide(b12, q), ALU.add).then_inc(s.s_xb, 1)
                if g := stage(0):
                    c, w, q, at = g
                    gp.wait_ge(s.ld[w], uses(K, c, w) * 16 + 16)
                    if again_step(n):
                        gp.wait_ge(s.s_h1, c - DSLOTS + 1)
                    hold(gp, s)
                    nc.gpsimd.tensor_tensor(xa[w][0:q], x[w][0:q], wide(K.b2row, q), ALU.add).then_inc(s.s_xa, 1)

                if u != 1 and (r := record_of(K, n, u)) is not None:
                    (record_gathers if u == 0 else record_scatters)(nc, gp, s, R, K, r)

            steps(gp, K, 1, body)
            gp.wait_ge(s.rec_sent, K.NCH * (16 * 2 * T))

        @block.vector
        def _(v):
            nc.vector.tensor_tensor(b12[:], K.b1row[:], K.b2row[:], ALU.add).then_inc(s.s_b12, 1)

            def scale(j, g):
                if g:
                    c, w, q, at = g
                    v.wait_ge(sd[j], c + 1)
                    ln_scale(nc, v, L[j][w], GT, q)
                    nc.vector.drain().then_inc(sc[j], 1)

            def body(n, u, stage):
                g0, g2, g3, g4 = (stage(d) for d in (0, 2, 3, 4))
                if u == 0 and (r := record_of(K, n, u)) is not None:
                    record_indices(nc, v, s, R, K, r)
                if g2:
                    c, w, q, at = g2
                    v.wait_ge(s.s_m1, c + 1)
                    v.wait_ge(s.s_xb, c + 1)
                    nc.vector.tensor_tensor(xb[w][0:q], xb[w][0:q], ps_y[0:q, 0:GT, :], ALU.add)
                    v.drain()
                    ln_stats(nc, v, L[1][w], xb[w][0:q], GT)
                    nc.vector.drain().then_inc(var[1], 1)
                if g3:
                    c, w, q, at = g3
                    v.wait_ge(s.s_h2, c + 1)
                    v.wait_ge(s.st[w], uses(K, c, w) * 16)
                    nc.vector.scalar_tensor_tensor(out=row[w][0:q, :, 0:D], in0=h2[0:q], scalar=0.25, in1=xb[w][0:q],
                                                   op0=ALU.mult, op1=ALU.add)
                    nc.vector.drain().then_inc(s.s_x3, 1)
                scale(1, g2)
                if g3:
                    c, w, q, at = g3
                    if again_step(c):
                        v.wait_ge(s.s_h3, c - DSLOTS + 1)
                    ln_stats(nc, v, L[2][w], row[w][0:q, :, 0:D], GT)
                    nc.vector.drain().then_inc(var[2], 1)
                if g0:
                    c, w, q, at = g0
                    v.wait_ge(s.s_xa, c + 1)
                    if again_step(n):
                        v.wait_ge(s.s_h1, c - DSLOTS + 1)
                    ln_stats(nc, v, L[0][w], xa[w][0:q], GT)
                    nc.vector.drain().then_inc(var[0], 1)
                scale(2, g3)
                if g4:
                    c, w, q, at = g4
                    v.wait_ge(s.s_m3, c + 1)
                    nc.vector.tensor_tensor(row[w][0:q, :, 2 * D:ROW], ps_g[0:q],
                                            K.bdrow[0:q, :].unsqueeze(1).to_broadcast((q, GT, HEADS)), ALU.add)
                    nc.vector.drain().then_inc(s.s_row, 1)
                scale(0, g0)

                if u == 1 and (r := record_of(K, n, u)) is not None:
                    record_make(nc, v, s, R, K, r)

            steps(v, K, 4, body)

        @block.scalar
        def _(act):
            def root(j, g):
                if g:
                    c, w, q, at = g
                    act.wait_ge(var[j], c + 1)
                    nc.scalar.activation(L[j][w].sd[0:q], L[j][w].var[0:q], ACT.Sqrt).then_inc(sd[j], 1)

            def relus(j, g, out, src, done):
                c, w, q, at = g
                act.wait_ge(sc[j], c + 1)
                for t in range(GT):
                    nc.scalar.activation(out[0:q, t, :], src[0:q, t, 0:D], ACT.Relu, bias=L[j][w].shift[0:q, t:t + 1],
                                         scale=L[j][w].rstd[0:q, t:t + 1])
                nc.scalar.drain().then_inc(done, 1)

            def body(n, u, stage):
                g0, g1, g2, g3, g4 = (stage(d) for d in range(5))
                if g4:
                    c, w, q, at = g4
                    act.wait_ge(s.s_t3, c + 1)
                    act.wait_ge(s.s_m3, c)
                    nc.scalar.copy(ht3[:, :, 0:q], ps_t3[:, 0:GT, 0:q]).then_inc(s.s_c3, 1)
                root(1, g2)
                if g1:
                    c, w, q, at = g1
                    act.wait_ge(s.s_t1, c + 1)
                    act.wait_ge(s.s_m1, c)
                    nc.scalar.copy(ht1[:, :, 0:q], ps_t1[:, 0:GT, 0:q]).then_inc(s.s_c1, 1)
                if g2:
                    act.wait_ge(s.s_x3, g2[0])
                    relus(1, g2, h2, xb[g2[1]], s.s_h2)
                root(2, g3)
                root(0, g0)
                if g3:
                    relus(2, g3, row[g3[1]][:, :, D:2 * D], row[g3[1]], s.s_h3)
                if g0:
                    act.wait_ge(s.s_t1, g0[0])
                    relus(0, g0, h1, xa[g0[1]], s.s_h1)

                if u == 1 and (r := record_of(K, n, u)) is not None:
                    act.wait_ge(s.rec_arg, r + 1)
                    nc.scalar.activation(R.root[:], R.arg[:], ACT.Sqrt).then_inc(s.rec_root, 1)

            steps(act, K, 4, body)

        @block.tensor
        def _(pe):
            def body(n, u, stage):
                g1, g4 = stage(1), stage(4)
                if g4:
                    c, w, q, at = g4
                    pe.wait_ge(s.s_h3, c + 1)
                    pe.wait_ge(s.s_c3, c)
                    for t in range(GT):
                        last = nc.tensor.transpose(ps_t3[:, t, 0:q], row[w][0:q, t, D:2 * D], K.ident[0:q, 0:q])
                    last.then_inc(s.s_t3, 1)
                if g1:
                    c, w, q, at = g1
                    pe.wait_ge(s.s_h1, c + 1)
                    pe.wait_ge(s.s_c1, c)
                    for t in range(GT):
                        last = nc.tensor.transpose(ps_t1[:, t, 0:q], h1[0:q, t, :], K.ident[0:q, 0:q])
                    last.then_inc(s.s_t1, 1)
                if g4:
                    c, w, q, at = g4
                    pe.wait_ge(s.s_c3, c + 1)
                    pe.wait_ge(s.s_row, c)
                    for t in range(GT):
                        last = nc.tensor.matmul(ps_g[0:q, t, :], ht3[:, t, 0:q], K.wd[:], start=True, stop=True)
                    last.then_inc(s.s_m3, 1)
                if g1:
                    c, w, q, at = g1
                    pe.wait_ge(s.s_c1, c + 1)
                    pe.wait_ge(var[1], c)
                    for t in range(GT):
                        last = nc.tensor.matmul(ps_y[0:q, t, :], ht1[:, t, 0:q], K.w1[:], start=True, stop=True)
                    last.then_inc(s.s_m1, 1)

            steps(pe, K, 4, body)


def dense_last(nc, K):
    ZB = DSLOTS
    names = ["s_tp", "s_ct", "s_mx", "s_exp", "s_x3"]
    with phase(nc, "last", names, ["ld", "st", "comb", "zdone", "zread"], DSLOTS) as (block, s):
        row = [s.sb(f"row{u}", [D, GT, ROW]) for u in range(DSLOTS)]
        res = [s.sb(f"res{u}", [D, GT, D]) for u in range(DSLOTS)]
        at_ = [s.sb(f"at{u}", [D, GT, D]) for u in range(DSLOTS)]
        z = [s.sb(f"z{u}", [D, GT, HEADS, D]) for u in range(DSLOTS)]
        gate = [s.sb(f"gate{u}", [D, GT, HEADS]) for u in range(DSLOTS)]
        sm, rs = s.sb("sm", [D, GT]), s.sb("rs", [D, GT])
        ps_t = s.ps("t", [D, 8, D])
        ps_z = [s.ps(f"z{n}", [D, HEADS, D]) for n in range(ZB)]

        def tile(c, w, t):
            j = w * GT + t
            return j % ZB, uses(K, c, w) * (DSLOTS * GT // ZB) + j // ZB

        @block.sync
        def _(sp):
            def body(n, u, stage):
                if g := stage(0):
                    c, w, q, at = g
                    if again_step(n):
                        sp.wait_ge(s.s_x3, c - DSLOTS + 1)
                        hold(sp, s)
                    sp.dma_start(row[w][0:q], node_rows(K.rows, q, at)).then_inc(s.ld[w], 16)

            steps(sp, K, 0, body)

        @block.gpsimd
        def _(gp):
            def body(n, u, stage):
                if g := stage(2):
                    c, w, q, at = g
                    gp.wait_ge(s.comb[w], uses(K, c, w) + 1)
                    hold(gp, s)
                    gp.dma_start(node_rows(K.out, q, at), res[w][0:q]).then_inc(s.st[w], 16)

            steps(gp, K, 2, body)
            for u in range(DSLOTS):
                gp.wait_ge(s.st[u], 16 * (K.NGI + (1 if K.REM and u == 0 else 0)))

        @block.tensor
        def _(pe):
            def body(n, u, stage):
                if g := stage(0):
                    c, w, q, at = g
                    pe.wait_ge(s.ld[w], uses(K, c, w) * 16 + 16)
                    pe.wait_ge(s.s_ct, c)
                    for t in range(GT):
                        last = nc.tensor.transpose(ps_t[:, t, 0:q], row[w][0:q, t, D:2 * D], K.ident[0:q, 0:q])
                    last.then_inc(s.s_tp, 1)
                if g := stage(1):
                    c, w, q, at = g
                    pe.wait_ge(s.s_ct, c + 1)
                    for t in range(GT):
                        b, before = tile(c, w, t)
                        pe.wait_ge(s.zread[b], before)
                        for half in (0, 1):
                            hs = slice(half * 4, half * 4 + 4)
                            nc.tensor.matmul(ps_z[b][0:q, hs, :], at_[w][:, t, 0:q], K.w3[:, hs, :], start=True, stop=False)
                            last = nc.tensor.matmul(ps_z[b][0:q, hs, :], K.onesb[0:3, 0:q], K.b3s[:, hs, :],
                                                    start=False, stop=True)
                        last.then_inc(s.zdone[b], 1)

            steps(pe, K, 1, body)

        @block.scalar
        def _(act):
            def body(n, u, stage):
                if g := stage(0):
                    c, w, q, at = g
                    act.wait_ge(s.s_tp, c + 1)
                    nc.scalar.copy(at_[w][:, :, 0:q], ps_t[:, 0:GT, 0:q]).then_inc(s.s_ct, 1)
                    act.wait_ge(s.s_mx, c + 1)
                    nc.scalar.activation(gate[w][0:q], gate[w][0:q], ACT.Exp).then_inc(s.s_exp, 1)
                if g := stage(1):
                    c, w, q, at = g
                    act.wait_ge(s.comb[w], uses(K, c, w))
                    for t in range(GT):
                        b, before = tile(c, w, t)
                        act.wait_ge(s.zdone[b], before + 1)
                        nc.scalar.activation(z[w][0:q, t], ps_z[b][0:q], ACT.Relu).then_inc(s.zread[b], 1)

            steps(act, K, 1, body)

        @block.vector
        def _(v):
            def body(n, u, stage):
                if g := stage(0):
                    c, w, q, at = g
                    lg = row[w][0:q, :, 2 * D:ROW]
                    v.wait_ge(s.ld[w], uses(K, c, w) * 16 + 16)
                    nc.vector.tensor_reduce(out=sm[0:q], in_=lg, axis=mybir.AxisListType.X, op=ALU.max)
                    v.drain()
                    nc.vector.tensor_tensor(gate[w][0:q], lg, sm[0:q].unsqueeze(2).to_broadcast((q, GT, HEADS)), ALU.subtract)
                    nc.vector.drain().then_inc(s.s_mx, 1)
                if g := stage(2):
                    c, w, q, at = g
                    v.wait_ge(s.s_exp, c + 1)
                    nc.vector.tensor_reduce(out=sm[0:q], in_=gate[w][0:q], axis=mybir.AxisListType.X, op=ALU.add)
                    v.drain()
                    nc.vector.reciprocal(rs[0:q], sm[0:q])
                    v.drain()
                    nc.vector.tensor_tensor(gate[w][0:q], gate[w][0:q], rs[0:q].unsqueeze(2).to_broadcast((q, GT, HEADS)), ALU.mult)
                    v.drain()
                    for t in range(GT):
                        b, before = tile(c, w, t)
                        v.wait_ge(s.zread[b], before + 1)
                    v.wait_ge(s.st[w], uses(K, c, w) * 16)
                    for k in range(HEADS):
                        for t in range(GT):
                            before = row[w][0:q, t, 0:D] if k == 0 else res[w][0:q, t, :]
                            nc.vector.scalar_tensor_tensor(out=res[w][0:q, t, :], in0=z[w][0:q, t, k, :],
                                                           scalar=gate[w][0:q, t, k:k + 1], in1=before,
                                                           op0=ALU.mult, op1=ALU.add)
                        drained = nc.vector.drain()
                        if k == 0:
                            drained.then_inc(s.s_x3, 1)
                    drained.then_inc(s.comb[w], 1)

            steps(v, K, 2, body)


def build(nc, a, out):
    K = Box()
    K.N, K.E = a["x"].shape[0], a["src"].shape[0]
    K.NT, K.NCH = K.E // P, K.E // CH
    K.NI = K.NCH // SLOTS
    assert K.E == K.NI * SLOTS * CH and K.NT <= D
    K.NP = -(-K.N // LO)
    K.NGI, rest = divmod(K.N, DSLOTS * GT * D)
    K.REM = rest // GT
    assert rest == K.REM * GT and K.REM <= D
    K.x, K.out = a["x"], out
    dram = lambda name, shape: nc.dram_tensor(name, shape, F32, kind="Internal").ap()
    K.info = dram("node_info", (K.NP * LO, 4))
    K.recd, K.recj = dram("records_d", (K.E, REC)), dram("records_j", (K.E, 4))
    K.tab = [dram(f"gat_out{l}", (K.E + 1, D)) for l in range(3)]
    K.tabu, K.taba = dram("gcn_sum", (K.E + 1, D)), dram("hops_sum", (K.E + 1, D))
    K.tabe = [dram(f"hop{n}", (K.E + 1, D)) for n in range(2)]
    K.xs, K.xd, K.vs, K.vd, K.h2 = (dram(n, (K.E, D)) for n in ("x_src", "x_dst", "self_src", "self_dst", "h2_dst"))
    K.rows = dram("node_rows", (K.N, ROW))
    with ExitStack() as ctx:
        sb = lambda c, n, shape, dt=F32: c.enter_context(nc.sbuf_tensor("k_" + n, shape, dt))
        K.wl, K.wr, K.we = sb(ctx, "wl", [D, 3, D]), sb(ctx, "wr", [D, 3, D]), sb(ctx, "we", [32, 3, D])
        K.att, K.bcol = sb(ctx, "att", [D, 3, D]), sb(ctx, "bcol", [D, 3])
        K.w1, K.w3, K.wd = sb(ctx, "w1", [D, D]), sb(ctx, "w3", [D, HEADS, D]), sb(ctx, "wd", [D, HEADS])
        K.b1row, K.b2row, K.bdrow = sb(ctx, "b1row", [D, D]), sb(ctx, "b2row", [D, D]), sb(ctx, "bdrow", [D, HEADS])
        K.b3s = sb(ctx, "b3s", [3, HEADS, D], BF16)
        K.ident, K.identb = sb(ctx, "ident", [D, D]), sb(ctx, "identb", [D, D], BF16)
        K.onesb = sb(ctx, "onesb", [D, D], BF16)
        with ExitStack() as c1:
            K.before, K.carry, K.block2 = sb(c1, "before", [D, D]), sb(c1, "carry", [D, D]), sb(c1, "block2", [D, D])
            K.iota, K.part = sb(c1, "iota", [D, LO]), sb(c1, "part", [D, 1])
            K.cnt = {k: sb(c1, f"cnt_{k}", [K.NP, LO]) for k in ("src", "dst")}
            K.col = {k: sb(c1, f"col_{k}", [P, K.NT]) for k in ("src", "dst")}
            K.occ = {k: sb(c1, f"occ_{k}", [P, K.NT]) for k in ("src", "dst")}
            K.wcol = sb(c1, "wcol", [P, K.NT])
            constants(nc, K, a)
            ranks(nc, K, a)
            node_table(nc, K)
            dense_first(nc, K, a)
        with ExitStack() as c2:
            K.nstart = sb(c2, "nstart", [D, K.E], BF16)
            K.nlast = sb(c2, "nlast", [D, K.E], BF16)
            K.hd = K.u = sb(c2, "hd", [D, K.E])
            flags(nc, K, "flags_d", K.recd, (R_NSTART, R_NLAST), (K.nstart, K.nlast), REC)
            start_form(nc, K, "bounds", True)
            for l in range(3):
                gat(nc, K, a, l)
                spread_back(nc, K, f"spread{l}", K.hd)
            start_form(nc, K, "factors", False)
            gcn_messages(nc, K)
            spread_back(nc, K, "spread_u", K.u)
            gcn_update(nc, K)
            flags(nc, K, "flags_j", K.recj, (J_NSTART,), (K.nstart,), 4)
            for n in range(3):
                hop(nc, K, n)
        with ExitStack() as c2:
            K.nstart = sb(c2, "nstart2", [D, K.E], BF16)
            flags(nc, K, "flags_3", K.recd, (R_NSTART,), (K.nstart,), REC)
            gate_messages(nc, K)
        dense_last(nc, K)


_INS = ["x", "src", "dst", "edge_attr_32", "edge_weight"] + [
    f"L0_gnn_{w}{l}" for l in range(3) for w in ("Wl", "Wr", "We", "att", "b")] + [
    "L1_gnn_weight", "L1_gnn_bias", "L3_gnn_W", "L3_gnn_b", "L3_gnn_W_dict", "L3_gnn_b_dict"]


def kernel(**inputs):
    import numpy as _np
    import concourse.bacc as _bacc
    from concourse.bass_utils import run_bass_kernel_spmd as _run

    nc = _bacc.Bacc("TRN2", target_bir_lowering=False, num_devices=1)
    arrays, args = {}, {}
    for name in _INS:
        v = _np.ascontiguousarray(inputs[name])
        arrays[f"in_{name}"] = v
        args[name] = nc.dram_tensor(f"in_{name}", v.shape, mybir.dt.from_np(v.dtype), kind="ExternalInput").ap()
    shape = inputs["x"].shape
    out = nc.dram_tensor("out", shape, F32, kind="ExternalOutput").ap()
    build(nc, args, out)
    return _run(nc, [arrays], core_ids=[0]).results[0]["out"]
```
